# Optimizing a Trainium2 kernel written in Bass

```python
import numpy as np
import jax
import jax.numpy as jnp

def _softmax(x, axis=-1):
    return jax.nn.softmax(x, axis=axis)

def _gelu(x):
    return jax.nn.gelu(x, approximate=True)

def _silu(x):
    return jax.nn.silu(x)

def _sigmoid(x):
    return jax.nn.sigmoid(x)

def _layernorm(x, axis=-1, eps=1e-05):
    m = jnp.mean(x, axis=axis, keepdims=True)
    v = jnp.var(x, axis=axis, keepdims=True)
    return (x - m) / jnp.sqrt(v + eps)

def _scatter_add(tgt, idx, src, axis=0):
    return tgt.at[idx].add(src)

def _segment_sum(src, seg, n):
    return jax.ops.segment_sum(src, seg, n)
kernel_name = 'mk_seq_preln_d2_jaxref_r8_37e264'

def setup_inputs(seed: int=0):
    np.random.seed(seed)
    _w = jnp.asarray

    def _L0_attn_setup():
        import jax, jax.numpy as jnp
        import numpy as np
        D_MODEL = 128
        N_LAYERS = 2
        N_HEADS = 16
        HEAD_DIM = D_MODEL // N_HEADS
        D_FFN = 4 * D_MODEL
        B, L = (4, 128)

        def layer_norm(x, g, b, eps=1e-05):
            mu = jnp.mean(x, axis=-1, keepdims=True)
            var = jnp.var(x, axis=-1, keepdims=True)
            return (x - mu) * jax.lax.rsqrt(var + eps) * g + b

        def make_decay(length):
            gamma = 1.0 - 2.0 ** (-5.0 - jnp.arange(N_HEADS, dtype=jnp.float32))
            n = jnp.arange(length, dtype=jnp.float32)[:, None]
            m = jnp.arange(length, dtype=jnp.float32)[None, :]
            diff = n - m
            pow_ = gamma[:, None, None] ** diff[None]
            return jnp.where(diff[None] >= 0, pow_, 0.0)

        def _forward(x, proj_w, proj_b, reto_w, reto_b, ln1_g, ln1_b, ln2_g, ln2_b, ffn1_w, ffn1_b, ffn2_w, ffn2_b, lnf_g, lnf_b):
            Bx, Lx, _ = x.shape
            D = make_decay(Lx)
            for i in range(N_LAYERS):
                ln_x = layer_norm(x, ln1_g[i], ln1_b[i])
                p = ln_x @ proj_w[i] + proj_b[i]
                q, k, v, xo = jnp.split(p, 4, axis=-1)
                q = q.reshape(Bx, Lx, N_HEADS, HEAD_DIM).transpose(0, 2, 1, 3)
                k = k.reshape(Bx, Lx, N_HEADS, HEAD_DIM).transpose(0, 2, 1, 3)
                v = v.reshape(Bx, Lx, N_HEADS, HEAD_DIM).transpose(0, 2, 1, 3)
                scores = jnp.einsum('bhld,bhmd->bhlm', q, k) * D[None]
                ret = jnp.einsum('bhlm,bhmd->bhld', scores, v)
                ret = ret.transpose(0, 2, 1, 3).reshape(Bx, Lx, D_MODEL)
                ret = ret * jax.nn.silu(xo)
                ret = ret @ reto_w[i] + reto_b[i]
                x = x + ret
                h = layer_norm(x, ln2_g[i], ln2_b[i])
                h = jax.nn.gelu(h @ ffn1_w[i] + ffn1_b[i], approximate=False) @ ffn2_w[i] + ffn2_b[i]
                x = x + h
            return layer_norm(x, lnf_g, lnf_b)
        key = jax.random.key(seed)
        ks = jax.random.split(key, 16)
        s = 0.02
        inp = {'x': jax.random.normal(ks[0], (B, L, D_MODEL), jnp.float32), 'proj_w': jax.random.normal(ks[1], (N_LAYERS, D_MODEL, 4 * D_MODEL), jnp.float32) * s, 'proj_b': jnp.zeros((N_LAYERS, 4 * D_MODEL), jnp.float32), 'reto_w': jax.random.normal(ks[2], (N_LAYERS, D_MODEL, D_MODEL), jnp.float32) * s, 'reto_b': jnp.zeros((N_LAYERS, D_MODEL), jnp.float32), 'ln1_g': jnp.ones((N_LAYERS, D_MODEL), jnp.float32), 'ln1_b': jnp.zeros((N_LAYERS, D_MODEL), jnp.float32), 'ln2_g': jnp.ones((N_LAYERS, D_MODEL), jnp.float32), 'ln2_b': jnp.zeros((N_LAYERS, D_MODEL), jnp.float32), 'ffn1_w': jax.random.normal(ks[3], (N_LAYERS, D_MODEL, D_FFN), jnp.float32) * s, 'ffn1_b': jnp.zeros((N_LAYERS, D_FFN), jnp.float32), 'ffn2_w': jax.random.normal(ks[4], (N_LAYERS, D_FFN, D_MODEL), jnp.float32) * s, 'ffn2_b': jnp.zeros((N_LAYERS, D_MODEL), jnp.float32), 'lnf_g': jnp.ones((D_MODEL,), jnp.float32), 'lnf_b': jnp.zeros((D_MODEL,), jnp.float32)}
        return inp
    _L0_attn_in = _L0_attn_setup()

    def _L0_ffn_setup():
        import jax, jax.numpy as jnp
        import numpy as np
        LN_EPS = 1e-05

        def layer_norm(x, g, b):
            mu = jnp.mean(x, axis=-1, keepdims=True)
            var = jnp.var(x, axis=-1, keepdims=True)
            return (x - mu) / jnp.sqrt(var + LN_EPS) * g + b

        def balanced_assignment(scores):
            T, E = scores.shape
            C = T // E
            taken = jnp.zeros((T,), dtype=bool)
            parts = []
            for e in range(E):
                s = jnp.where(taken, -jnp.inf, scores[:, e])
                _, idx = jax.lax.top_k(s, C)
                parts.append(idx)
                taken = taken.at[idx].set(True)
            return jnp.concatenate(parts)
        key = jax.random.key(seed)
        ks = jax.random.split(key, 4)
        B, S, D, F, E = (4, 256, 128, 512, 8)
        return {'x': jax.random.normal(ks[0], (B, S, D), dtype=jnp.float32), 'centroids': jax.random.normal(ks[1], (E, D), dtype=jnp.float32) * 0.1, 'ln_g': jnp.ones((D,), dtype=jnp.float32), 'ln_b': jnp.zeros((D,), dtype=jnp.float32), 'w1': jax.random.normal(ks[2], (E, D, F), dtype=jnp.float32) * 0.02, 'b1': jnp.zeros((E, F), dtype=jnp.float32), 'w2': jax.random.normal(ks[3], (E, F, D), dtype=jnp.float32) * 0.02, 'b2': jnp.zeros((E, D), dtype=jnp.float32)}
    _L0_ffn_in = _L0_ffn_setup()

    def _L1_attn_setup():
        import jax, jax.numpy as jnp
        import numpy as np
        import math
        DIM, DIM_QK, DIM_V = (128, 128, 128)
        NUM_BUCKETS, MAX_DISTANCE = (32, 128)

        def silu(x):
            return x * jax.nn.sigmoid(x)

        def laplacian_attn_fn(x):
            mu = math.sqrt(0.5)
            std = math.sqrt(0.25 * math.pi)
            return (1.0 + jax.lax.erf((x - mu) / (std * math.sqrt(2.0)))) * 0.5

        def rel_pos_bias(seq_len, table, scale):
            q_pos = jnp.arange(seq_len)
            k_pos = jnp.arange(seq_len)
            rel_pos = k_pos[None, :] - q_pos[:, None]
            n = jnp.maximum(-rel_pos, 0)
            max_exact = NUM_BUCKETS // 2
            is_small = n < max_exact
            n_safe = jnp.maximum(n, 1).astype(jnp.float32)
            val_if_large = max_exact + (jnp.log(n_safe / max_exact) / math.log(MAX_DISTANCE / max_exact) * (NUM_BUCKETS - max_exact)).astype(jnp.int32)
            val_if_large = jnp.minimum(val_if_large, NUM_BUCKETS - 1)
            bucket = jnp.where(is_small, n, val_if_large)
            return table[bucket] * scale
        key = jax.random.key(seed)
        ks = jax.random.split(key, 8)
        B, S = (4, 256)
        lin_std_qk = 1.0 / math.sqrt(DIM)
        return {'x': jax.random.normal(ks[0], (B, S, DIM), dtype=jnp.float32), 'wqk': jax.random.uniform(ks[1], (DIM, DIM_QK), minval=-lin_std_qk, maxval=lin_std_qk, dtype=jnp.float32), 'bqk': jnp.zeros((DIM_QK,), dtype=jnp.float32), 'gamma': 1.0 + 0.02 * jax.random.normal(ks[2], (2, DIM_QK), dtype=jnp.float32), 'beta': jnp.zeros((2, DIM_QK), dtype=jnp.float32), 'wv': jax.random.uniform(ks[3], (DIM, DIM_V), minval=-lin_std_qk, maxval=lin_std_qk, dtype=jnp.float32), 'bv': jnp.zeros((DIM_V,), dtype=jnp.float32), 'rel_bias': jax.random.normal(ks[4], (NUM_BUCKETS,), dtype=jnp.float32)}
    _L1_attn_in = _L1_attn_setup()

    def _L1_ffn_setup():
        import jax, jax.numpy as jnp
        import numpy as np
        EMBED = 128
        D_FF = 4 * EMBED
        N_EXPERTS = 8
        TOP_K = 2
        B, S = (2, 128)
        key = jax.random.key(seed)
        ks = jax.random.split(key, 10)
        sc_d = 1.0 / np.sqrt(EMBED)
        sc_h = 1.0 / np.sqrt(D_FF)
        return {'inputs': jax.random.normal(ks[0], (B, S, EMBED), jnp.float32), 'rw1': jax.random.normal(ks[1], (EMBED, D_FF), jnp.float32) * sc_d, 'rb1': jnp.zeros((D_FF,), jnp.float32), 'rw2': jax.random.normal(ks[2], (D_FF, N_EXPERTS), jnp.float32) * sc_h, 'rb2': jnp.zeros((N_EXPERTS,), jnp.float32), 'W1': jax.random.normal(ks[3], (N_EXPERTS, EMBED, D_FF), jnp.float32) * sc_d, 'b1': jnp.zeros((N_EXPERTS, D_FF), jnp.float32), 'W2': jax.random.normal(ks[4], (N_EXPERTS, D_FF, EMBED), jnp.float32) * sc_h, 'b2': jnp.zeros((N_EXPERTS, EMBED), jnp.float32)}
    _L1_ffn_in = _L1_ffn_setup()
    _d = {'L0_attn_x': _L0_attn_in['x'], 'L0_attn_proj_w': _L0_attn_in['proj_w'], 'L0_attn_proj_b': _L0_attn_in['proj_b'], 'L0_attn_reto_w': _L0_attn_in['reto_w'], 'L0_attn_reto_b': _L0_attn_in['reto_b'], 'L0_attn_ln1_g': _L0_attn_in['ln1_g'], 'L0_attn_ln1_b': _L0_attn_in['ln1_b'], 'L0_attn_ln2_g': _L0_attn_in['ln2_g'], 'L0_attn_ln2_b': _L0_attn_in['ln2_b'], 'L0_attn_ffn1_w': _L0_attn_in['ffn1_w'], 'L0_attn_ffn1_b': _L0_attn_in['ffn1_b'], 'L0_attn_ffn2_w': _L0_attn_in['ffn2_w'], 'L0_attn_ffn2_b': _L0_attn_in['ffn2_b'], 'L0_attn_lnf_g': _L0_attn_in['lnf_g'], 'L0_attn_lnf_b': _L0_attn_in['lnf_b'], 'L0_ffn_centroids': _L0_ffn_in['centroids'], 'L0_ffn_ln_g': _L0_ffn_in['ln_g'], 'L0_ffn_ln_b': _L0_ffn_in['ln_b'], 'L0_ffn_w1': _L0_ffn_in['w1'], 'L0_ffn_b1': _L0_ffn_in['b1'], 'L0_ffn_w2': _L0_ffn_in['w2'], 'L0_ffn_b2': _L0_ffn_in['b2'], 'L1_attn_wqk': _L1_attn_in['wqk'], 'L1_attn_bqk': _L1_attn_in['bqk'], 'L1_attn_gamma': _L1_attn_in['gamma'], 'L1_attn_beta': _L1_attn_in['beta'], 'L1_attn_wv': _L1_attn_in['wv'], 'L1_attn_bv': _L1_attn_in['bv'], 'L1_attn_rel_bias': _L1_attn_in['rel_bias'], 'L1_ffn_rw1': _L1_ffn_in['rw1'], 'L1_ffn_rb1': _L1_ffn_in['rb1'], 'L1_ffn_rw2': _L1_ffn_in['rw2'], 'L1_ffn_rb2': _L1_ffn_in['rb2'], 'L1_ffn_W1': _L1_ffn_in['W1'], 'L1_ffn_b1': _L1_ffn_in['b1'], 'L1_ffn_W2': _L1_ffn_in['W2'], 'L1_ffn_b2': _L1_ffn_in['b2']}
    _x0 = _d['L0_attn_x']
    _d['L0_attn_x'] = jax.random.normal(jax.random.fold_in(jax.random.key(seed), 1), (4, 1024, 128), dtype=_x0.dtype)
    del _x0
    return _d

def reference(L0_attn_x, L0_attn_proj_w, L0_attn_proj_b, L0_attn_reto_w, L0_attn_reto_b, L0_attn_ln1_g, L0_attn_ln1_b, L0_attn_ln2_g, L0_attn_ln2_b, L0_attn_ffn1_w, L0_attn_ffn1_b, L0_attn_ffn2_w, L0_attn_ffn2_b, L0_attn_lnf_g, L0_attn_lnf_b, L0_ffn_centroids, L0_ffn_ln_g, L0_ffn_ln_b, L0_ffn_w1, L0_ffn_b1, L0_ffn_w2, L0_ffn_b2, L1_attn_wqk, L1_attn_bqk, L1_attn_gamma, L1_attn_beta, L1_attn_wv, L1_attn_bv, L1_attn_rel_bias, L1_ffn_rw1, L1_ffn_rb1, L1_ffn_rw2, L1_ffn_rb2, L1_ffn_W1, L1_ffn_b1, L1_ffn_W2, L1_ffn_b2):

    def _L0_attn_ref(x, proj_w, proj_b, reto_w, reto_b, ln1_g, ln1_b, ln2_g, ln2_b, ffn1_w, ffn1_b, ffn2_w, ffn2_b, lnf_g, lnf_b):
        import jax, jax.numpy as jnp
        import numpy as np
        D_MODEL = 128
        N_LAYERS = 2
        N_HEADS = 16
        HEAD_DIM = D_MODEL // N_HEADS
        D_FFN = 4 * D_MODEL
        B, L = (4, 128)

        def layer_norm(x, g, b, eps=1e-05):
            mu = jnp.mean(x, axis=-1, keepdims=True)
            var = jnp.var(x, axis=-1, keepdims=True)
            return (x - mu) * jax.lax.rsqrt(var + eps) * g + b

        def make_decay(length):
            gamma = 1.0 - 2.0 ** (-5.0 - jnp.arange(N_HEADS, dtype=jnp.float32))
            n = jnp.arange(length, dtype=jnp.float32)[:, None]
            m = jnp.arange(length, dtype=jnp.float32)[None, :]
            diff = n - m
            pow_ = gamma[:, None, None] ** diff[None]
            return jnp.where(diff[None] >= 0, pow_, 0.0)

        def _forward(x, proj_w, proj_b, reto_w, reto_b, ln1_g, ln1_b, ln2_g, ln2_b, ffn1_w, ffn1_b, ffn2_w, ffn2_b, lnf_g, lnf_b):
            Bx, Lx, _ = x.shape
            D = make_decay(Lx)
            for i in range(N_LAYERS):
                ln_x = layer_norm(x, ln1_g[i], ln1_b[i])
                p = ln_x @ proj_w[i] + proj_b[i]
                q, k, v, xo = jnp.split(p, 4, axis=-1)
                q = q.reshape(Bx, Lx, N_HEADS, HEAD_DIM).transpose(0, 2, 1, 3)
                k = k.reshape(Bx, Lx, N_HEADS, HEAD_DIM).transpose(0, 2, 1, 3)
                v = v.reshape(Bx, Lx, N_HEADS, HEAD_DIM).transpose(0, 2, 1, 3)
                scores = jnp.einsum('bhld,bhmd->bhlm', q, k) * D[None]
                ret = jnp.einsum('bhlm,bhmd->bhld', scores, v)
                ret = ret.transpose(0, 2, 1, 3).reshape(Bx, Lx, D_MODEL)
                ret = ret * jax.nn.silu(xo)
                ret = ret @ reto_w[i] + reto_b[i]
                x = x + ret
                h = layer_norm(x, ln2_g[i], ln2_b[i])
                h = jax.nn.gelu(h @ ffn1_w[i] + ffn1_b[i], approximate=False) @ ffn2_w[i] + ffn2_b[i]
                x = x + h
            return layer_norm(x, lnf_g, lnf_b)
        return _forward(x, proj_w, proj_b, reto_w, reto_b, ln1_g, ln1_b, ln2_g, ln2_b, ffn1_w, ffn1_b, ffn2_w, ffn2_b, lnf_g, lnf_b)

    def _L0_ffn_ref(x, centroids, ln_g, ln_b, w1, b1, w2, b2):
        import jax, jax.numpy as jnp
        import numpy as np
        LN_EPS = 1e-05

        def layer_norm(x, g, b):
            mu = jnp.mean(x, axis=-1, keepdims=True)
            var = jnp.var(x, axis=-1, keepdims=True)
            return (x - mu) / jnp.sqrt(var + LN_EPS) * g + b

        def balanced_assignment(scores):
            T, E = scores.shape
            C = T // E
            taken = jnp.zeros((T,), dtype=bool)
            parts = []
            for e in range(E):
                s = jnp.where(taken, -jnp.inf, scores[:, e])
                _, idx = jax.lax.top_k(s, C)
                parts.append(idx)
                taken = taken.at[idx].set(True)
            return jnp.concatenate(parts)
        D = x.shape[-1]
        feat = x.reshape(-1, D)
        T = feat.shape[0]
        E = centroids.shape[0]
        C = T // E
        norm = layer_norm(feat, ln_g, ln_b)
        scores = jax.lax.stop_gradient(norm @ centroids.T)
        sort_by_expert = balanced_assignment(scores)
        routed = feat[sort_by_expert].reshape(E, C, D)
        h = layer_norm(routed, ln_g, ln_b)
        h = jax.nn.gelu(jnp.einsum('ecd,edf->ecf', h, w1) + b1[:, None, :])
        h = jnp.einsum('ecf,efd->ecd', h, w2) + b2[:, None, :]
        out = routed + h
        inv = jnp.zeros((T,), dtype=jnp.int32).at[sort_by_expert].set(jnp.arange(T, dtype=jnp.int32))
        return out.reshape(T, D)[inv].reshape(x.shape)

    def _L1_attn_ref(x, wqk, bqk, gamma, beta, wv, bv, rel_bias):
        import jax, jax.numpy as jnp
        import numpy as np
        import math
        DIM, DIM_QK, DIM_V = (128, 128, 128)
        NUM_BUCKETS, MAX_DISTANCE = (32, 128)

        def silu(x):
            return x * jax.nn.sigmoid(x)

        def laplacian_attn_fn(x):
            mu = math.sqrt(0.5)
            std = math.sqrt(0.25 * math.pi)
            return (1.0 + jax.lax.erf((x - mu) / (std * math.sqrt(2.0)))) * 0.5

        def rel_pos_bias(seq_len, table, scale):
            q_pos = jnp.arange(seq_len)
            k_pos = jnp.arange(seq_len)
            rel_pos = k_pos[None, :] - q_pos[:, None]
            n = jnp.maximum(-rel_pos, 0)
            max_exact = NUM_BUCKETS // 2
            is_small = n < max_exact
            n_safe = jnp.maximum(n, 1).astype(jnp.float32)
            val_if_large = max_exact + (jnp.log(n_safe / max_exact) / math.log(MAX_DISTANCE / max_exact) * (NUM_BUCKETS - max_exact)).astype(jnp.int32)
            val_if_large = jnp.minimum(val_if_large, NUM_BUCKETS - 1)
            bucket = jnp.where(is_small, n, val_if_large)
            return table[bucket] * scale
        B, S, _ = x.shape
        qk = silu(x @ wqk + bqk)
        q = qk * gamma[0] + beta[0]
        k = qk * gamma[1] + beta[1]
        v = silu(x @ wv + bv)
        scale = 1.0 / S
        sim = jnp.einsum('bid,bjd->bij', q, k) * scale
        sim = sim + rel_pos_bias(S, rel_bias, DIM_QK ** 0.5)[None, :, :]
        attn = laplacian_attn_fn(sim)
        causal_mask = jnp.triu(jnp.ones((S, S), dtype=bool), k=1)
        attn = jnp.where(causal_mask[None, :, :], 0.0, attn)
        return jnp.einsum('bij,bjd->bid', attn, v)

    def _L1_ffn_ref(inputs, rw1, rb1, rw2, rb2, W1, b1, W2, b2):
        import jax, jax.numpy as jnp
        import numpy as np
        EMBED = 128
        D_FF = 4 * EMBED
        N_EXPERTS = 8
        TOP_K = 2
        B, S = (2, 128)
        Bb, Ss, D = inputs.shape
        T = Bb * Ss
        xf = inputs.reshape(T, D)
        score = jax.nn.relu(xf @ rw1 + rb1) @ rw2 + rb2
        _, topi = jax.lax.top_k(score, TOP_K)
        mask = jnp.zeros(score.shape, bool).at[jnp.arange(T)[:, None], topi].set(True)
        gate = jax.nn.softmax(jnp.where(mask, score, -jnp.inf), axis=-1)
        out = jnp.zeros_like(xf)
        for e in range(N_EXPERTS):
            h = jax.nn.relu(xf @ W1[e] + b1[e])
            y = h @ W2[e] + b2[e]
            out = out + gate[:, e:e + 1] * y
        return out.reshape(Bb, Ss, D)
    x = L0_attn_x
    x = x + _L0_attn_ref(_layernorm(x, axis=-1), L0_attn_proj_w, L0_attn_proj_b, L0_attn_reto_w, L0_attn_reto_b, L0_attn_ln1_g, L0_attn_ln1_b, L0_attn_ln2_g, L0_attn_ln2_b, L0_attn_ffn1_w, L0_attn_ffn1_b, L0_attn_ffn2_w, L0_attn_ffn2_b, L0_attn_lnf_g, L0_attn_lnf_b)
    x = x + _L0_ffn_ref(_layernorm(x, axis=-1), L0_ffn_centroids, L0_ffn_ln_g, L0_ffn_ln_b, L0_ffn_w1, L0_ffn_b1, L0_ffn_w2, L0_ffn_b2)
    x = x + _L1_attn_ref(_layernorm(x, axis=-1), L1_attn_wqk, L1_attn_bqk, L1_attn_gamma, L1_attn_beta, L1_attn_wv, L1_attn_bv, L1_attn_rel_bias)
    x = x + _L1_ffn_ref(_layernorm(x, axis=-1), L1_ffn_rw1, L1_ffn_rb1, L1_ffn_rw2, L1_ffn_rb2, L1_ffn_W1, L1_ffn_b1, L1_ffn_W2, L1_ffn_b2)
    return x

_drawn_inputs = setup_inputs


def setup_inputs(seed=0):
    import zlib

    import numpy as np

    out = dict(_drawn_inputs(seed))
    spreads = {'L0_attn_proj_b': (0.0, 0.1),
     'L0_attn_reto_b': (0.0, 0.1),
     'L0_attn_ln1_g': (1.0, 0.6),
     'L0_attn_ln1_b': (0.0, 0.705),
     'L0_attn_ln2_g': (1.0, 0.6),
     'L0_attn_ln2_b': (0.0, 0.703),
     'L0_attn_ffn1_b': (0.0, 0.1),
     'L0_attn_ffn2_b': (0.0, 0.1),
     'L0_attn_lnf_g': (1.0, 0.2),
     'L0_attn_lnf_b': (0.0, 0.1),
     'L0_ffn_ln_g': (1.0, 0.6),
     'L0_ffn_ln_b': (0.0, 0.8),
     'L0_ffn_b1': (0.0, 0.8),
     'L0_ffn_b2': (0.0, 0.421),
     'L1_attn_bqk': (0.0, 2.0),
     'L1_attn_beta': (0.0, 2.0),
     'L1_attn_bv': (0.0, 0.1),
     'L1_ffn_rb1': (0.0, 0.8),
     'L1_ffn_rb2': (0.0, 0.8),
     'L1_ffn_b1': (0.0, 0.8),
     'L1_ffn_b2': (0.0, 2.0)}
    factors = {'L0_attn_ffn1_w': 2.897,
     'L0_ffn_centroids': 8.0,
     'L0_ffn_w1': 8.0,
     'L0_ffn_w2': 6.175,
     'L1_attn_wqk': 8.0,
     'L1_attn_gamma': 64.0,
     'L1_ffn_rw1': 7.016,
     'L1_ffn_rw2': 5.83,
     'L1_ffn_W1': 6.873,
     'L1_ffn_W2': 5.667}
    for name, (base, spread) in spreads.items():
        noise = np.random.default_rng([zlib.crc32(name.encode()), seed]).standard_normal(out[name].shape)
        drawn = base * np.exp(spread * noise) if base else spread * noise
        out[name] = jnp.asarray(drawn.astype(out[name].dtype))
    for name, factor in factors.items():
        out[name] = (out[name] * factor).astype(out[name].dtype)
    return out
```

```python
from contextlib import ExitStack

import numpy as np

import concourse.bass as bass
from concourse import mybir

F32 = mybir.dt.float32
I32 = mybir.dt.int32
U32 = mybir.dt.uint32
ALU = mybir.AluOpType
ACT = mybir.ActivationFunctionType
AX = mybir.AxisListType

P = 128
NB = 4
SEQ = 1024
TPS = SEQ // P
NT = NB * TPS
NG = NT // 4
TOK = NT * P
LAYERS = 2
SUB = 32
EPS = 1e-5
NE = 8
CAP = TOK // NE
FF = 4
MU = 0.5 ** 0.5
STD = (0.25 * np.pi) ** 0.5
CREDIT = 4
COUNTS = 12


def constants():
    head_gamma = 1.0 - 2.0 ** (-5.0 - np.arange(16, dtype=np.float64))
    g = np.repeat(head_gamma, 8)
    n = np.arange(SEQ, dtype=np.float64)
    p = np.arange(P)
    decay_q = g[:, None] ** n[None]
    decay_k = g[:, None] ** -n[None]
    slot = (p // 8) % 4
    m = p % SUB
    chunk = np.arange(SEQ // SUB)
    decay_rows = g[None, None, :] ** -(chunk[None, :, None] * SUB + m[:, None, None])
    decay_rows = decay_rows * (p[:, None, None] // SUB == slot[None, None, :])
    slot_rows = (p[:, None] // SUB == slot[None]).astype(np.float64)
    causal = (np.tile(np.arange(SUB), 4)[None] >= m[:, None]).astype(np.float64)
    slot_mask = (slot[:, None] == np.arange(4)[None]).astype(np.float64)
    quad_mask = (p[:, None] // 32 == np.arange(4)[None]).astype(np.float64)
    ident = np.eye(P)
    order = np.tile(8.0 - np.arange(8), (P, 1))
    small = np.concatenate([ident, causal, slot_rows, slot_mask, quad_mask, order], 1)
    d = np.maximum(np.arange(-P + 1, SEQ), 0)
    large = 16 + (np.log(np.maximum(d, 1) / 16) / np.log(8) * 16 + 1e-9).astype(int)
    bucket = np.where(d < 16, d, np.minimum(large, 31))
    onehot = (np.arange(32)[:, None] == bucket[None])
    onehot = np.concatenate([onehot, np.zeros((32, 1))], 1)
    dig, part = p // 8, p % 8
    steps = np.array([4096, 256, 16, 1])
    digit_hot = (dig[:, None] == np.arange(16)[None]).astype(np.float64)
    before = np.cumsum(steps) - steps
    thr = 1 + dig[:, None] * steps[None] - before[None]
    earlier = ((dig[:, None] == dig[None]) & (part[:, None] < part[None])).astype(np.float64)
    same = (dig[:, None] == dig[None]).astype(np.float64)
    search = np.concatenate([digit_hot, thr, earlier, same], 1)
    f = np.float32
    return {
        "decay_q": decay_q.astype(f), "decay_k": decay_k.astype(f),
        "decay_rows": decay_rows.reshape(P, -1).astype(f), "small": small.astype(f),
        "onehot": onehot.astype(f), "search": search.astype(f),
    }


def after(n):
    return n + 1 + CREDIT


def mega_kernel(nc, w, out):
    with ExitStack() as ctx:
        def sb(name, shape, dt=F32):
            return ctx.enter_context(nc.sbuf_tensor(name, shape, dt))

        def sem(name):
            return ctx.enter_context(nc.semaphore(name))

        X = sb("X", [P, NT, P])
        R = sb("R", [P, NT, P])
        small = sb("small", [P, 400])
        ident, causal, slot_rows = small[:, 0:128], small[:, 128:256], small[:, 256:384]
        slot_mask, quad_mask = small[:, 384:388], small[:, 388:392]
        order = small[:, 392:400]
        ones_row = sb("ones_row", [1, P])
        zeros = sb("zeros", [P, P])
        decay_rows = sb("decay_rows", [P, SEQ // SUB, P])
        decay_q = sb("decay_q", [P, SEQ])
        decay_k = sb("decay_k", [P, SEQ])
        proj_w = sb("proj_w", [P, LAYERS, 512])
        proj_bc = sb("proj_bc", [P, LAYERS, 4])
        kv_bias = sb("kv_bias", [P, LAYERS, 256])
        reto_w = sb("reto_w", [P, LAYERS, P])
        reto_b = sb("reto_b", [1, LAYERS, P])
        ln1_g, ln1_b = sb("ln1_g", [P, LAYERS]), sb("ln1_b", [P, LAYERS])
        ln2_g, ln2_b = sb("ln2_g", [P, LAYERS]), sb("ln2_b", [P, LAYERS])
        ffn1_w = sb("ffn1_w", [P, LAYERS, 512])
        ffn1_b = sb("ffn1_b", [P, LAYERS, FF])
        ffn2_w = sb("ffn2_w", [P, LAYERS, FF, P])
        ffn2_b = sb("ffn2_b", [P, LAYERS, P])
        lnf_g, lnf_b = sb("lnf_g", [P, P]), sb("lnf_b", [P, P])
        moe_w1 = sb("moe_w1", [P, NE, 512])
        moe_w2 = sb("moe_w2", [P, NE, FF, P])
        moe_b1 = sb("moe_b1", [P, NE, FF])
        moe_b2 = sb("moe_b2", [P, NE, P])
        moe_g, moe_b = sb("moe_g", [P, 1]), sb("moe_b", [P, 1])
        centroids = sb("centroids", [P, NE])
        arena = sb("arena", [P, TOK])
        keys_hi = decay_rows[:].rearrange("p c f -> p (c f)").rearrange("p (e f) -> p e f", e=NE)
        keys_lo = arena[:].rearrange("p (e f) -> p e f", e=NE)
        search = sb("search", [P, 276])
        digit_hot, thr_const = search[:, 0:16], search[:, 16:20]
        earlier, same_digit = search[:, 20:148], search[:, 148:276]
        all_ones = sb("all_ones", [P, P])
        score = sb("score", [P, NE, NT])
        key = decay_q[:].bitcast(U32).rearrange("p (a n) -> p a n", a=4)
        key_f, key_t = [decay_k[:, 512 * j:512 * (j + 1)].rearrange("p (a n) -> p a n", a=4) for j in range(2)]
        cols = sb("cols", [P, 16])
        hot_counts = sb("hot_counts", [P, 16])
        hot_junk = sb("hot_junk", [P, 16])
        slots = sb("slots", [P, NT], U32)
        keys_d = nc.dram_tensor("keys_d", (2, NE, NT, P), F32).ap()
        routed_d = nc.dram_tensor("routed_d", (TOK, P), F32).ap()
        moe_d = nc.dram_tensor("moe_d", (TOK, P), F32).ap()
        wqk, wv = sb("wqk", [P, P]), sb("wv", [P, P])
        bqk = sb("bqk", [P, 1])
        gam_bet = sb("gam_bet", [P, 2, 2])
        bv_row = sb("bv_row", [1, P])
        rel_bias = sb("rel_bias", [32, 1])
        rel_rows = sb("rel_rows", [32, P])
        toeplitz = sb("toeplitz", [P, SEQ])
        qT_all = moe_w1[:].rearrange("p e n -> p (e n)")
        kT_all = moe_w2[:].rearrange("p e f n -> p (e f n)")
        v_all = R
        bias_d = nc.dram_tensor("bias_d", (P, SEQ + P), F32).ap()
        rw1 = sb("rw1", [P, 512])
        rw2 = sb("rw2", [P, FF, NE])
        rb1 = sb("rb1", [P, FF])
        rb2 = sb("rb2", [P, NE])
        top_b1 = sb("top_b1", [P, NE, FF])
        top_b2 = sb("top_b2", [NE, P])
        top_w1 = decay_rows[:].rearrange("p (e f) n -> p e (f n)", e=NE)
        top_w2 = arena[:].rearrange("p (e f n) -> p e f n", e=NE, f=FF)
        logits = score[:].rearrange("p a b -> p (a b)").rearrange("p (t e) -> p t e", e=NE)
        gates = sb("gates", [P, NT, NE])
        route = sb("route", [P, 4, NT, NE])
        peak = sb("peak", [P, 4, NT])
        gatesT = sb("gatesT", [NE, 2, 512])
        stats = sb("stats", [P, 2, 4, 6])
        mv = sb("mv", [P, 2, 4, 2])
        veps = sb("veps", [P, 2, 4])
        rstd = sb("rstd", [P, 2, 4])
        mhalf, eps4 = sb("mhalf", [P, 4]), sb("eps4", [P, 4])
        xn = sb("xn", [P, 2, 512])
        xT = sb("xT", [P, 2, 512])
        x_rows = sb("x_rows", [P, 2, 4, 4, SUB])
        qs, ks = sb("qs", [P, P]), sb("ks", [P, P])
        q_quads = sb("q_quads", [P, 2, 4, 4, SUB])
        k_slots = sb("k_slots", [P, 2, 4, 4, SUB])
        gate_x = sb("gate_x", [P, 2, P])
        kv = sb("kv", [P, 2, 4, 256])
        probs = sb("probs", [P, 4, P])
        snap = sb("snap", [P, 4, P])
        ret = sb("ret", [P, 2, P])
        hid = sb("hid", [P, 2, FF, 512])

        routed = q_quads[:].rearrange("p u s g n -> p u (s g n)")
        onehot = hid[0:32].rearrange("p u f n -> p (u f n)")[:, 0:SEQ + P]
        dist_bias = hid[:].rearrange("p u f n -> p (u f n)")[:, 2048:2048 + SEQ + P]
        rows512 = hid[:].rearrange("p u f n -> p (u f) n")
        hi_left, lo_left, free, slot_sum, chosen, scan, tie, scan_tie = [rows512[:, j, :] for j in range(8)]
        above, junk, zeros512 = xT[:, 0, :], xT[:, 1, :], xn[:, 0, :]
        CNT = 5

        z_sb, gelu_sb, recip_sb, w_sb = [rows512[:, 2 * j:2 * j + 2, :] for j in range(4)]
        av_sb = xT

        psum = [ctx.enter_context(nc.psum_tensor(f"ps{i}", [P, 512], F32)) for i in range(2)]
        psum2 = ctx.enter_context(nc.psum_tensor("psb", [P, 1024], F32))
        psum += [None, None] + [ctx.enter_context(nc.psum_tensor(f"ps{i}", [P, 512], F32)) for i in range(4, 8)]
        ps_xt = psum[0][:, 0:128]
        ps_y = psum[5][:, 0:128]
        ps_gate = psum[7][:, 0:128]
        ps_fm = psum[1]
        ps_kv = psum2[:, :].rearrange("p (s c) -> p s c", s=4)
        ps_sc = psum[4][:, :].rearrange("p (s c) -> p s c", s=4)
        ps_o = psum[5][:, :].rearrange("p (s g n) -> p s g n", s=4, g=4)
        ps_st = psum[6][:, 0:128]
        ps_t4 = psum[0]
        ps_h = [psum[1], psum[4], psum[5], psum[6]]
        ps_y4 = psum[7]
        ps_sim = [psum[1], psum[4], psum[5]]
        ps_av = [psum[6], psum[7]]
        ps_top = [psum[0], psum[7]]

        def YT(h, u):
            return R[:].rearrange("p (g t) d -> p g (t d)", t=4)[:, 2 * h + u, :]

        names = {}

        def counter(name, engine):
            s = sem(name)
            names.setdefault(engine, []).append(s)
            return s

        loaded = sem("loaded")
        passed = sem("passed")
        stored = sem("stored")
        const_ok = sem("const_ok")
        ln_stats = counter("ln_stats", "dve")
        ln_moments = counter("ln_moments", "dve")
        ln_veps = counter("ln_veps", "pool")
        ln_rstd = counter("ln_rstd", "pool")
        ln_out = counter("ln_out", "dve")
        xt_ps = counter("xt_ps", "pe")
        xt_sb = counter("xt_sb", "act")
        fm_ps = counter("fm_ps", "pe")
        gate_ps = counter("gate_ps", "pe")
        kv_ps = counter("kv_ps", "pe")
        qk_sb = counter("qk_sb", "dve")
        gate_sb = counter("gate_sb", "act")
        kv_biased = counter("kv_biased", "dve")
        kv_ready = counter("kv_ready", "pool")
        qk_spread = counter("qk_spread", "pool")
        scores_ps = counter("scores_ps", "pe")
        probs_sb = counter("probs_sb", "dve")
        state_ps = sem("state_ps")
        snap_sb = sem("snap_sb")
        o_ps = counter("o_ps", "pe")
        ret_sb = counter("ret_sb", "dve")
        y_ps = counter("y_ps", "pe")
        res_done = counter("res_done", "dve")
        t4_ps = counter("t4_ps", "pe")
        t4_sb = counter("t4_sb", "act")
        h_ps = counter("h_ps", "pe")
        h_sb = counter("h_sb", "act")
        y4_ps = counter("y4_ps", "pe")
        y4_done = counter("y4_done", "dve")
        bias_done = counter("bias_done", "pool")
        fin_g = counter("fin_g", "pool")
        fin_b = counter("fin_b", "pool")
        fin_x = counter("fin_x", "dve")
        rsd = counter("rsd", "dve")

        y_norm = counter("y_norm", "dve")
        score_ps = counter("score_ps", "pe")
        score_sb = counter("score_sb", "dve")
        key_ok = sem("key_ok")
        key_tp = sem("key_tp")
        key_out = sem("key_out")
        key_in = [sem(f"key_in{e}") for e in range(NE)]
        step_ok = sem("step_ok")
        count_in = sem("count_in")
        count_ps = sem("count_ps")
        slots_tp = sem("slots_tp")
        slots_ok = sem("slots_ok")
        scattered = sem("scattered")
        routed_in = [sem(f"routed_in{u}") for u in range(2)]
        routed_t = sem("routed_t")
        routed_T = sem("routed_T")
        moe_h_ps = sem("moe_h_ps")
        moe_h_sb = sem("moe_h_sb")
        moe_y_ps = sem("moe_y_ps")
        moe_y_sb = sem("moe_y_sb")
        moe_out = sem("moe_out")
        moe_stored = [sem(f"moe_stored{u}") for u in range(2)]
        gathered = sem("gathered")
        moe_added = sem("moe_added")

        qk_ps = counter("qk_ps", "pe")
        z_ready = counter("z_ready", "act")
        v_ready = counter("v_ready", "act")
        qk_ready = counter("qk_ready", "dve")
        late = sem("late")
        bias_ok = sem("bias_ok")
        bias_ps = sem("bias_ps")
        bias_out = sem("bias_out")
        bias_in = sem("bias_in")
        sim_ps = sem("sim_ps")
        z1_sb = sem("z1_sb")
        z_ok = sem("z_ok")
        gelu_ok = sem("gelu_ok")
        recip_ok = sem("recip_ok")
        w_ok = sem("w_ok")
        masked = sem("masked")
        av_ps = sem("av_ps")
        pv_done = sem("pv_done")
        av_ok = sem("av_ok")
        avT_ps = sem("avT_ps")
        av_added = sem("av_added")
        rel_ok = sem("rel_ok")
        logit_ps = counter("logit_ps", "pe")
        logit_sb = counter("logit_sb", "dve")
        shift_ok = sem("shift_ok")
        exp_ok = sem("exp_ok")
        gates_ok = sem("gates_ok")
        gate_t = sem("gate_t")
        gate_T = sem("gate_T")
        gate_b = sem("gate_b")
        gate_added = sem("gate_added")
        top_h_ps = counter("top_h_ps", "pe")
        top_h_sb = counter("top_h_sb", "act")
        top_y_ps = counter("top_y_ps", "pe")
        top_added = counter("top_added", "dve")

        UNITS = [(b, half, m, max(512 * half, P * m), 512 * (half + 1) - max(512 * half, P * m))
                 for b in range(NB) for half in range(2) for m in range(4 * half + 4)]
        NU = len(UNITS)
        DIAG = [i for i, x in enumerate(UNITS) if x[3] == P * x[2]]
        ENDS = [i for i, x in enumerate(UNITS) if x[2] == 4 * x[1] + 3]

        def masks_before(i):
            return sum(d <= i for d in DIAG)

        n_loads = [0]

        def ln_begin(dve, tiles, k, u):
            for j, t in enumerate(tiles):
                last = nc.vector.bn_stats(stats[:, u, j, :], t)
            last.then_inc(ln_stats, 1)
            dve.wait_ge(ln_stats, after(k))
            dve.sem_inc(passed, 1)
            for j in range(len(tiles)):
                last = nc.vector.bn_aggr(mv[:, u, j, :], stats[:, u, j, :])
            last.then_inc(ln_moments, 1)

        def ln_root(pool, n, k, u):
            pool.wait_ge(ln_moments, after(k))
            nc.gpsimd.tensor_tensor(veps[:, u, 0:n], mv[:, u, 0:n, 1], eps4[:, 0:n], ALU.add).then_inc(ln_veps, 1)
            pool.wait_ge(ln_veps, after(k))
            nc.gpsimd.tensor_tensor(rstd[:, u, 0:n], veps[:, u, 0:n], mhalf[:, 0:n], ALU.pow).then_inc(ln_rstd, 1)

        def ln_end(dve, tiles, outs, k, u):
            dve.wait_ge(ln_rstd, after(k))
            for j, (t, o) in enumerate(zip(tiles, outs)):
                last = nc.vector.tensor_scalar(o, t, mv[:, u, j, 0:1], rstd[:, u, j:j + 1],
                                               ALU.subtract, ALU.mult)
            last.then_inc(ln_out, 1)

        def quarters(ap):
            return [ap[:, P * j:P * (j + 1)] for j in range(4)]

        LN0 = 0
        LN_RET = [LN0 + NG, LN0 + NG + NT + NG]
        LN_FFN = [x + NT for x in LN_RET]
        LN_FIN = LN_FFN[1] + NG
        LN_MOE = LN_FIN + 3 * NG
        LN_ATT = LN_MOE + NE
        LN_TOP = LN_ATT + NG
        T4_ATT = (LAYERS + 1) * NG
        T4_TOP = T4_ATT + NG

        block = ctx.enter_context(nc.Block())

        @block.sync
        def _(sp):
            def load(dst, src):
                sp.dma_start(dst, src, allow_slow_non_contiguous=True).then_inc(loaded, 16)
                n_loads[0] += 1
            for b in range(NB):
                load(X[:, b * TPS:(b + 1) * TPS, :], w["L0_attn_x"][b].rearrange("(t p) d -> p t d", p=P))
            load(small[:], w["small"])
            load(proj_w[:], w["L0_attn_proj_w"].rearrange("l k n -> k l n"))
            load(decay_q[:], w["decay_q"])
            load(decay_k[:], w["decay_k"])
            load(decay_rows[:].rearrange("p c f -> p (c f)"), w["decay_rows"])
            for l in range(LAYERS):
                for j in range(4):
                    load(proj_bc[:, l, j:j + 1], w["L0_attn_proj_b"][l, P * j:P * (j + 1)].rearrange("(p o) -> p o", o=1))
                    load(ffn1_b[:, l, j:j + 1], w["L0_attn_ffn1_b"][l, P * j:P * (j + 1)].rearrange("(p o) -> p o", o=1))
                load(kv_bias[:, l, :], w["L0_attn_proj_b"][l:l + 1, P:3 * P].to_broadcast([P, 2 * P]))
                load(ffn2_b[:, l, :], w["L0_attn_ffn2_b"][l:l + 1, :].to_broadcast([P, P]))
                for dst, name in ((ln1_g, "ln1_g"), (ln1_b, "ln1_b"), (ln2_g, "ln2_g"), (ln2_b, "ln2_b")):
                    load(dst[:, l:l + 1], w["L0_attn_" + name][l].rearrange("(p o) -> p o", o=1))
            load(reto_w[:], w["L0_attn_reto_w"].rearrange("l k n -> k l n"))
            load(reto_b[:], w["L0_attn_reto_b"].rearrange("(o l) n -> o l n", o=1))
            load(ffn1_w[:], w["L0_attn_ffn1_w"].rearrange("l k n -> k l n"))
            load(ffn2_w[:], w["L0_attn_ffn2_w"].rearrange("l (f k) n -> k l f n", k=P))
            load(lnf_g[:], w["L0_attn_lnf_g"].rearrange("(o n) -> o n", o=1).to_broadcast([P, P]))
            load(lnf_b[:], w["L0_attn_lnf_b"].rearrange("(o n) -> o n", o=1).to_broadcast([P, P]))
            load(moe_w1[:], w["L0_ffn_w1"].rearrange("e k n -> k e n"))
            load(moe_w2[:], w["L0_ffn_w2"].rearrange("e (f k) n -> k e f n", k=P))
            for e in range(NE):
                load(moe_b1[:, e, :], w["L0_ffn_b1"][e].rearrange("(f p) -> p f", p=P))
                load(moe_b2[:, e, :], w["L0_ffn_b2"][e:e + 1, :].to_broadcast([P, P]))
                load(centroids[:, e:e + 1], w["L0_ffn_centroids"][e].rearrange("(p o) -> p o", o=1))
            load(moe_g[:], w["L0_ffn_ln_g"].rearrange("(p o) -> p o", o=1))
            load(moe_b[:], w["L0_ffn_ln_b"].rearrange("(p o) -> p o", o=1))
            load(search[:], w["search"])
            load(wqk[:], w["L1_attn_wqk"])
            load(wv[:], w["L1_attn_wv"])
            load(bqk[:], w["L1_attn_bqk"].rearrange("(p o) -> p o", o=1))
            for j in range(2):
                load(gam_bet[:, 0, j:j + 1], w["L1_attn_gamma"][j].rearrange("(p o) -> p o", o=1))
                load(gam_bet[:, 1, j:j + 1], w["L1_attn_beta"][j].rearrange("(p o) -> p o", o=1))
            load(bv_row[:], w["L1_attn_bv"].rearrange("(o n) -> o n", o=1))
            load(rel_bias[:], w["L1_attn_rel_bias"].rearrange("(p o) -> p o", o=1))
            load(onehot, w["onehot"])
            load(rw1[:], w["L1_ffn_rw1"])
            load(rw2[:], w["L1_ffn_rw2"].rearrange("(f k) n -> k f n", k=P))
            load(rb1[:], w["L1_ffn_rb1"].rearrange("(f p) -> p f", p=P))
            load(rb2[:], w["L1_ffn_rb2"].rearrange("(o n) -> o n", o=1).to_broadcast([P, NE]))
            for e in range(NE):
                load(top_b1[:, e, :], w["L1_ffn_b1"][e].rearrange("(f p) -> p f", p=P))
            load(top_b2[:], w["L1_ffn_b2"])

            sp.wait_ge(bias_ok, 3)
            sp.dma_start(bias_d, dist_bias).then_inc(bias_out, 16)
            sp.wait_ge(bias_out, 16)
            sp.dma_start(toeplitz[:], bass.AP(bias_d.tensor, P - 1, [[SEQ + P - 1, P], [1, SEQ]])).then_inc(bias_in, 16)

            sp.wait_ge(key_ok, 3)
            sp.dma_start(keys_d.rearrange("h (a e) t n -> (e t) (h a) n", a=2), key_t).then_inc(key_out, 16)
            sp.wait_ge(key_out, 16)
            for e in range(NE):
                for h, keys in enumerate((keys_hi, keys_lo)):
                    for c in range(16):
                        sp.dma_start(keys[8 * c:8 * c + 8, e, :],
                                     keys_d[h, e].rearrange("(q t) n -> q (t n)", q=8)).then_inc(key_in[e], 16)

            sp.wait_ge(slots_ok, 2)
            sp.dma_start(top_w1, w["L1_ffn_W1"].rearrange("e k n -> k e n")).then_inc(late, 16)
            sp.dma_start(top_w2, w["L1_ffn_W2"].rearrange("e (f k) n -> k e f n", k=P)).then_inc(late, 16)

            sp.wait_ge(scattered, 16 * NT)
            def rows_of(t, e):
                return t[CAP * e:CAP * (e + 1), :].rearrange("(t p) d -> p t d", p=P)
            for e in range(NE + 2):
                if e < NE:
                    if e >= 2:
                        sp.wait_ge(moe_stored[e % 2], 16 * (e // 2))
                    sp.dma_start(routed[:, e % 2, :].rearrange("p (t d) -> p t d", t=4),
                                 rows_of(routed_d, e)).then_inc(routed_in[e % 2], 16)
                if 1 <= e <= NE:
                    sp.wait_ge(moe_out, e)
                    sp.dma_start(rows_of(moe_d, e - 1),
                                 routed[:, (e - 1) % 2, :].rearrange("p (t d) -> p t d", t=4)).then_inc(moe_stored[(e - 1) % 2], 16)
            sp.wait_ge(top_added, after(NE * NG - 1))
            sp.dma_start(out.rearrange("b (t p) d -> p (b t) d", p=P), X[:]).then_inc(stored, 16)
            sp.wait_ge(stored, 16)

        LOADS = n_loads[0]

        @block.tensor
        def _(pe):
            for s in names["pe"]:
                pe.sem_inc(s, CREDIT)
            pe.wait_ge(loaded, 16 * LOADS)
            pe.wait_ge(const_ok, 4)
            pe.wait_ge(rel_ok, 1)
            for j, (c0, n) in enumerate(((0, 512), (512, 512), (1024, P))):
                m = nc.tensor.matmul(psum[(0, 1, 4)[j]][0:P, 0:n], rel_rows[:], onehot[:, c0:c0 + n], start=True, stop=True)
            m.then_inc(bias_ps, 1)
            pe.wait_ge(bias_ok, 3)

            def transpose_tile(T, u, lnk):
                pe.wait_ge(ln_out, after(lnk))
                pe.wait_ge(xt_sb, after(T - 1))
                nc.tensor.transpose(ps_xt, xn[:, u, 0:P], ident).then_inc(xt_ps, 1)

            def project(T, u, l):
                pe.wait_ge(xt_sb, after(T))
                pe.wait_ge(qk_sb, after(T - 1))
                x = x_rows[:, u, :, 0, :]
                for c in range(2):
                    last = nc.tensor.matmul(ps_fm[:, c * P:(c + 1) * P], proj_w[:, l, c * P:(c + 1) * P], x,
                                            start=True, stop=True)
                last.then_inc(fm_ps, 1)
                pe.wait_ge(gate_sb, after(T - 1))
                nc.tensor.matmul(ps_gate, proj_w[:, l, 3 * P:4 * P], x, start=True, stop=True).then_inc(gate_ps, 1)
                pe.wait_ge(kv_biased, after(T - 1))
                for s in range(4):
                    rows = x_rows[:, u, s].rearrange("p a b -> p (a b)")
                    last = nc.tensor.matmul(ps_kv[:, s, :], rows, proj_w[:, l, P:3 * P], start=True, stop=True)
                last.then_inc(kv_ps, 1)

            def scores(T, u):
                pe.wait_ge(qk_spread, after(T))
                pe.wait_ge(probs_sb, after(T - 1))
                for s in range(4):
                    last = nc.tensor.matmul(ps_sc[:, s, :], k_slots[:, u, s].rearrange("p a b -> p (a b)"),
                                            q_quads[:, u, s].rearrange("p a b -> p (a b)"), start=True, stop=True)
                last.then_inc(scores_ps, 1)

            def retain(T, u, seq, i):
                if i == 0:
                    nc.tensor.matmul(ps_st, zeros[:], zeros[:], start=True, stop=False,
                                     skip_group_check=True).then_inc(state_ps, 1)
                pe.wait_ge(kv_ready, after(T))
                pe.wait_ge(ret_sb, after(T - 1))
                pe.wait_ge(res_done, after(T - 1))
                for s in range(4):
                    pe.wait_ge(snap_sb, 32 * seq + 4 * i + s + 1)
                    nc.tensor.matmul(ps_st, kv[:, u, s, 0:P], kv[:, u, s, P:2 * P], start=False, stop=False,
                                     skip_group_check=True).then_inc(state_ps, 1)
                    o = ps_o[:, s].rearrange("p g n -> p (g n)")
                    nc.tensor.matmul(o, snap[:, s, :], q_quads[:, u, s].rearrange("p a b -> p (a b)"),
                                     start=True, stop=False)
                    if s == 0:
                        pe.wait_ge(probs_sb, after(T))
                    last = nc.tensor.matmul(o, kv[:, u, s, P:2 * P], probs[:, s, :], start=False, stop=True)
                last.then_inc(o_ps, 1)

            def project_out(T, u, l):
                pe.wait_ge(ret_sb, after(T))
                nc.tensor.matmul(ps_y, ret[:, u, :], reto_w[:, l, :], start=True, stop=False)
                nc.tensor.matmul(ps_y, ones_row[0:1, :], reto_b[0:1, l, :], start=False, stop=True).then_inc(y_ps, 1)

            def retention_tile(b, i, l, first=False, last=False):
                T, k = l * NT + TPS * b + i, LN_RET[l] + TPS * b + i
                u = i % 2
                scores(T, u)
                if not last:
                    transpose_tile(T + 1, 1 - u, k + 1)
                if not first:
                    project_out(T - 1, 1 - u, l)
                if not last:
                    project(T + 1, 1 - u, l)
                retain(T, u, l * NB + b, i)

            def ffn_group(g, u, G, k, l, last=False, first=False):
                def transposes(G1, k1, u1):
                    pe.wait_ge(ln_out, after(k1))
                    pe.wait_ge(t4_sb, after(G1 - 1))
                    for j in range(4):
                        t = nc.tensor.transpose(ps_t4[:, P * j:P * (j + 1)], xn[:, u1, P * j:P * (j + 1)], ident)
                    t.then_inc(t4_ps, 1)
                if first:
                    transposes(G, k, u)
                pe.wait_ge(t4_sb, after(G))
                for f in range(FF):
                    pe.wait_ge(h_sb, after(4 * (G - 1) + f))
                    nc.tensor.matmul(ps_h[f][:, :], ffn1_w[:, l, P * f:P * (f + 1)], xT[:, u, :],
                                     start=True, stop=True).then_inc(h_ps, 1)
                if not last:
                    transposes(G + 1, k + 1, 1 - u)
                pe.wait_ge(h_sb, after(4 * G + 3))
                pe.wait_ge(y4_done, after(G - 1))
                for j in range(4):
                    for f in range(FF):
                        m = nc.tensor.matmul(ps_y4[:, P * j:P * (j + 1)], hid[:, u, f, P * j:P * (j + 1)],
                                             ffn2_w[:, l, f, :], start=(f == 0), stop=(f == FF - 1))
                m.then_inc(y4_ps, 1)

            for l in range(LAYERS):
                transpose_tile(l * NT, 0, LN_RET[l])
                project(l * NT, 0, l)
                for i in range(TPS):
                    retention_tile(0, i, l, first=i == 0)
                with pe.Fori(1, NB - 1) as b:
                    for i in range(TPS):
                        retention_tile(b, i, l)
                for i in range(TPS):
                    retention_tile(NB - 1, i, l, last=i == TPS - 1)
                project_out(l * NT + NT - 1, 1, l)
                for u in range(2):
                    ffn_group(u, u, l * NG + u, LN_FFN[l] + u, l, first=u == 0)
                with pe.Fori(1, NG // 2 - 1) as h:
                    for u in range(2):
                        ffn_group(2 * h + u, u, 2 * h + (l * NG + u), 2 * h + (LN_FFN[l] + u), l)
                for u in range(2):
                    ffn_group(NG - 2 + u, u, l * NG + NG - 2 + u, LN_FFN[l] + NG - 2 + u, l, last=u == 1)

            def score_group(h, u):
                G = 2 * h + (LAYERS * NG + u)
                pe.wait_ge(ln_out, after(6 * h + (LN_FIN + 3 * u + 2)))
                pe.wait_ge(t4_sb, after(G - 1))
                for j in range(4):
                    t = nc.tensor.transpose(ps_t4[:, P * j:P * (j + 1)], xn[:, u, P * j:P * (j + 1)], ident)
                t.then_inc(t4_ps, 1)
                pe.wait_ge(t4_sb, after(G))
                pe.wait_ge(score_sb, after(2 * h + (u - 1)))
                for j in range(4):
                    m = nc.tensor.matmul(ps_y4[:, NE * j:NE * (j + 1)], xT[:, u, P * j:P * (j + 1)], centroids[:],
                                         start=True, stop=True)
                m.then_inc(score_ps, 1)
            with pe.Fori(0, NG // 2) as h:
                for u in range(2):
                    score_group(h, u)

            pe.wait_ge(key_ok, 1)
            for j in range(4):
                t = nc.tensor.transpose(ps_t4[:, P * j:P * (j + 1)], key_f[:, j, :], ident)
            t.then_inc(key_tp, 1)

            with pe.Fori(0, NE) as e:
                for n in range(COUNTS):
                    pe.wait_ge(count_in, COUNTS * e + (n + 1))
                    if n < 4 or 5 <= n < 9:
                        m = nc.tensor.matmul(ps_fm[:, 0:16], all_ones[:], hot_counts[:], start=True, stop=True)
                    elif n in (4, 9):
                        m = nc.tensor.matmul(ps_fm[:, 16:17], same_digit, cols[:, CNT:CNT + 1], start=True, stop=True)
                    elif n == 10:
                        m = nc.tensor.matmul(ps_fm[:, 16:17], earlier, scan_tie[:, 511:512], start=True, stop=True)
                    else:
                        m = nc.tensor.matmul(ps_fm[:, 17:18], earlier, scan[:, 511:512], start=True, stop=True)
                    m.then_inc(count_ps, 1)
            pe.wait_ge(slots_ok, 1)
            for j in range(4):
                t = nc.tensor.transpose(ps_t4[:, 8 * j:8 * j + 8], slot_sum[0:8, P * j:P * (j + 1)], ident[0:8, 0:8])
            t.then_inc(slots_tp, 1)

            for e in range(NE):
                u = e % 2
                pe.wait_ge(ln_out, after(LN_MOE + e))
                if e == 0:
                    pe.wait_ge(slots_ok, 2)
                for j in range(4):
                    t = nc.tensor.transpose(ps_t4[:, P * j:P * (j + 1)], xn[:, u, P * j:P * (j + 1)], ident)
                t.then_inc(routed_t, 1)
                pe.wait_ge(routed_T, e + 1)
                for f in range(FF):
                    if e:
                        pe.wait_ge(moe_h_sb, 4 * (e - 1) + f + 1)
                    nc.tensor.matmul(ps_h[f][:, :], moe_w1[:, e, P * f:P * (f + 1)], xT[:, u, :],
                                     start=True, stop=True).then_inc(moe_h_ps, 1)
                pe.wait_ge(moe_h_sb, 4 * e + 4)
                if e:
                    pe.wait_ge(moe_y_sb, e)
                for j in range(4):
                    for f in range(FF):
                        m = nc.tensor.matmul(ps_y4[:, P * j:P * (j + 1)], hid[:, u, f, P * j:P * (j + 1)],
                                             moe_w2[:, e, f, :], start=(f == 0), stop=(f == FF - 1))
                m.then_inc(moe_y_ps, 1)

            def group_transposes(k, G, u):
                pe.wait_ge(ln_out, after(k))
                pe.wait_ge(t4_sb, after(G - 1))
                for j in range(4):
                    t = nc.tensor.transpose(ps_t4[:, P * j:P * (j + 1)], xn[:, u, P * j:P * (j + 1)], ident)
                t.then_inc(t4_ps, 1)
                pe.wait_ge(t4_sb, after(G))

            pe.wait_ge(moe_added, 1)
            with pe.Fori(0, NG // 2) as h:
                for u in range(2):
                    g = 2 * h + u
                    group_transposes(2 * h + (LN_ATT + u), 2 * h + (T4_ATT + u), u)
                    pe.wait_ge(z_ready, after(2 * h + (u - 1)))
                    nc.tensor.matmul(ps_h[0][:, :], wqk[:], xT[:, u, :], start=True, stop=True)
                    pe.wait_ge(v_ready, after(2 * h + (u - 1)))
                    for j in range(4):
                        o = ps_h[1][:, P * j:P * (j + 1)]
                        nc.tensor.matmul(o, xT[:, u, P * j:P * (j + 1)], wv[:], start=True, stop=False)
                        m = nc.tensor.matmul(o, ones_row[0:1, :], bv_row[0:1, :], start=False, stop=True)
                    m.then_inc(qk_ps, 1)

            def similarity(i):
                b, half, m, n0, n = UNITS[i]
                if i >= 3:
                    pe.wait_ge(z1_sb, i - 2)
                if i == 0:
                    pe.wait_ge(qk_ready, after(NG - 1))
                    pe.wait_ge(v_ready, after(NG - 1))
                nc.tensor.matmul(ps_sim[i % 3][:, 0:n], kT_all[:, SEQ * b + P * m:SEQ * b + P * (m + 1)],
                                 qT_all[:, SEQ * b + n0:SEQ * b + n0 + n], start=True, stop=True).then_inc(sim_ps, 1)

            def weigh(i, group):
                b, half, m, n0, n = UNITS[i]
                if m == 0 and group >= 2:
                    pe.wait_ge(av_ok, group - 1)
                pe.wait_ge(w_ok, i + 1)
                if i in DIAG:
                    pe.wait_ge(masked, masks_before(i))
                x = nc.tensor.matmul(ps_av[group % 2][:, n0 - 512 * half:512], v_all[:, TPS * b + m, :], w_sb[:, i % 2, 0:n],
                                     start=(m == 0), stop=(i in ENDS))
                x.then_inc(pv_done, 1)

            def turn(group):
                pe.wait_ge(av_ok, group + 1)
                if group:
                    pe.wait_ge(av_added, group)
                for j in range(4):
                    t = nc.tensor.transpose(ps_t4[:, P * j:P * (j + 1)], av_sb[:, group % 2, P * j:P * (j + 1)], ident)
                t.then_inc(avT_ps, 1)

            similarity(0)
            similarity(1)
            group = 0
            for i in range(NU):
                if i + 2 < NU:
                    similarity(i + 2)
                weigh(i, group)
                if group and i == ENDS[group - 1] + 1:
                    turn(group - 1)
                if i in ENDS:
                    group += 1
            turn(group - 1)

            pe.wait_ge(av_added, group)
            with pe.Fori(0, NG // 2) as h:
                for u in range(2):
                    g = 2 * h + u
                    group_transposes(2 * h + (LN_TOP + u), 2 * h + (T4_TOP + u), u)
                    for f in range(FF):
                        pe.wait_ge(top_h_sb, after(8 * h + (4 * u + f - 4)))
                        nc.tensor.matmul(ps_h[f][:, :], rw1[:, P * f:P * (f + 1)], YT(h, u),
                                         start=True, stop=True).then_inc(top_h_ps, 1)
                    pe.wait_ge(top_h_sb, after(8 * h + (4 * u + 3)))
                    pe.wait_ge(logit_sb, after(2 * h + (u - 1)))
                    for j in range(4):
                        for f in range(FF):
                            m = nc.tensor.matmul(ps_y4[:, NE * j:NE * (j + 1)], hid[:, u, f, P * j:P * (j + 1)],
                                                 rw2[:, f, :], start=(f == 0), stop=(f == FF - 1))
                    m.then_inc(logit_ps, 1)

            pe.wait_ge(gates_ok, 1)
            for g in range(NG):
                u = g % 2
                if g:
                    pe.wait_ge(gate_T, g)
                for j in range(4):
                    t = nc.tensor.transpose(ps_t4[0:NE, P * j:P * (j + 1)], gates[:, 4 * g + j, :], ident)
                t.then_inc(gate_t, 1)
                pe.wait_ge(gate_T, g + 1)
                if g:
                    pe.wait_ge(gate_added, g)
                for j in range(4):
                    m = nc.tensor.matmul(ps_y4[:, P * j:P * (j + 1)], gatesT[:, u, P * j:P * (j + 1)], top_b2[:],
                                         start=True, stop=True)
                m.then_inc(gate_b, 1)
            pe.wait_ge(gate_added, NG)
            pe.wait_ge(late, 32)
            for e in range(NE):
                with pe.Fori(0, NG // 2) as h:
                    for u in range(2):
                        U = 2 * h + (NG * e + u)
                        for f in range(FF):
                            pe.wait_ge(top_h_sb, after(8 * h + (4 * (NG * (e + 1) + u) + f - 4)))
                            nc.tensor.matmul(ps_h[f][:, :], top_w1[:, e, P * f:P * (f + 1)], YT(h, u),
                                             start=True, stop=True).then_inc(top_h_ps, 1)
                        pe.wait_ge(top_h_sb, after(8 * h + (4 * (NG * (e + 1) + u) + 3)))
                        pe.wait_ge(top_added, after(2 * h + (NG * e + u - 2)))
                        for j in range(4):
                            for f in range(FF):
                                m = nc.tensor.matmul(ps_top[u][:, P * j:P * (j + 1)], hid[:, u, f, P * j:P * (j + 1)],
                                                     top_w2[:, e, f, :], start=(f == 0), stop=(f == FF - 1))
                        m.then_inc(top_y_ps, 1)

        @block.scalar
        def _(act):
            for s in names["act"]:
                act.sem_inc(s, CREDIT)
            act.wait_ge(loaded, 16 * LOADS)
            act.wait_ge(bias_out, 16)

            def copy_xt(T, u, l):
                act.wait_ge(xt_ps, after(T))
                act.wait_ge(kv_ps, after(T - 2))
                src = ps_xt.rearrange("p (s m) -> p s m", s=4).unsqueeze(2).to_broadcast([P, 4, 4, SUB])
                nc.scalar.activation(x_rows[:, u], src, ACT.Identity, bias=ln1_b[:, l:l + 1],
                                     scale=ln1_g[:, l:l + 1]).then_inc(xt_sb, 1)

            def silu_gate(T, u, l):
                act.wait_ge(gate_ps, after(T))
                act.wait_ge(ret_sb, after(T - 2))
                nc.scalar.activation(gate_x[:, u, :], ps_gate, ACT.Silu,
                                     bias=proj_bc[:, l, 3:4]).then_inc(gate_sb, 1)

            def snapshots(T, seq, i):
                act.wait_ge(o_ps, after(T - 1))
                for s in range(4):
                    act.wait_ge(state_ps, 33 * seq + 1 + 4 * i + s)
                    nc.scalar.activation(snap[:, s, :], ps_st, ACT.Copy).then_inc(snap_sb, 1)

            def retention_tile(b, i, l, last=False):
                T = l * NT + TPS * b + i
                if not last:
                    copy_xt(T + 1, 1 - i % 2, l)
                    silu_gate(T + 1, 1 - i % 2, l)
                snapshots(T, l * NB + b, i)

            def ffn_group(G, u, l, first=False, last=False):
                def copy_t4(G1, u1):
                    act.wait_ge(t4_ps, after(G1))
                    nc.scalar.activation(xT[:, u1, :], ps_t4[:, :], ACT.Identity, bias=ln2_b[:, l:l + 1],
                                         scale=ln2_g[:, l:l + 1]).then_inc(t4_sb, 1)
                if first:
                    copy_t4(G, u)
                for f in range(FF):
                    act.wait_ge(h_ps, after(4 * G + f))
                    if f == 0:
                        act.wait_ge(y4_ps, after(G - 2))
                    nc.scalar.activation(hid[:, u, f, :], ps_h[f][:, :], ACT.Gelu,
                                         bias=ffn1_b[:, l, f:f + 1]).then_inc(h_sb, 1)
                if not last:
                    copy_t4(G + 1, 1 - u)

            for l in range(LAYERS):
                nc.scalar.preload_act_table(ACT.Silu)
                copy_xt(l * NT, 0, l)
                silu_gate(l * NT, 0, l)
                with act.Fori(0, NB - 1) as b:
                    for i in range(TPS):
                        retention_tile(b, i, l)
                for i in range(TPS):
                    retention_tile(NB - 1, i, l, last=i == TPS - 1)
                nc.scalar.preload_act_table(ACT.Gelu)
                for u in range(2):
                    ffn_group(l * NG + u, u, l, first=u == 0)
                with act.Fori(1, NG // 2 - 1) as h:
                    for u in range(2):
                        ffn_group(2 * h + (l * NG + u), u, l)
                for u in range(2):
                    ffn_group(l * NG + NG - 2 + u, u, l, last=u == 1)

            def copy_scores(G, u):
                act.wait_ge(t4_ps, after(G))
                nc.scalar.activation(xT[:, u, :], ps_t4[:, :], ACT.Identity, bias=moe_b[:, 0:1],
                                     scale=moe_g[:, 0:1]).then_inc(t4_sb, 1)
            with act.Fori(0, NG // 2) as h:
                for u in range(2):
                    copy_scores(2 * h + (LAYERS * NG + u), u)

            for e in range(NE):
                u = e % 2
                act.wait_ge(routed_t, e + 1)
                nc.scalar.activation(xT[:, u, :], ps_t4[:, :], ACT.Identity, bias=moe_b[:, 0:1],
                                     scale=moe_g[:, 0:1]).then_inc(routed_T, 1)
                for f in range(FF):
                    act.wait_ge(moe_h_ps, 4 * e + f + 1)
                    nc.scalar.activation(hid[:, u, f, :], ps_h[f][:, :], ACT.Gelu_apprx_tanh,
                                         bias=moe_b1[:, e, f:f + 1]).then_inc(moe_h_sb, 1)

            nc.scalar.preload_act_table(ACT.Silu)
            act.wait_ge(moe_added, 1)
            with act.Fori(0, NG // 2) as h:
                for u in range(2):
                    G = 2 * h + (T4_ATT + u)
                    act.wait_ge(t4_ps, after(G))
                    nc.scalar.activation(xT[:, u, :], ps_t4[:, :], ACT.Copy).then_inc(t4_sb, 1)
                    act.wait_ge(qk_ps, after(2 * h + u))
                    act.wait_ge(qk_ready, after(2 * h + (u - 2)))
                    nc.scalar.activation(rows512[:, u, :], ps_h[0][:, :], ACT.Silu, bias=bqk[:, 0:1]).then_inc(z_ready, 1)
                    nc.scalar.activation(YT(h, u), ps_h[1][:, :], ACT.Silu).then_inc(v_ready, 1)

            nc.scalar.preload_act_table(ACT.Gelu)
            group = 0
            def copy_av(group):
                act.wait_ge(pv_done, ENDS[group] + 1)
                if group >= 2:
                    act.wait_ge(avT_ps, group - 1)
                nc.scalar.activation(av_sb[:, group % 2, :], ps_av[group % 2][:, :], ACT.Copy).then_inc(av_ok, 1)
            for i in range(NU):
                n = UNITS[i][4]
                act.wait_ge(z_ok, i + 1)
                if i >= 2:
                    act.wait_ge(w_ok, i - 1)
                nc.scalar.activation(gelu_sb[:, i % 2, 0:n], z_sb[:, i % 2, 0:n], ACT.Gelu).then_inc(gelu_ok, 1)
                if group < len(ENDS) and i == ENDS[group] + 1:
                    copy_av(group)
                    group += 1
            copy_av(group)

            nc.scalar.preload_act_table(ACT.Exp)
            act.wait_ge(av_added, group + 1)
            def relu_hidden(u, bias, base):
                for f in range(FF):
                    act.wait_ge(top_h_ps, after(base(f)))
                    nc.scalar.activation(hid[:, u, f, :], ps_h[f][:, :], ACT.Relu, bias=bias[:, f:f + 1]).then_inc(top_h_sb, 1)
            with act.Fori(0, NG // 2) as h:
                for u in range(2):
                    act.wait_ge(t4_ps, after(2 * h + (T4_TOP + u)))
                    nc.scalar.activation(YT(h, u), ps_t4[:, :], ACT.Copy).then_inc(t4_sb, 1)
                    act.wait_ge(logit_ps, after(2 * h + (u - 2)))
                    relu_hidden(u, rb1, lambda f: 8 * h + (4 * u + f))
            act.wait_ge(shift_ok, 1)
            nc.scalar.activation(route[:, 3].rearrange("p t e -> p (t e)"), route[:, 2].rearrange("p t e -> p (t e)"),
                                 ACT.Exp).then_inc(exp_ok, 1)
            for g in range(NG):
                act.wait_ge(gate_t, g + 1)
                if g >= 2:
                    act.wait_ge(gate_b, g - 1)
                nc.scalar.activation(gatesT[:, g % 2, :], ps_t4[0:NE, :], ACT.Copy).then_inc(gate_T, 1)
            for e in range(NE):
                with act.Fori(0, NG // 2) as h:
                    for u in range(2):
                        act.wait_ge(top_y_ps, after(2 * h + (NG * e + u - 2)))
                        relu_hidden(u, top_b1[:, e, :], lambda f: 8 * h + (4 * (NG * (e + 1) + u) + f))

        @block.vector
        def _(dve):
            for s in names["dve"]:
                dve.sem_inc(s, CREDIT)
            nc.vector.memset(ones_row[:], 1.0).then_inc(const_ok, 1)
            nc.vector.memset(zeros[:], 0.0).then_inc(const_ok, 1)
            dve.wait_ge(loaded, 16 * LOADS)

            dve.wait_ge(const_ok, 4)

            nc.vector.tensor_scalar(rel_rows[:], zeros[0:32, :], rel_bias[:, 0:1], None, ALU.add).then_inc(rel_ok, 1)
            dve.wait_ge(bias_ps, 1)
            for j, (c0, n) in enumerate(((0, 512), (512, 512), (1024, P))):
                nc.vector.tensor_scalar(dist_bias[:, c0:c0 + n], psum[(0, 1, 4)[j]][:, 0:n], float(P ** 0.5 / STD),
                                        float(0.75 - MU / STD), ALU.mult, ALU.add).then_inc(bias_ok, 1)

            def first_norm(h, u):
                g = 2 * h + u
                xs = [X[:, 4 * (2 * h + u) + j, :] for j in range(4)]
                rs = [R[:, 4 * (2 * h + u) + j, :] for j in range(4)]
                ln_begin(dve, xs, g, u)
                ln_end(dve, xs, rs, g, u)
            with dve.Fori(0, NG // 2) as h:
                for u in range(2):
                    first_norm(h, u)
            dve.wait_ge(ln_out, after(NG - 1))

            def norm_begin(t, T, u, l, k):
                ln_begin(dve, [R[:, t, :]], k, u)

            def norm_end(t, T, u, l, k):
                dve.wait_ge(xt_ps, after(T - 2))
                ln_end(dve, [R[:, t, :]], [xn[:, u, 0:P]], k, u)

            def read_products(T, i, u, l):
                dve.wait_ge(fm_ps, after(T))
                dve.wait_ge(qk_spread, after(T - 1))
                n0 = P * (i % TPS)
                nc.vector.scalar_tensor_tensor(qs[:], ps_fm[:, 0:P], proj_bc[:, l, 0:1],
                                               decay_q[:, n0:n0 + P], ALU.add, ALU.mult)
                nc.vector.scalar_tensor_tensor(ks[:], ps_fm[:, P:2 * P], proj_bc[:, l, 1:2],
                                               decay_k[:, n0:n0 + P], ALU.add, ALU.mult).then_inc(qk_sb, 1)
                dve.wait_ge(kv_ps, after(T))
                dve.wait_ge(o_ps, after(T - 2))
                nc.vector.tensor_tensor(kv[:, u], ps_kv, kv_bias[:, l, :].unsqueeze(1).to_broadcast([P, 4, 256]),
                                        ALU.add).then_inc(kv_biased, 1)

            def make_probs(T):
                dve.wait_ge(scores_ps, after(T))
                dve.wait_ge(o_ps, after(T - 1))
                nc.vector.tensor_tensor(probs[:], ps_sc, causal.unsqueeze(1).to_broadcast([P, 4, P]),
                                        ALU.mult).then_inc(probs_sb, 1)

            def gate_out(T, u):
                dve.wait_ge(o_ps, after(T))
                dve.wait_ge(gate_sb, after(T))
                dve.wait_ge(y_ps, after(T - 2))
                for g in range(4):
                    q = slice(32 * g, 32 * g + 32)
                    last = nc.vector.tensor_tensor(
                        ret[q, u, :].rearrange("p (s n) -> p s n", s=4), ps_o[q, :, g, :],
                        gate_x[q, u, :].rearrange("p (s n) -> p s n", s=4), ALU.mult)
                last.then_inc(ret_sb, 1)

            def add_residual(t, T):
                dve.wait_ge(y_ps, after(T))
                nc.vector.tensor_tensor(R[:, t, :], R[:, t, :], ps_y, ALU.add).then_inc(res_done, 1)

            def retention_tile(b, i, l, first=False, left=8):
                t, T, k = TPS * b + i, TPS * b + (l * NT + i), TPS * b + (LN_RET[l] + i)
                u = i % 2
                if left > 2:
                    norm_begin(TPS * b + i + 2 if isinstance(b, int) or i < 6 else TPS * (b + 1) + i - 6, T + 2, u, l, k + 2)
                if not first:
                    gate_out(T - 1, 1 - u)
                make_probs(T)
                if left > 1:
                    read_products(T + 1, i + 1, 1 - u, l)
                if not first:
                    add_residual(TPS * b + i - 1 if isinstance(b, int) or i > 0 else TPS * (b - 1) + 7, T - 1)
                if left > 2:
                    norm_end(TPS * b + i + 2 if isinstance(b, int) or i < 6 else TPS * (b + 1) + i - 6, T + 2, u, l, k + 2)

            def tiles_of(h, u):
                return [R[:, 8 * h + (4 * u + j), :] for j in range(4)]

            def ffn_norm(h, u, l, shift=0):
                k = 2 * h + (LN_FFN[l] + u)
                G = 2 * h + (l * NG + u)
                ts = tiles_of(h, u)
                ln_begin(dve, ts, k, u)
                dve.wait_ge(t4_ps, after(G - 2))
                ln_end(dve, ts, quarters(xn[:, u, :]), k, u)

            def ffn_add(h, u, l):
                G = 2 * h + (l * NG + u)
                dve.wait_ge(y4_ps, after(G))
                r = R[:, :, :].rearrange("p (g t) d -> p g (t d)", t=4)[:, 2 * h + u, :]
                nc.vector.tensor_tensor(r, r, ps_y4[:, :], ALU.add).then_inc(y4_done, 1)

            for l in range(LAYERS):
                if l:
                    dve.wait_ge(bias_done, after(NG - 1))
                for i in range(2):
                    norm_begin(i, l * NT + i, i, l, LN_RET[l] + i)
                    norm_end(i, l * NT + i, i, l, LN_RET[l] + i)
                read_products(l * NT, 0, 0, l)
                for i in range(TPS):
                    retention_tile(0, i, l, first=i == 0)
                with dve.Fori(1, NB - 1) as b:
                    for i in range(TPS):
                        retention_tile(b, i, l)
                for i in range(TPS):
                    retention_tile(NB - 1, i, l, left=TPS - i)
                gate_out(l * NT + NT - 1, 1)
                add_residual(NT - 1, l * NT + NT - 1)
                dve.wait_ge(res_done, after(l * NT + NT - 1))
                ffn_norm(0, 0, l)
                ffn_norm(0, 1, l)
                with dve.Fori(0, NG // 2 - 1) as h:
                    for u in range(2):
                        ffn_add(h, u, l)
                        ffn_norm(h + 1, u, l)
                for u in range(2):
                    ffn_add(NG // 2 - 1, u, l)

            dve.wait_ge(bias_done, after(2 * NG - 1))
            def final_norm(h, u):
                k = 6 * h + (LN_FIN + 3 * u)
                g = 2 * h + u
                ts = tiles_of(h, u)
                ln_begin(dve, ts, k, u)
                ln_end(dve, ts, quarters(xn[:, u, :]), k, u)
                dve.wait_ge(fin_b, after(g))
                xg = X[:, :, :].rearrange("p (g t) d -> p g (t d)", t=4)[:, 2 * h + u, :]
                nc.vector.tensor_tensor(xg, xg, xn[:, u, :], ALU.add).then_inc(fin_x, 1)
                dve.wait_ge(fin_x, after(g))
                dve.sem_inc(passed, 1)
                xs = [X[:, 8 * h + (4 * u + j), :] for j in range(4)]
                ln_begin(dve, xs, k + 1, u)
                ln_end(dve, xs, ts, k + 1, u)
                dve.wait_ge(ln_out, after(k + 1))
                dve.sem_inc(passed, 1)
                ln_begin(dve, ts, k + 2, u)
                ln_end(dve, ts, quarters(xn[:, u, :]), k + 2, u)
                dve.wait_ge(score_ps, after(g))
                nc.vector.tensor_copy(
                    score[:].rearrange("p e (g j) -> p e g j", j=4)[:, :, 2 * h + u, :],
                    ps_y4[:, 0:4 * NE].rearrange("p (j e) -> p e j", e=NE)).then_inc(score_sb, 1)
            with dve.Fori(0, NG // 2) as h:
                for u in range(2):
                    final_norm(h, u)

            n_steps = [0]

            def step(ins):
                n_steps[0] += 1
                ins.then_inc(step_ok, 1)
                dve.wait_ge(step_ok, n_steps[0])
            dve.wait_ge(score_sb, after(NG - 1))
            bits = score[:].rearrange("p e t -> p (e t)")
            step(nc.vector.tensor_scalar(key[:, 0, :].bitcast(I32), bits.bitcast(I32), 31, -2 ** 31,
                                         ALU.arith_shift_right, ALU.bitwise_or))
            step(nc.vector.tensor_tensor(key[:, 1, :], bits.bitcast(U32), key[:, 0, :], ALU.bitwise_xor))
            step(nc.vector.tensor_scalar(key[:, 2, :], key[:, 1, :], 16, None, ALU.logical_shift_right))
            step(nc.vector.tensor_scalar(key[:, 3, :], key[:, 1, :], 65535, None, ALU.bitwise_and))
            for j in range(2):
                last = nc.vector.tensor_scalar(key_f[:, 2 * j:2 * j + 2, :].rearrange("p a n -> p (a n)"),
                                               key[:, 2 + j, :], 1.0, None, ALU.add)
            last.then_inc(key_ok, 1)
            dve.wait_ge(key_tp, 1)
            nc.vector.tensor_copy(key_t.rearrange("p a n -> p (a n)"), ps_t4[:, :]).then_inc(key_ok, 1)
            nc.vector.memset(all_ones[:], 1.0)
            nc.vector.memset(zeros512, 0.0)
            nc.vector.memset(cols[:, 0:9], 0.0)
            nc.vector.memset(free, 1.0)
            nc.vector.memset(slot_sum, 0.0)
            step(nc.vector.memset(cols[:, 9:10], -1.0))
            nc.vector.tensor_copy(junk, zeros512).then_inc(key_ok, 1)

            def col(n):
                return cols[:, n:n + 1]
            STEPS = 4 * 2 * 5 + 18
            start = n_steps[0]

            def assign(e):
                m = [0]
                c = [0]

                def step(ins):
                    m[0] += 1
                    ins.then_inc(step_ok, 1)
                    dve.wait_ge(step_ok, STEPS * e + (start + m[0]))

                def summed(ins):
                    c[0] += 1
                    ins.then_inc(count_in, 1)
                    dve.wait_ge(count_ps, COUNTS * e + c[0])

                def search_key(row, need):
                    for it in range(4):
                        size = 16.0 ** (3 - it)
                        if it:
                            step(nc.vector.tensor_tensor(col(2), col(it % 2), thr_const[:, it:it + 1], ALU.add))
                        thr = col(2) if it else thr_const[:, 0:1]
                        step(nc.vector.tensor_scalar(junk, row, thr, None, ALU.is_ge, ALU.add, accum_out=col(4)))
                        summed(nc.vector.tensor_scalar(hot_counts[:], digit_hot, col(4), None, ALU.mult))
                        step(nc.vector.tensor_scalar(hot_junk[:], ps_fm[:, 0:16], need, None, ALU.is_ge, ALU.add,
                                                     accum_out=col(3)))
                        if it:
                            step(nc.vector.scalar_tensor_tensor(col((it + 1) % 2), col(3), size, col(it % 2),
                                                                ALU.mult, ALU.add))
                        else:
                            step(nc.vector.tensor_scalar(col(1), col(3), size, None, ALU.mult))
                    step(nc.vector.tensor_scalar(col(6), col(0), -4368.0, None, ALU.add))

                step(nc.vector.tensor_tensor(hi_left, keys_hi[:, e, :], free, ALU.mult))
                search_key(hi_left, float(CAP))
                summed(nc.vector.tensor_scalar(above, hi_left, col(6), None, ALU.is_gt, ALU.add, accum_out=col(CNT)))
                nc.vector.tensor_scalar(col(7), ps_fm[:, 16:17], -1.0, float(CAP), ALU.mult, ALU.add)
                step(nc.vector.scalar_tensor_tensor(lo_left, hi_left, col(6), keys_lo[:, e, :], ALU.is_equal, ALU.mult))
                search_key(lo_left, col(7))
                nc.vector.tensor_scalar(tie, lo_left, col(6), None, ALU.is_equal)
                summed(nc.vector.tensor_scalar(chosen, lo_left, col(6), None, ALU.is_gt, ALU.add, accum_out=col(CNT)))
                step(nc.vector.tensor_tensor(col(8), col(7), ps_fm[:, 16:17], ALU.subtract))
                summed(nc.vector.tensor_tensor_scan(scan_tie, tie, zeros512, 0.0, ALU.add, ALU.add))
                step(nc.vector.tensor_tensor(col(8), col(8), ps_fm[:, 16:17], ALU.subtract))
                step(nc.vector.scalar_tensor_tensor(tie, scan_tie, col(8), tie, ALU.is_le, ALU.mult))
                step(nc.vector.tensor_tensor(above, above, tie, ALU.add))
                step(nc.vector.tensor_tensor(chosen, chosen, above, ALU.add))
                nc.vector.tensor_tensor(free, free, chosen, ALU.subtract)
                summed(nc.vector.tensor_tensor_scan(scan, chosen, zeros512, 0.0, ALU.add, ALU.add))
                step(nc.vector.tensor_tensor(col(10), ps_fm[:, 17:18], col(9), ALU.add))
                nc.vector.tensor_scalar(col(9), col(9), float(CAP), None, ALU.add)
                step(nc.vector.scalar_tensor_tensor(scan, scan, col(10), chosen, ALU.add, ALU.mult))
                step(nc.vector.tensor_tensor(slot_sum, slot_sum, scan, ALU.add))
                while m[0] < STEPS:
                    m[0] += 1
                    dve.sem_inc(step_ok, 1)
                assert m[0] == STEPS and c[0] == COUNTS, (m, c)
            for e in range(NE):
                dve.wait_ge(key_in[e], 16 * 32)
            with dve.Fori(0, NE) as e:
                assign(e)
            dve.sem_inc(slots_ok, 1)
            dve.wait_ge(slots_tp, 1)
            nc.vector.tensor_copy(slots[:].rearrange("p (q j) -> p q j", j=4),
                                  ps_t4[:, 0:32].rearrange("p (j q) -> p q j", q=8)).then_inc(slots_ok, 1)

            for e in range(NE):
                u = e % 2
                k = LN_MOE + e
                dve.wait_ge(routed_in[u], 16 * (e // 2 + 1))
                if e >= 2:
                    dve.wait_ge(routed_t, e - 1)
                tiles = quarters(routed[:, u, :])
                ln_begin(dve, tiles, k, u)
                ln_end(dve, tiles, quarters(xn[:, u, :]), k, u)
                dve.wait_ge(moe_y_ps, e + 1)
                nc.vector.tensor_tensor(routed[:, u, :], routed[:, u, :], ps_y4[:, :], ALU.add).then_inc(moe_y_sb, 1)
            dve.wait_ge(gathered, 16 * NT)
            flat = "p t d -> p (t d)"
            nc.vector.tensor_tensor(X[:].rearrange(flat), X[:].rearrange(flat), R[:].rearrange(flat),
                                    ALU.add).then_inc(moe_added, 1)

            dve.wait_ge(moe_added, 1)
            with dve.Fori(0, NG // 2) as h:
                for u in range(2):
                    k, G = 2 * h + (LN_ATT + u), 2 * h + (T4_ATT + u)
                    xs = [X[:, 8 * h + (4 * u + j), :] for j in range(4)]
                    ln_begin(dve, xs, k, u)
                    dve.wait_ge(t4_ps, after(G - 2))
                    ln_end(dve, xs, quarters(xn[:, u, :]), k, u)
                    dve.wait_ge(z_ready, after(2 * h + u))
                    for j, dst in enumerate((qT_all, kT_all)):
                        last = nc.vector.tensor_scalar(dst.rearrange("p (g n) -> p g n", n=512)[:, 2 * h + u, :],
                                                       rows512[:, u, :], gam_bet[:, 0, j:j + 1], gam_bet[:, 1, j:j + 1],
                                                       ALU.mult, ALU.add)
                    last.then_inc(qk_ready, 1)

            dve.wait_ge(bias_in, 16)
            group = 0
            def add_av(group):
                b, half = UNITS[ENDS[group]][0:2]
                dve.wait_ge(avT_ps, group + 1)
                t0 = TPS * b + 4 * half
                xg = X[:, t0:t0 + 4, :].rearrange("p t d -> p (t d)")
                nc.vector.tensor_tensor(xg, xg, ps_t4[:, :], ALU.add).then_inc(av_added, 1)
            def make_z(i):
                b, half, m, n0, n = UNITS[i]
                x0, z = n0 - P * m, z_sb[:, i % 2, 0:n]
                dve.wait_ge(sim_ps, i + 1)
                if i >= 2:
                    dve.wait_ge(gelu_ok, i - 1)
                nc.vector.scalar_tensor_tensor(z, ps_sim[i % 3][:, 0:n], float(1 / (SEQ * STD)), toeplitz[:, x0:x0 + n],
                                               ALU.mult, ALU.add).then_inc(z1_sb, 1)
                dve.wait_ge(z1_sb, i + 1)
                nc.vector.tensor_scalar(z, z, 0.75, 2.0 ** -26, ALU.subtract, ALU.add).then_inc(z_ok, 1)
                dve.wait_ge(z_ok, i + 1)
                nc.vector.reciprocal(recip_sb[:, i % 2, 0:n], z).then_inc(recip_ok, 1)
            def make_w(i):
                n = UNITS[i][4]
                dve.wait_ge(gelu_ok, i + 1)
                dve.wait_ge(recip_ok, i + 1)
                if i >= 2:
                    dve.wait_ge(pv_done, i - 1)
                nc.vector.tensor_tensor(w_sb[:, i % 2, 0:n], gelu_sb[:, i % 2, 0:n], recip_sb[:, i % 2, 0:n],
                                        ALU.mult).then_inc(w_ok, 1)
            make_z(0)
            for i in range(NU):
                if i + 1 < NU:
                    make_z(i + 1)
                make_w(i)
                if group < len(ENDS) and i == ENDS[group] + 3:
                    add_av(group)
                    group += 1
            add_av(group)
            dve.wait_ge(av_added, group + 1)

            with dve.Fori(0, NG // 2) as h:
                for u in range(2):
                    k, G = 2 * h + (LN_TOP + u), 2 * h + (T4_TOP + u)
                    xs = [X[:, 8 * h + (4 * u + j), :] for j in range(4)]
                    ln_begin(dve, xs, k, u)
                    dve.wait_ge(t4_ps, after(G - 2))
                    ln_end(dve, xs, quarters(xn[:, u, :]), k, u)
                    dve.wait_ge(logit_ps, after(2 * h + u))
                    nc.vector.tensor_tensor(logits.rearrange("p (g t) e -> p g t e", t=4)[:, 2 * h + u],
                                            ps_y4[:, 0:4 * NE].rearrange("p (t e) -> p t e", e=NE),
                                            rb2[:].unsqueeze(1).to_broadcast([P, 4, NE]), ALU.add).then_inc(logit_sb, 1)
            dve.wait_ge(logit_sb, after(NG - 1))

            n_steps[0] = start + NE * STEPS

            def over(ap):
                return ap.unsqueeze(2).to_broadcast([P, NT, NE])

            def first_of(values, top, out):
                step(nc.vector.tensor_tensor(out, values, over(top), ALU.is_equal))
                step(nc.vector.tensor_tensor(out, out, order.unsqueeze(1).to_broadcast([P, NT, NE]), ALU.mult))
                step(nc.vector.tensor_reduce(peak[:, 3, :], out, AX.X, ALU.max))
                step(nc.vector.tensor_tensor(out, out, over(peak[:, 3, :]), ALU.is_equal))
            step(nc.vector.tensor_reduce(peak[:, 0, :], logits, AX.X, ALU.max))
            nc.vector.tensor_tensor(route[:, 2], logits, over(peak[:, 0, :]), ALU.subtract).then_inc(shift_ok, 1)
            first_of(logits, peak[:, 0, :], route[:, 0])
            step(nc.vector.scalar_tensor_tensor(
                route[:, 1].rearrange("p t e -> p (t e)"), route[:, 0].rearrange("p t e -> p (t e)"), -3e38,
                logits.rearrange("p t e -> p (t e)"), ALU.mult, ALU.add))
            step(nc.vector.tensor_reduce(peak[:, 1, :], route[:, 1], AX.X, ALU.max))
            first_of(route[:, 1], peak[:, 1, :], gates[:])
            step(nc.vector.tensor_tensor(gates[:], gates[:], route[:, 0], ALU.add))
            dve.wait_ge(exp_ok, 1)
            step(nc.vector.tensor_tensor(gates[:], gates[:], route[:, 3], ALU.mult))
            step(nc.vector.tensor_reduce(peak[:, 2, :], gates[:], AX.X, ALU.add))
            step(nc.vector.reciprocal(peak[:, 1, :], peak[:, 2, :]))
            nc.vector.tensor_tensor(gates[:], gates[:], over(peak[:, 1, :]), ALU.mult).then_inc(gates_ok, 1)
            for g in range(NG):
                dve.wait_ge(gate_b, g + 1)
                xg = X[:, 4 * g:4 * g + 4, :].rearrange("p t d -> p (t d)")
                nc.vector.tensor_tensor(xg, xg, ps_y4[:, :], ALU.add).then_inc(gate_added, 1)
            dve.wait_ge(gate_added, NG)
            for e in range(NE):
                with dve.Fori(0, NG // 2) as h:
                    for u in range(2):
                        U = 2 * h + (NG * e + u)
                        dve.wait_ge(top_y_ps, after(U))
                        if e:
                            dve.wait_ge(top_added, after(2 * h + (NG * (e - 1) + u)))
                        for j in range(4):
                            t = 8 * h + (4 * u + j)
                            last = nc.vector.scalar_tensor_tensor(X[:, t, :], ps_top[u][:, P * j:P * (j + 1)],
                                                                  gates[:, t, e:e + 1], X[:, t, :], ALU.mult, ALU.add)
                        last.then_inc(top_added, 1)

        @block.gpsimd
        def _(pool):
            for s in names["pool"]:
                pool.sem_inc(s, CREDIT)
            nc.gpsimd.memset(mhalf[:], -0.5).then_inc(const_ok, 1)
            nc.gpsimd.memset(eps4[:], EPS).then_inc(const_ok, 1)
            pool.wait_ge(const_ok, 4)
            pool.wait_ge(loaded, 16 * LOADS)
            with pool.Fori(0, NG // 2) as h:
                for u in range(2):
                    ln_root(pool, 4, 2 * h + u, u)

            def spread(T, u):
                pool.wait_ge(qk_sb, after(T))
                pool.wait_ge(o_ps, after(T - 2))
                for src, mask, dst in ((qs, quad_mask, q_quads), (ks, slot_mask, k_slots)):
                    last = nc.gpsimd.tensor_tensor(
                        dst[:, u], src[:, :].rearrange("p (s n) -> p s n", s=4).unsqueeze(2).to_broadcast([P, 4, 4, SUB]),
                        mask.unsqueeze(1).unsqueeze(3).to_broadcast([P, 4, 4, SUB]), ALU.mult)
                last.then_inc(qk_spread, 1)

            def decay_kv(T, i, u):
                pool.wait_ge(kv_biased, after(T))
                c0 = 4 * (i % TPS)
                nc.gpsimd.tensor_tensor(kv[:, u, :, 0:P], kv[:, u, :, 0:P], decay_rows[:, c0:c0 + 4, :], ALU.mult)
                nc.gpsimd.tensor_tensor(kv[:, u, :, P:2 * P], kv[:, u, :, P:2 * P],
                                        slot_rows.unsqueeze(1).to_broadcast([P, 4, P]), ALU.mult).then_inc(kv_ready, 1)

            def retention_tile(b, i, l, left=8):
                T, k = TPS * b + (l * NT + i), TPS * b + (LN_RET[l] + i)
                u = i % 2
                if left > 2:
                    ln_root(pool, 1, k + 2, u)
                if left > 1:
                    spread(T + 1, 1 - u)
                    decay_kv(T + 1, i + 1, 1 - u)

            def ffn_bias(h, u, l):
                G = 2 * h + (l * NG + u)
                pool.wait_ge(y4_done, after(G))
                r = R[:, :, :].rearrange("p (g t) d -> p g t d", t=4)[:, 2 * h + u, :, :]
                nc.gpsimd.tensor_tensor(r, r, ffn2_b[:, l, :].unsqueeze(1).to_broadcast([P, 4, P]),
                                        ALU.add).then_inc(bias_done, 1)

            for l in range(LAYERS):
                for i in range(2):
                    ln_root(pool, 1, LN_RET[l] + i, i)
                spread(l * NT, 0)
                decay_kv(l * NT, 0, 0)
                with pool.Fori(0, NB - 1) as b:
                    for i in range(TPS):
                        retention_tile(b, i, l)
                for i in range(TPS):
                    retention_tile(NB - 1, i, l, left=TPS - i)
                ln_root(pool, 4, LN_FFN[l], 0)
                ln_root(pool, 4, LN_FFN[l] + 1, 1)
                with pool.Fori(0, NG // 2 - 1) as h:
                    for u in range(2):
                        ffn_bias(h, u, l)
                        ln_root(pool, 4, 2 * h + (LN_FFN[l] + u + 2), u)
                for u in range(2):
                    ffn_bias(NG // 2 - 1, u, l)
            with pool.Fori(0, NG // 2) as h:
                for u in range(2):
                    g, k = 2 * h + u, 6 * h + (LN_FIN + 3 * u)
                    ln_root(pool, 4, k, u)
                    pool.wait_ge(ln_out, after(k))
                    y = xn[:, u, :].rearrange("p (t d) -> p t d", t=4)
                    nc.gpsimd.tensor_tensor(y, y, lnf_g[:, :].unsqueeze(1).to_broadcast([P, 4, P]), ALU.mult).then_inc(fin_g, 1)
                    pool.wait_ge(fin_g, after(g))
                    nc.gpsimd.tensor_tensor(y, y, lnf_b[:, :].unsqueeze(1).to_broadcast([P, 4, P]), ALU.add).then_inc(fin_b, 1)
                    ln_root(pool, 4, k + 1, u)
                    ln_root(pool, 4, k + 2, u)

            pool.wait_ge(slots_ok, 2)
            for t in range(NT):
                nc.gpsimd.indirect_dma_start(
                    out=routed_d, out_offset=bass.IndirectOffsetOnAxis(ap=slots[:, t:t + 1], axis=0),
                    in_=R[:, t, :], in_offset=None).then_inc(scattered, 16)
            for e in range(NE):
                ln_root(pool, 4, LN_MOE + e, e % 2)
                pool.wait_ge(moe_y_sb, e + 1)
                r = routed[:, e % 2, :].rearrange("p (t d) -> p t d", t=4)
                nc.gpsimd.tensor_tensor(r, r, moe_b2[:, e, :].unsqueeze(1).to_broadcast([P, 4, P]),
                                        ALU.add).then_inc(moe_out, 1)
            for u in range(2):
                pool.wait_ge(moe_stored[u], 16 * NE // 2)
            for t in range(NT):
                nc.gpsimd.indirect_dma_start(
                    out=R[:, t, :], out_offset=None, in_=moe_d,
                    in_offset=bass.IndirectOffsetOnAxis(ap=slots[:, t:t + 1], axis=0)).then_inc(gathered, 16)

            with pool.Fori(0, NG // 2) as h:
                for u in range(2):
                    ln_root(pool, 4, 2 * h + (LN_ATT + u), u)
            for n, i in enumerate(DIAG):
                pool.wait_ge(w_ok, i + 1)
                nc.gpsimd.affine_select(out=w_sb[:, i % 2, 0:P], in_=w_sb[:, i % 2, 0:P], compare_op=ALU.is_ge, fill=0.0,
                                        base=0, pattern=[[1, P]], channel_multiplier=-1).then_inc(masked, 1)
            with pool.Fori(0, NG // 2) as h:
                for u in range(2):
                    ln_root(pool, 4, 2 * h + (LN_TOP + u), u)


def kernel(**inputs):
    import numpy as _np
    import concourse.bacc as _bacc
    from concourse import mybir as _mybir
    from concourse.bass_utils import run_bass_kernel_spmd as _run

    nc = _bacc.Bacc("TRN2", target_bir_lowering=False, num_devices=1)
    arrays, aps = {}, {}
    for name, a in list(inputs.items()) + list(constants().items()):
        a = _np.ascontiguousarray(a)
        arrays[f"in_{name}_dram"] = a
        aps[name] = nc.dram_tensor(f"in_{name}_dram", a.shape, _mybir.dt.from_np(a.dtype), kind="ExternalInput").ap()
    out = nc.dram_tensor("out_0_dram", (NB, SEQ, P), F32, kind="ExternalOutput").ap()
    mega_kernel(nc, aps, out)
    r = _run(nc, [arrays], core_ids=[0])
    return r.results[0]["out_0_dram"]
```

```python
from contextlib import ExitStack

import numpy as np

import concourse.bass as bass
from concourse import mybir

F32 = mybir.dt.float32
I32 = mybir.dt.int32
U32 = mybir.dt.uint32
ALU = mybir.AluOpType
ACT = mybir.ActivationFunctionType
AX = mybir.AxisListType

P = 128
NB = 4
SEQ = 1024
TPS = SEQ // P
NT = NB * TPS
NG = NT // 4
TOK = NT * P
LAYERS = 2
SUB = 32
EPS = 1e-5
NE = 8
CAP = TOK // NE
FF = 4
MU = 0.5 ** 0.5
STD = (0.25 * np.pi) ** 0.5
CREDIT = 4
COUNTS = 12


COLUMNS = [("L0_attn_proj_b", np.s_[:], LAYERS * 4), ("L0_attn_ffn1_b", np.s_[:], LAYERS * FF),
           ("L0_attn_ln1_g", np.s_[:], LAYERS), ("L0_attn_ln1_b", np.s_[:], LAYERS),
           ("L0_attn_ln2_g", np.s_[:], LAYERS), ("L0_attn_ln2_b", np.s_[:], LAYERS),
           ("L0_ffn_b1", np.s_[:], NE * FF), ("L0_ffn_ln_g", np.s_[:], 1), ("L0_ffn_ln_b", np.s_[:], 1),
           ("L0_ffn_centroids", np.s_[:], NE), ("L1_attn_bqk", np.s_[:], 1),
           ("L1_attn_gamma", np.s_[:], 2), ("L1_attn_beta", np.s_[:], 2),
           ("L1_ffn_rb1", np.s_[:], FF), ("L1_ffn_b1", np.s_[:], NE * FF)]
REPEATED = [("L0_attn_proj_b", np.s_[:, P:3 * P], LAYERS * 2 * P), ("L0_attn_ffn2_b", np.s_[:], LAYERS * P),
            ("L0_attn_lnf_g", np.s_[:], P), ("L0_attn_lnf_b", np.s_[:], P),
            ("L0_ffn_b2", np.s_[:], NE * P), ("L1_ffn_rb2", np.s_[:], NE)]


def pack(inputs):
    columns = [np.asarray(inputs[name])[part].reshape(n, P).T for name, part, n in COLUMNS]
    rows = [np.asarray(inputs[name])[part].reshape(1, n) for name, part, n in REPEATED]
    return {"vectors": np.concatenate(columns, 1), "repeated": np.concatenate(rows, 1)}


def constants():
    head_gamma = 1.0 - 2.0 ** (-5.0 - np.arange(16, dtype=np.float64))
    g = np.repeat(head_gamma, 8)
    n = np.arange(SEQ, dtype=np.float64)
    p = np.arange(P)
    decay_q = g[:, None] ** n[None]
    decay_k = g[:, None] ** -n[None]
    slot = (p // 8) % 4
    m = p % SUB
    chunk = np.arange(SEQ // SUB)
    decay_rows = g[None, None, :] ** -(chunk[None, :, None] * SUB + m[:, None, None])
    decay_rows = decay_rows * (p[:, None, None] // SUB == slot[None, None, :])
    slot_rows = (p[:, None] // SUB == slot[None]).astype(np.float64)
    causal = (np.tile(np.arange(SUB), 4)[None] >= m[:, None]).astype(np.float64)
    slot_mask = (slot[:, None] == np.arange(4)[None]).astype(np.float64)
    quad_mask = (p[:, None] // 32 == np.arange(4)[None]).astype(np.float64)
    ident = np.eye(P)
    order = np.tile(8.0 - np.arange(8), (P, 1))
    small = np.concatenate([ident, causal, slot_rows, slot_mask, quad_mask, order], 1)
    d = np.maximum(np.arange(-P + 1, SEQ), 0)
    large = 16 + (np.log(np.maximum(d, 1) / 16) / np.log(8) * 16 + 1e-9).astype(int)
    bucket = np.where(d < 16, d, np.minimum(large, 31))
    onehot = (np.arange(32)[:, None] == bucket[None])
    onehot = np.concatenate([onehot, np.zeros((32, 1))], 1)
    dig, part = p // 8, p % 8
    steps = np.array([4096, 256, 16, 1])
    digit_hot = (dig[:, None] == np.arange(16)[None]).astype(np.float64)
    before = np.cumsum(steps) - steps
    thr = 1 + dig[:, None] * steps[None] - before[None]
    earlier = ((dig[:, None] == dig[None]) & (part[:, None] < part[None])).astype(np.float64)
    same = (dig[:, None] == dig[None]).astype(np.float64)
    search = np.concatenate([digit_hot, thr, earlier, same], 1)
    f = np.float32
    return {
        "decay_q": decay_q.astype(f), "decay_k": decay_k.astype(f),
        "decay_rows": decay_rows.reshape(P, -1).astype(f), "small": small.astype(f),
        "onehot": onehot.astype(f), "search": search.astype(f),
    }


def after(n):
    return n + 1 + CREDIT


def mega_kernel(nc, w, out):
    with ExitStack() as ctx:
        def sb(name, shape, dt=F32):
            return ctx.enter_context(nc.sbuf_tensor(name, shape, dt))

        def sem(name):
            return ctx.enter_context(nc.semaphore(name))

        X = sb("X", [P, NT, P])
        R = sb("R", [P, NT, P])
        small = sb("small", [P, 400])
        ident, causal, slot_rows = small[:, 0:128], small[:, 128:256], small[:, 256:384]
        slot_mask, quad_mask = small[:, 384:388], small[:, 388:392]
        order = small[:, 392:400]
        ones_row = sb("ones_row", [1, P])
        zeros = sb("zeros", [P, P])
        vectors = sb("vectors", [P, sum(n for _, _, n in COLUMNS)])
        repeated = sb("repeated", [P, sum(n for _, _, n in REPEATED)])

        def packed(buf, table):
            views, c = [], 0
            for _, _, n in table:
                views.append(buf[:, c:c + n])
                c += n
            return views
        (proj_bc, ffn1_b, ln1_g, ln1_b, ln2_g, ln2_b, moe_b1, moe_g, moe_b, centroids, bqk, gamma, beta,
         rb1, top_b1) = packed(vectors, COLUMNS)
        proj_bc = proj_bc.rearrange("p (l j) -> p l j", l=LAYERS)
        ffn1_b = ffn1_b.rearrange("p (l j) -> p l j", l=LAYERS)
        moe_b1 = moe_b1.rearrange("p (e f) -> p e f", e=NE)
        top_b1 = top_b1.rearrange("p (e f) -> p e f", e=NE)
        kv_bias, ffn2_b, lnf_g, lnf_b, moe_b2, rb2 = packed(repeated, REPEATED)
        kv_bias = kv_bias.rearrange("p (l n) -> p l n", l=LAYERS)
        ffn2_b = ffn2_b.rearrange("p (l n) -> p l n", l=LAYERS)
        moe_b2 = moe_b2.rearrange("p (e n) -> p e n", e=NE)
        decay_rows = sb("decay_rows", [P, SEQ // SUB, P])
        decay_q = sb("decay_q", [P, SEQ])
        decay_k = sb("decay_k", [P, SEQ])
        proj_w = sb("proj_w", [P, LAYERS, 512])
        reto_w = sb("reto_w", [P, LAYERS, P])
        reto_b = sb("reto_b", [1, LAYERS, P])
        ffn1_w = sb("ffn1_w", [P, LAYERS, 512])
        ffn2_w = sb("ffn2_w", [P, LAYERS, FF, P])
        moe_w1 = sb("moe_w1", [P, NE, 512])
        moe_w2 = sb("moe_w2", [P, NE, FF, P])
        arena = sb("arena", [P, TOK])
        keys_hi = decay_rows[:].rearrange("p c f -> p (c f)").rearrange("p (e f) -> p e f", e=NE)
        keys_lo = arena[:].rearrange("p (e f) -> p e f", e=NE)
        search = sb("search", [P, 276])
        digit_hot, thr_const = search[:, 0:16], search[:, 16:20]
        earlier, same_digit = search[:, 20:148], search[:, 148:276]
        all_ones = sb("all_ones", [P, P])
        score = sb("score", [P, NE, NT])
        key = decay_q[:].bitcast(U32).rearrange("p (a n) -> p a n", a=4)
        key_f, key_t = [decay_k[:, 512 * j:512 * (j + 1)].rearrange("p (a n) -> p a n", a=4) for j in range(2)]
        cols = sb("cols", [P, 16])
        hot_counts = sb("hot_counts", [P, 16])
        hot_junk = sb("hot_junk", [P, 16])
        slots = sb("slots", [P, NT], U32)
        keys_d = nc.dram_tensor("keys_d", (2, NE, NT, P), F32).ap()
        routed_d = nc.dram_tensor("routed_d", (TOK, P), F32).ap()
        moe_d = nc.dram_tensor("moe_d", (TOK, P), F32).ap()
        wqk, wv = sb("wqk", [P, P]), sb("wv", [P, P])
        bv_row = sb("bv_row", [1, P])
        rel_bias = sb("rel_bias", [32, 1])
        rel_rows = sb("rel_rows", [32, P])
        toeplitz = sb("toeplitz", [P, SEQ])
        qT_all = moe_w1[:].rearrange("p e n -> p (e n)")
        kT_all = moe_w2[:].rearrange("p e f n -> p (e f n)")
        v_all = R
        bias_d = nc.dram_tensor("bias_d", (P, SEQ + P), F32).ap()
        rw1 = sb("rw1", [P, 512])
        rw2 = sb("rw2", [P, FF, NE])
        top_b2 = sb("top_b2", [NE, P])
        top_w1 = decay_rows[:].rearrange("p (e f) n -> p e (f n)", e=NE)
        top_w2 = arena[:].rearrange("p (e f n) -> p e f n", e=NE, f=FF)
        logits = score[:].rearrange("p a b -> p (a b)").rearrange("p (t e) -> p t e", e=NE)
        gates = sb("gates", [P, NT, NE])
        route = sb("route", [P, 4, NT, NE])
        peak = sb("peak", [P, 4, NT])
        gatesT = sb("gatesT", [NE, 2, 512])
        stats = sb("stats", [P, 2, 4, 6])
        mv = sb("mv", [P, 2, 4, 2])
        veps = sb("veps", [P, 2, 4])
        rstd = sb("rstd", [P, 2, 4])
        mhalf, eps4 = sb("mhalf", [P, 4]), sb("eps4", [P, 4])
        xn = sb("xn", [P, 2, 512])
        xT = sb("xT", [P, 2, 512])
        x_rows = sb("x_rows", [P, 2, 4, 4, SUB])
        qs, ks = sb("qs", [P, P]), sb("ks", [P, P])
        q_quads = sb("q_quads", [P, 2, 4, 4, SUB])
        k_slots = sb("k_slots", [P, 2, 4, 4, SUB])
        gate_x = sb("gate_x", [P, 2, P])
        kv = sb("kv", [P, 2, 4, 256])
        probs = sb("probs", [P, 4, P])
        snap = sb("snap", [P, 4, P])
        ret = sb("ret", [P, 2, P])
        hid = sb("hid", [P, 2, FF, 512])

        routed = [b[:].rearrange("p u s g n -> p u (s g n)")[:, u, :] for b in (q_quads, k_slots) for u in range(2)]
        onehot = hid[0:32].rearrange("p u f n -> p (u f n)")[:, 0:SEQ + P]
        dist_bias = hid[:].rearrange("p u f n -> p (u f n)")[:, 2048:2048 + SEQ + P]
        rows512 = hid[:].rearrange("p u f n -> p (u f) n")
        hi_left, lo_left, free, slot_sum, chosen, scan, tie, scan_tie = [rows512[:, j, :] for j in range(8)]
        above, junk, zeros512 = xT[:, 0, :], xT[:, 1, :], xn[:, 0, :]
        CNT = 5

        _, gelu_sb, recip_sb, w_sb = [rows512[:, 2 * j:2 * j + 2, :] for j in range(4)]
        z_sb = [rows512[:, 0, :], rows512[:, 1, :], xn[:, 0, :]]
        av_sb = xT

        psum = [ctx.enter_context(nc.psum_tensor(f"ps{i}", [P, 512], F32)) for i in range(2)]
        psum2 = ctx.enter_context(nc.psum_tensor("psb", [P, 1024], F32))
        psum += [None, None] + [ctx.enter_context(nc.psum_tensor(f"ps{i}", [P, 512], F32)) for i in range(4, 8)]
        ps_xt = psum[0][:, 0:128]
        ps_y = psum[5][:, 0:128]
        ps_gate = psum[7][:, 0:128]
        ps_fm = psum[1]
        ps_kv = psum2[:, :].rearrange("p (s c) -> p s c", s=4)
        ps_sc = psum[4][:, :].rearrange("p (s c) -> p s c", s=4)
        ps_o = psum[5][:, :].rearrange("p (s g n) -> p s g n", s=4, g=4)
        ps_st = psum[6][:, 0:128]
        ps_t4 = psum[0]
        ps_h = [psum[1], psum[4], psum[5], psum[6]]
        ps_y4 = psum[7]
        ps_sim = [psum[1], psum[4], psum[5]]
        ps_av = [psum[6], psum[7]]
        ps_top = [psum[0], psum[7]]

        def YT(h, u):
            return R[:].rearrange("p (g t) d -> p g (t d)", t=4)[:, 2 * h + u, :]

        names = {}

        def counter(name, engine):
            s = sem(name)
            names.setdefault(engine, []).append(s)
            return s

        loaded = {phase: sem(f"loaded_{phase}") for phase in ("x0", "x", "bias", "retention", "decays", "ffn", "moe", "rest")}
        passed = sem("passed")
        stored = sem("stored")
        const_ok = sem("const_ok")
        ln_stats = counter("ln_stats", "dve")
        ln_moments = counter("ln_moments", "dve")
        ln_veps = counter("ln_veps", "pool")
        ln_rstd = counter("ln_rstd", "pool")
        ln_out = counter("ln_out", "dve")
        xt_ps = counter("xt_ps", "pe")
        xt_sb = counter("xt_sb", "act")
        fm_ps = counter("fm_ps", "pe")
        gate_ps = counter("gate_ps", "pe")
        kv_ps = counter("kv_ps", "pe")
        qk_sb = counter("qk_sb", "dve")
        gate_sb = counter("gate_sb", "act")
        kv_biased = counter("kv_biased", "dve")
        kv_ready = counter("kv_ready", "pool")
        qk_spread = counter("qk_spread", "pool")
        scores_ps = counter("scores_ps", "pe")
        probs_sb = counter("probs_sb", "dve")
        state_ps = sem("state_ps")
        snap_sb = sem("snap_sb")
        o_ps = counter("o_ps", "pe")
        ret_sb = counter("ret_sb", "dve")
        y_ps = counter("y_ps", "pe")
        res_done = counter("res_done", "dve")
        t4_ps = counter("t4_ps", "pe")
        t4_sb = counter("t4_sb", "act")
        h_ps = counter("h_ps", "pe")
        h_sb = counter("h_sb", "act")
        y4_ps = counter("y4_ps", "pe")
        y4_done = counter("y4_done", "dve")
        bias_done = counter("bias_done", "pool")
        fin_g = counter("fin_g", "pool")
        fin_b = counter("fin_b", "pool")
        fin_x = counter("fin_x", "dve")
        rsd = counter("rsd", "dve")

        y_norm = counter("y_norm", "dve")
        score_ps = counter("score_ps", "pe")
        score_sb = counter("score_sb", "dve")
        key_ok = sem("key_ok")
        key_tp = sem("key_tp")
        key_out = sem("key_out")
        key_in = [sem(f"key_in{e}") for e in range(NE)]
        step_ok = sem("step_ok")
        count_in = sem("count_in")
        count_ps = sem("count_ps")
        slots_tp = sem("slots_tp")
        slots_ok = sem("slots_ok")
        scattered = sem("scattered")
        routed_in = [sem(f"routed_in{u}") for u in range(4)]
        routed_t = sem("routed_t")
        routed_T = sem("routed_T")
        moe_h_ps = sem("moe_h_ps")
        moe_h_sb = sem("moe_h_sb")
        moe_y_ps = sem("moe_y_ps")
        moe_y_sb = sem("moe_y_sb")
        moe_out = sem("moe_out")
        moe_stored = [sem(f"moe_stored{u}") for u in range(4)]
        gathered = sem("gathered")
        moe_added = sem("moe_added")

        qk_ps = counter("qk_ps", "pe")
        v_ps = counter("v_ps", "pe")
        z_ready = counter("z_ready", "act")
        v_ready = counter("v_ready", "act")
        qk_ready = counter("qk_ready", "dve")
        late = sem("late")
        bias_ok = sem("bias_ok")
        bias_ps = sem("bias_ps")
        bias_out = sem("bias_out")
        bias_in = sem("bias_in")
        sim_ps = sem("sim_ps")
        z1_sb = sem("z1_sb")
        z_ok = sem("z_ok")
        gelu_ok = sem("gelu_ok")
        recip_ok = sem("recip_ok")
        w_ok = sem("w_ok")
        masked = sem("masked")
        av_ps = sem("av_ps")
        pv_done = sem("pv_done")
        av_ok = sem("av_ok")
        avT_ps = sem("avT_ps")
        av_added = sem("av_added")
        rel_ok = sem("rel_ok")
        logit_ps = counter("logit_ps", "pe")
        logit_sb = counter("logit_sb", "dve")
        shift_ok = sem("shift_ok")
        exp_ok = sem("exp_ok")
        gates_ok = sem("gates_ok")
        gate_t = sem("gate_t")
        gate_T = sem("gate_T")
        gate_b = sem("gate_b")
        gate_added = sem("gate_added")
        top_h_ps = counter("top_h_ps", "pe")
        top_h_sb = counter("top_h_sb", "act")
        top_y_ps = counter("top_y_ps", "pe")
        top_added = counter("top_added", "dve")

        UNITS = [(b, half, m, max(512 * half, P * m), 512 * (half + 1) - max(512 * half, P * m))
                 for b in range(NB) for half in range(2) for m in range(4 * half + 4)]
        NU = len(UNITS)
        DIAG = [i for i, x in enumerate(UNITS) if x[3] == P * x[2]]
        ENDS = [i for i, x in enumerate(UNITS) if x[2] == 4 * x[1] + 3]

        def masks_before(i):
            return sum(d <= i for d in DIAG)

        n_loads = {}

        def inputs_in(engine, *phases):
            for phase in phases:
                engine.wait_ge(loaded[phase], n_loads[phase])

        def ln_begin(dve, tiles, k, u):
            for j, t in enumerate(tiles):
                last = nc.vector.bn_stats(stats[:, u, j, :], t)
            last.then_inc(ln_stats, 1)
            dve.wait_ge(ln_stats, after(k))
            dve.sem_inc(passed, 1)
            for j in range(len(tiles)):
                last = nc.vector.bn_aggr(mv[:, u, j, :], stats[:, u, j, :])
            last.then_inc(ln_moments, 1)

        def ln_root(pool, n, k, u):
            pool.wait_ge(ln_moments, after(k))
            nc.gpsimd.tensor_tensor(veps[:, u, 0:n], mv[:, u, 0:n, 1], eps4[:, 0:n], ALU.add).then_inc(ln_veps, 1)
            pool.wait_ge(ln_veps, after(k))
            nc.gpsimd.tensor_tensor(rstd[:, u, 0:n], veps[:, u, 0:n], mhalf[:, 0:n], ALU.pow).then_inc(ln_rstd, 1)

        def ln_end(dve, tiles, outs, k, u):
            dve.wait_ge(ln_rstd, after(k))
            for j, (t, o) in enumerate(zip(tiles, outs)):
                last = nc.vector.tensor_scalar(o, t, mv[:, u, j, 0:1], rstd[:, u, j:j + 1],
                                               ALU.subtract, ALU.mult)
            last.then_inc(ln_out, 1)

        def quarters(ap):
            return [ap[:, P * j:P * (j + 1)] for j in range(4)]

        LN0 = 0
        LN_RET = [LN0 + NG, LN0 + NG + NT + NG]
        LN_FFN = [x + NT for x in LN_RET]
        LN_FIN = LN_FFN[1] + NG
        LN_MOE = LN_FIN + 3 * NG
        LN_ATT = LN_MOE + NE
        LN_TOP = LN_ATT + NG
        T4_ATT = (LAYERS + 1) * NG
        T4_TOP = T4_ATT + NG

        block = ctx.enter_context(nc.Block())

        @block.sync
        def _(sp):
            def load(phase, dst, src):
                sp.dma_start(dst, src, allow_slow_non_contiguous=True).then_inc(loaded[phase], 16)
                n_loads[phase] = n_loads.get(phase, 0) + 16
            load("x0", X[:, 0:TPS, :], w["L0_attn_x"][0].rearrange("(t p) d -> p t d", p=P))
            for b in range(1, NB):
                load("x", X[:, b * TPS:(b + 1) * TPS, :], w["L0_attn_x"][b].rearrange("(t p) d -> p t d", p=P))
            load("bias", rel_bias[:], w["L1_attn_rel_bias"].rearrange("(p o) -> p o", o=1))
            load("bias", onehot, w["onehot"])
            load("retention", small[:], w["small"])
            load("retention", vectors[:], w["vectors"])
            load("retention", proj_w[:], w["L0_attn_proj_w"].rearrange("l k n -> k l n"))
            load("retention", decay_q[:], w["decay_q"])
            load("retention", decay_k[:], w["decay_k"])
            load("retention", reto_w[:], w["L0_attn_reto_w"].rearrange("l k n -> k l n"))
            load("retention", reto_b[:], w["L0_attn_reto_b"].rearrange("(o l) n -> o l n", o=1))
            load("retention", repeated[:], w["repeated"].to_broadcast([P, repeated.shape[1]]))
            load("decays", decay_rows[:].rearrange("p c f -> p (c f)"), w["decay_rows"])
            load("ffn", ffn1_w[:], w["L0_attn_ffn1_w"].rearrange("l k n -> k l n"))
            load("ffn", ffn2_w[:], w["L0_attn_ffn2_w"].rearrange("l (f k) n -> k l f n", k=P))
            load("moe", moe_w1[:], w["L0_ffn_w1"].rearrange("e k n -> k e n"))
            load("moe", moe_w2[:], w["L0_ffn_w2"].rearrange("e (f k) n -> k e f n", k=P))
            load("moe", search[:], w["search"])
            load("rest", wqk[:], w["L1_attn_wqk"])
            load("rest", wv[:], w["L1_attn_wv"])
            load("rest", bv_row[:], w["L1_attn_bv"].rearrange("(o n) -> o n", o=1))
            load("rest", rw1[:], w["L1_ffn_rw1"])
            load("rest", rw2[:], w["L1_ffn_rw2"].rearrange("(f k) n -> k f n", k=P))
            load("rest", top_b2[:], w["L1_ffn_b2"])

            sp.wait_ge(bias_ok, 3)
            sp.dma_start(bias_d, dist_bias).then_inc(bias_out, 16)
            sp.wait_ge(bias_out, 16)
            sp.dma_start(toeplitz[:], bass.AP(bias_d.tensor, P - 1, [[SEQ + P - 1, P], [1, SEQ]])).then_inc(bias_in, 16)

            sp.wait_ge(key_ok, 3)
            sp.dma_start(keys_d.rearrange("h (a e) t n -> (e t) (h a) n", a=2), key_t).then_inc(key_out, 16)
            sp.wait_ge(key_out, 16)
            for e in range(NE):
                for h, keys in enumerate((keys_hi, keys_lo)):
                    src = keys_d[h, e].rearrange("(q t) n -> q (t n)", q=8).unsqueeze(0).to_broadcast([16, 8, 512])
                    sp.dma_start(keys[:, e, :], src).then_inc(key_in[e], 16)

            sp.wait_ge(slots_ok, 2)
            sp.dma_start(top_w1, w["L1_ffn_W1"].rearrange("e k n -> k e n")).then_inc(late, 16)
            sp.dma_start(top_w2, w["L1_ffn_W2"].rearrange("e (f k) n -> k e f n", k=P)).then_inc(late, 16)

            sp.wait_ge(scattered, 16 * NT)
            def rows_of(t, e):
                return t[CAP * e:CAP * (e + 1), :].rearrange("(t p) d -> p t d", p=P)
            for e in range(NE + 3):
                if e < NE:
                    if e >= 4:
                        sp.wait_ge(moe_stored[e % 4], 16 * (e // 4))
                    sp.dma_start(routed[e % 4].rearrange("p (t d) -> p t d", t=4),
                                 rows_of(routed_d, e)).then_inc(routed_in[e % 4], 16)
                d = e - 3
                if d >= 0:
                    sp.wait_ge(moe_out, d + 1)
                    sp.dma_start(rows_of(moe_d, d),
                                 routed[d % 4].rearrange("p (t d) -> p t d", t=4)).then_inc(moe_stored[d % 4], 16)
            for g in range(NG):
                sp.wait_ge(top_added, after((NE - 1) * NG + g))
                sp.dma_start(out.rearrange("b (t p) d -> p (b t) d", p=P)[:, 4 * g:4 * g + 4, :],
                             X[:, 4 * g:4 * g + 4, :]).then_inc(stored, 16)
            sp.wait_ge(stored, 16 * NG)

        @block.tensor
        def _(pe):
            for s in names["pe"]:
                pe.sem_inc(s, CREDIT)
            pe.wait_ge(const_ok, 4)
            inputs_in(pe, "bias")
            pe.wait_ge(rel_ok, 1)
            for j, (c0, n) in enumerate(((0, 512), (512, 512), (1024, P))):
                m = nc.tensor.matmul(psum[(0, 1, 4)[j]][0:P, 0:n], rel_rows[:], onehot[:, c0:c0 + n], start=True, stop=True)
            m.then_inc(bias_ps, 1)
            pe.wait_ge(bias_ok, 3)
            inputs_in(pe, "retention")

            def transpose_tile(T, u, lnk):
                pe.wait_ge(ln_out, after(lnk))
                pe.wait_ge(xt_sb, after(T - 1))
                nc.tensor.transpose(ps_xt, xn[:, u, 0:P], ident).then_inc(xt_ps, 1)

            def project(T, u, l):
                pe.wait_ge(xt_sb, after(T))
                pe.wait_ge(qk_sb, after(T - 1))
                x = x_rows[:, u, :, 0, :]
                for c in range(2):
                    last = nc.tensor.matmul(ps_fm[:, c * P:(c + 1) * P], proj_w[:, l, c * P:(c + 1) * P], x,
                                            start=True, stop=True)
                last.then_inc(fm_ps, 1)
                pe.wait_ge(gate_sb, after(T - 1))
                nc.tensor.matmul(ps_gate, proj_w[:, l, 3 * P:4 * P], x, start=True, stop=True).then_inc(gate_ps, 1)

            def project_kv(T, u, l):
                pe.wait_ge(kv_biased, after(T - 1))
                for s in range(4):
                    rows = x_rows[:, u, s].rearrange("p a b -> p (a b)")
                    last = nc.tensor.matmul(ps_kv[:, s, :], rows, proj_w[:, l, P:3 * P], start=True, stop=True)
                last.then_inc(kv_ps, 1)

            def scores(T, u, slots):
                if slots[0] == 0:
                    pe.wait_ge(qk_spread, after(T))
                    pe.wait_ge(probs_sb, after(T - 1))
                for s in slots:
                    last = nc.tensor.matmul(ps_sc[:, s, :], k_slots[:, u, s].rearrange("p a b -> p (a b)"),
                                            q_quads[:, u, s].rearrange("p a b -> p (a b)"), start=True, stop=True)
                if slots[-1] == 3:
                    last.then_inc(scores_ps, 1)

            def retain(T, u, seq, i, k, left):
                if i == 0:
                    nc.tensor.matmul(ps_st, zeros[:], zeros[:], start=True, stop=False,
                                     skip_group_check=True).then_inc(state_ps, 1)
                pe.wait_ge(kv_ready, after(T))
                pe.wait_ge(ret_sb, after(T - 1))
                pe.wait_ge(res_done, after(T - 1))
                for s in range(4):
                    if s == 3 and left > 2:
                        transpose_tile(T + 2, u, k + 2)
                    pe.wait_ge(snap_sb, 32 * seq + 4 * i + s + 1)
                    nc.tensor.matmul(ps_st, kv[:, u, s, 0:P], kv[:, u, s, P:2 * P], start=False, stop=False,
                                     skip_group_check=True).then_inc(state_ps, 1)
                    o = ps_o[:, s].rearrange("p g n -> p (g n)")
                    nc.tensor.matmul(o, snap[:, s, :], q_quads[:, u, s].rearrange("p a b -> p (a b)"),
                                     start=True, stop=False)
                    if s == 0:
                        pe.wait_ge(probs_sb, after(T))
                    last = nc.tensor.matmul(o, kv[:, u, s, P:2 * P], probs[:, s, :], start=False, stop=True)
                    if s == 3:
                        last.then_inc(o_ps, 1)
                    if left > 1 and s:
                        scores(T + 1, 1 - u, ((), (0,), (1,), (2, 3))[s])

            def project_out(T, u, l):
                pe.wait_ge(ret_sb, after(T))
                nc.tensor.matmul(ps_y, ret[:, u, :], reto_w[:, l, :], start=True, stop=False)
                nc.tensor.matmul(ps_y, ones_row[0:1, :], reto_b[0:1, l, :], start=False, stop=True).then_inc(y_ps, 1)

            def retention_tile(b, i, l, first=False, left=8):
                T, k = l * NT + TPS * b + i, LN_RET[l] + TPS * b + i
                u = i % 2
                if left > 1:
                    project(T + 1, 1 - u, l)
                if not first:
                    project_out(T - 1, 1 - u, l)
                if left > 1:
                    project_kv(T + 1, 1 - u, l)
                retain(T, u, l * NB + b, i, k, left)

            def transposes(k, G, u):
                pe.wait_ge(ln_out, after(k))
                pe.wait_ge(t4_sb, after(G - 1))
                for j in range(4):
                    t = nc.tensor.transpose(ps_t4[:, P * j:P * (j + 1)], xn[:, u, P * j:P * (j + 1)], ident)
                t.then_inc(t4_ps, 1)

            def ffn_hidden(G, u, l):
                pe.wait_ge(t4_sb, after(G))
                for f in range(FF):
                    pe.wait_ge(h_sb, after(4 * (G - 1) + f))
                    nc.tensor.matmul(ps_h[f][:, :], ffn1_w[:, l, P * f:P * (f + 1)], xT[:, u, :],
                                     start=True, stop=True).then_inc(h_ps, 1)

            def ffn_out(G, u, l):
                pe.wait_ge(h_sb, after(4 * G + 3))
                pe.wait_ge(y4_done, after(G - 1))
                for j in range(4):
                    for f in range(FF):
                        m = nc.tensor.matmul(ps_y4[:, P * j:P * (j + 1)], hid[:, u, f, P * j:P * (j + 1)],
                                             ffn2_w[:, l, f, :], start=(f == 0), stop=(f == FF - 1))
                m.then_inc(y4_ps, 1)

            def ffn_step(g, u, l, left=NG):
                G, k = l * NG + g, LN_FFN[l] + g
                if left > 1:
                    ffn_hidden(G + 1, 1 - u, l)
                if left > 2:
                    transposes(k + 2, G + 2, u)
                ffn_out(G, u, l)

            for l in range(LAYERS):
                for i in range(2):
                    transpose_tile(l * NT + i, i, LN_RET[l] + i)
                project(l * NT, 0, l)
                project_kv(l * NT, 0, l)
                scores(l * NT, 0, (0, 1, 2, 3))
                for i in range(TPS):
                    retention_tile(0, i, l, first=i == 0)
                with pe.Fori(1, NB - 1) as b:
                    for i in range(TPS):
                        retention_tile(b, i, l)
                for i in range(TPS):
                    retention_tile(NB - 1, i, l, left=TPS - i)
                project_out(l * NT + NT - 1, 1, l)
                if l == 0:
                    inputs_in(pe, "ffn")
                transposes(LN_FFN[l], l * NG, 0)
                ffn_hidden(l * NG, 0, l)
                transposes(LN_FFN[l] + 1, l * NG + 1, 1)
                with pe.Fori(0, NG // 2 - 1) as h:
                    for u in range(2):
                        ffn_step(2 * h + u, u, l)
                for u in range(2):
                    ffn_step(NG - 2 + u, u, l, left=2 - u)

            def score_group(h, u):
                G = 2 * h + (LAYERS * NG + u)
                transposes(2 * h + (LN_FIN + 2 * NG + u), G, u)
                pe.wait_ge(t4_sb, after(G))
                pe.wait_ge(score_sb, after(2 * h + (u - 1)))
                for j in range(4):
                    m = nc.tensor.matmul(ps_y4[:, NE * j:NE * (j + 1)], xT[:, u, P * j:P * (j + 1)], centroids[:],
                                         start=True, stop=True)
                m.then_inc(score_ps, 1)
            with pe.Fori(0, NG // 2) as h:
                for u in range(2):
                    score_group(h, u)

            pe.wait_ge(key_ok, 1)
            for j in range(4):
                t = nc.tensor.transpose(ps_t4[:, P * j:P * (j + 1)], key_f[:, j, :], ident)
            t.then_inc(key_tp, 1)

            inputs_in(pe, "moe")
            with pe.Fori(0, NE) as e:
                for n in range(COUNTS):
                    pe.wait_ge(count_in, COUNTS * e + (n + 1))
                    if n < 4 or 5 <= n < 9:
                        m = nc.tensor.matmul(ps_fm[:, 0:16], all_ones[:], hot_counts[:], start=True, stop=True)
                    elif n in (4, 9):
                        m = nc.tensor.matmul(ps_fm[:, 16:17], same_digit, cols[:, CNT:CNT + 1], start=True, stop=True)
                    elif n == 10:
                        m = nc.tensor.matmul(ps_fm[:, 16:17], earlier, scan_tie[:, 511:512], start=True, stop=True)
                    else:
                        m = nc.tensor.matmul(ps_fm[:, 17:18], earlier, scan[:, 511:512], start=True, stop=True)
                    m.then_inc(count_ps, 1)
            pe.wait_ge(slots_ok, 1)
            for j in range(4):
                t = nc.tensor.transpose(ps_t4[:, 8 * j:8 * j + 8], slot_sum[0:8, P * j:P * (j + 1)], ident[0:8, 0:8])
            t.then_inc(slots_tp, 1)

            inputs_in(pe, "rest")
            def moe_transposes(e):
                pe.wait_ge(ln_out, after(LN_MOE + e))
                if e:
                    pe.wait_ge(routed_T, e)
                for j in range(4):
                    t = nc.tensor.transpose(ps_t4[:, P * j:P * (j + 1)], xn[:, e % 2, P * j:P * (j + 1)], ident)
                t.then_inc(routed_t, 1)

            def moe_hidden(e):
                pe.wait_ge(routed_T, e + 1)
                for f in range(FF):
                    if e:
                        pe.wait_ge(moe_h_sb, 4 * (e - 1) + f + 1)
                    nc.tensor.matmul(ps_h[f][:, :], moe_w1[:, e, P * f:P * (f + 1)], xT[:, e % 2, :],
                                     start=True, stop=True).then_inc(moe_h_ps, 1)

            pe.wait_ge(slots_ok, 2)
            moe_transposes(0)
            moe_hidden(0)
            moe_transposes(1)
            for e in range(NE):
                if e + 1 < NE:
                    moe_hidden(e + 1)
                if e + 2 < NE:
                    moe_transposes(e + 2)
                pe.wait_ge(moe_h_sb, 4 * e + 4)
                if e:
                    pe.wait_ge(moe_y_sb, e)
                for j in range(4):
                    for f in range(FF):
                        m = nc.tensor.matmul(ps_y4[:, P * j:P * (j + 1)], hid[:, e % 2, f, P * j:P * (j + 1)],
                                             moe_w2[:, e, f, :], start=(f == 0), stop=(f == FF - 1))
                m.then_inc(moe_y_ps, 1)

            pe.wait_ge(moe_added, 1)
            def projections(g, u, left=NG):
                if left > 1:
                    transposes(LN_ATT + g + 1, T4_ATT + g + 1, 1 - u)
                pe.wait_ge(t4_sb, after(T4_ATT + g))
                pe.wait_ge(z_ready, after(g - 2))
                nc.tensor.matmul(ps_h[2 * u][:, :], wqk[:], xT[:, u, :], start=True, stop=True).then_inc(qk_ps, 1)
                pe.wait_ge(v_ready, after(g - 2))
                for j in range(4):
                    o = ps_h[2 * u + 1][:, P * j:P * (j + 1)]
                    nc.tensor.matmul(o, xT[:, u, P * j:P * (j + 1)], wv[:], start=True, stop=False)
                    m = nc.tensor.matmul(o, ones_row[0:1, :], bv_row[0:1, :], start=False, stop=True)
                m.then_inc(v_ps, 1)
            transposes(LN_ATT, T4_ATT, 0)
            with pe.Fori(0, NG // 2 - 1) as h:
                for u in range(2):
                    projections(2 * h + u, u)
            for u in range(2):
                projections(NG - 2 + u, u, left=2 - u)

            def similarity(i):
                b, half, m, n0, n = UNITS[i]
                if i >= 3:
                    pe.wait_ge(z1_sb, i - 2)
                if i == 0:
                    pe.wait_ge(qk_ready, after(NG - 1))
                    pe.wait_ge(v_ready, after(NG - 1))
                nc.tensor.matmul(ps_sim[i % 3][:, 0:n], kT_all[:, SEQ * b + P * m:SEQ * b + P * (m + 1)],
                                 qT_all[:, SEQ * b + n0:SEQ * b + n0 + n], start=True, stop=True).then_inc(sim_ps, 1)

            def weigh(i, group):
                b, half, m, n0, n = UNITS[i]
                if m == 0 and group >= 2:
                    pe.wait_ge(av_ok, group - 1)
                pe.wait_ge(w_ok, i + 1)
                if i in DIAG:
                    pe.wait_ge(masked, masks_before(i))
                x = nc.tensor.matmul(ps_av[group % 2][:, n0 - 512 * half:512], v_all[:, TPS * b + m, :], w_sb[:, i % 2, 0:n],
                                     start=(m == 0), stop=(i in ENDS))
                x.then_inc(pv_done, 1)

            def turn(group):
                pe.wait_ge(av_ok, group + 1)
                if group:
                    pe.wait_ge(av_added, group)
                for j in range(4):
                    t = nc.tensor.transpose(ps_t4[:, P * j:P * (j + 1)], av_sb[:, group % 2, P * j:P * (j + 1)], ident)
                t.then_inc(avT_ps, 1)

            for i in range(3):
                similarity(i)
            group = 0
            for i in range(NU):
                if i + 3 < NU:
                    similarity(i + 3)
                weigh(i, group)
                if group and i == ENDS[group - 1] + 1:
                    turn(group - 1)
                if i in ENDS:
                    group += 1
            turn(group - 1)

            pe.wait_ge(av_added, group)
            def router_hidden(h, u):
                pe.wait_ge(t4_sb, after(2 * h + (T4_TOP + u)))
                for f in range(FF):
                    pe.wait_ge(top_h_sb, after(8 * h + (4 * u + f - 4)))
                    nc.tensor.matmul(ps_h[f][:, :], rw1[:, P * f:P * (f + 1)], YT(h, u),
                                     start=True, stop=True).then_inc(top_h_ps, 1)

            def router_step(h, u, left=NG):
                if left > 1:
                    router_hidden(h + u, 1 - u)
                if left > 2:
                    transposes(2 * h + (LN_TOP + u + 2), 2 * h + (T4_TOP + u + 2), u)
                pe.wait_ge(top_h_sb, after(8 * h + (4 * u + 3)))
                pe.wait_ge(logit_sb, after(2 * h + (u - 1)))
                for j in range(4):
                    for f in range(FF):
                        m = nc.tensor.matmul(ps_y4[:, NE * j:NE * (j + 1)], hid[:, u, f, P * j:P * (j + 1)],
                                             rw2[:, f, :], start=(f == 0), stop=(f == FF - 1))
                m.then_inc(logit_ps, 1)

            transposes(LN_TOP, T4_TOP, 0)
            router_hidden(0, 0)
            transposes(LN_TOP + 1, T4_TOP + 1, 1)
            with pe.Fori(0, NG // 2 - 1) as h:
                for u in range(2):
                    router_step(h, u)
            for u in range(2):
                router_step(NG // 2 - 1, u, left=2 - u)

            pe.wait_ge(gates_ok, 1)
            for g in range(NG):
                u = g % 2
                if g:
                    pe.wait_ge(gate_T, g)
                for j in range(4):
                    t = nc.tensor.transpose(ps_t4[0:NE, P * j:P * (j + 1)], gates[:, 4 * g + j, :], ident)
                t.then_inc(gate_t, 1)
                pe.wait_ge(gate_T, g + 1)
                if g:
                    pe.wait_ge(gate_added, g)
                for j in range(4):
                    m = nc.tensor.matmul(ps_y4[:, P * j:P * (j + 1)], gatesT[:, u, P * j:P * (j + 1)], top_b2[:],
                                         start=True, stop=True)
                m.then_inc(gate_b, 1)
            pe.wait_ge(gate_added, NG)
            pe.wait_ge(late, 32)
            def top_hidden(e, h, u):
                for f in range(FF):
                    pe.wait_ge(top_h_sb, after(8 * h + (4 * (NG * (e + 1) + u) + f - 4)))
                    nc.tensor.matmul(ps_h[f][:, :], top_w1[:, e, P * f:P * (f + 1)], YT(h, u),
                                     start=True, stop=True).then_inc(top_h_ps, 1)

            def top_out(e, h, u):
                pe.wait_ge(top_h_sb, after(8 * h + (4 * (NG * (e + 1) + u) + 3)))
                pe.wait_ge(top_added, after(2 * h + (NG * e + u - 2)))
                for j in range(4):
                    for f in range(FF):
                        m = nc.tensor.matmul(ps_top[u][:, P * j:P * (j + 1)], hid[:, u, f, P * j:P * (j + 1)],
                                             top_w2[:, e, f, :], start=(f == 0), stop=(f == FF - 1))
                m.then_inc(top_y_ps, 1)

            top_hidden(0, 0, 0)
            for e in range(NE):
                with pe.Fori(0, NG // 2 - 1) as h:
                    top_hidden(e, h, 1)
                    top_out(e, h, 0)
                    top_hidden(e, h + 1, 0)
                    top_out(e, h, 1)
                top_hidden(e, NG // 2 - 1, 1)
                top_out(e, NG // 2 - 1, 0)
                if e + 1 < NE:
                    top_hidden(e + 1, 0, 0)
                top_out(e, NG // 2 - 1, 1)

        @block.scalar
        def _(act):
            for s in names["act"]:
                act.sem_inc(s, CREDIT)
            inputs_in(act, "retention")

            def copy_xt(T, u, l):
                act.wait_ge(xt_ps, after(T))
                act.wait_ge(kv_ps, after(T - 2))
                src = ps_xt.rearrange("p (s m) -> p s m", s=4).unsqueeze(2).to_broadcast([P, 4, 4, SUB])
                nc.scalar.activation(x_rows[:, u], src, ACT.Identity, bias=ln1_b[:, l:l + 1],
                                     scale=ln1_g[:, l:l + 1]).then_inc(xt_sb, 1)

            def silu_gate(T, u, l):
                act.wait_ge(gate_ps, after(T))
                act.wait_ge(ret_sb, after(T - 2))
                nc.scalar.activation(gate_x[:, u, :], ps_gate, ACT.Silu,
                                     bias=proj_bc[:, l, 3:4]).then_inc(gate_sb, 1)

            def snapshots(T, seq, i):
                act.wait_ge(o_ps, after(T - 1))
                for s in range(4):
                    act.wait_ge(state_ps, 33 * seq + 1 + 4 * i + s)
                    nc.scalar.activation(snap[:, s, :], ps_st, ACT.Copy).then_inc(snap_sb, 1)

            def retention_tile(b, i, l, left=8):
                T = l * NT + TPS * b + i
                if left > 1:
                    silu_gate(T + 1, 1 - i % 2, l)
                snapshots(T, l * NB + b, i)
                if left > 2:
                    copy_xt(T + 2, i % 2, l)

            def copy_t4(G, u, bias, scale):
                act.wait_ge(t4_ps, after(G))
                nc.scalar.activation(xT[:, u, :], ps_t4[:, :], ACT.Identity, bias=bias, scale=scale).then_inc(t4_sb, 1)

            def ffn_gelu(G, u, l):
                act.wait_ge(y4_ps, after(G - 2))
                for f in range(FF):
                    act.wait_ge(h_ps, after(4 * G + f))
                    nc.scalar.activation(hid[:, u, f, :], ps_h[f][:, :], ACT.Gelu,
                                         bias=ffn1_b[:, l, f:f + 1]).then_inc(h_sb, 1)

            def ffn_step(G, u, l, left=NG):
                ffn_gelu(G, u, l)
                if left > 1:
                    copy_t4(G + 1, 1 - u, ln2_b[:, l:l + 1], ln2_g[:, l:l + 1])

            for l in range(LAYERS):
                nc.scalar.preload_act_table(ACT.Silu)
                for i in range(2):
                    copy_xt(l * NT + i, i, l)
                silu_gate(l * NT, 0, l)
                with act.Fori(0, NB - 1) as b:
                    for i in range(TPS):
                        retention_tile(b, i, l)
                for i in range(TPS):
                    retention_tile(NB - 1, i, l, left=TPS - i)
                nc.scalar.preload_act_table(ACT.Gelu)
                if l == 0:
                    act.wait_ge(bias_out, 16)
                copy_t4(l * NG, 0, ln2_b[:, l:l + 1], ln2_g[:, l:l + 1])
                with act.Fori(0, NG // 2 - 1) as h:
                    for u in range(2):
                        ffn_step(2 * h + (l * NG + u), u, l)
                for u in range(2):
                    ffn_step(l * NG + NG - 2 + u, u, l, left=2 - u)

            with act.Fori(0, NG // 2) as h:
                for u in range(2):
                    copy_t4(2 * h + (LAYERS * NG + u), u, moe_b[:, 0:1], moe_g[:, 0:1])

            nc.scalar.preload_act_table(ACT.Gelu_apprx_tanh)
            def copy_routed(e):
                act.wait_ge(routed_t, e + 1)
                nc.scalar.activation(xT[:, e % 2, :], ps_t4[:, :], ACT.Identity, bias=moe_b[:, 0:1],
                                     scale=moe_g[:, 0:1]).then_inc(routed_T, 1)
            copy_routed(0)
            for e in range(NE):
                if e >= 2:
                    act.wait_ge(moe_y_ps, e - 1)
                for f in range(FF):
                    act.wait_ge(moe_h_ps, 4 * e + f + 1)
                    nc.scalar.activation(hid[:, e % 2, f, :], ps_h[f][:, :], ACT.Gelu_apprx_tanh,
                                         bias=moe_b1[:, e, f:f + 1]).then_inc(moe_h_sb, 1)
                if e + 1 < NE:
                    copy_routed(e + 1)

            nc.scalar.preload_act_table(ACT.Silu)
            act.wait_ge(moe_added, 1)
            def copy_att(G, u):
                act.wait_ge(t4_ps, after(G))
                nc.scalar.activation(xT[:, u, :], ps_t4[:, :], ACT.Copy).then_inc(t4_sb, 1)
            def silus(h, u, left=NG):
                if left > 1:
                    copy_att(2 * h + (T4_ATT + u + 1), 1 - u)
                act.wait_ge(qk_ps, after(2 * h + u))
                act.wait_ge(qk_ready, after(2 * h + (u - 2)))
                nc.scalar.activation(rows512[:, u, :], ps_h[2 * u][:, :], ACT.Silu, bias=bqk[:, 0:1]).then_inc(z_ready, 1)
                act.wait_ge(v_ps, after(2 * h + u))
                nc.scalar.activation(YT(h, u), ps_h[2 * u + 1][:, :], ACT.Silu).then_inc(v_ready, 1)
            copy_att(T4_ATT, 0)
            with act.Fori(0, NG // 2 - 1) as h:
                for u in range(2):
                    silus(h, u)
            for u in range(2):
                silus(NG // 2 - 1, u, left=2 - u)

            nc.scalar.preload_act_table(ACT.Gelu)
            group = 0
            def copy_av(group):
                act.wait_ge(pv_done, ENDS[group] + 1)
                if group >= 2:
                    act.wait_ge(avT_ps, group - 1)
                nc.scalar.activation(av_sb[:, group % 2, :], ps_av[group % 2][:, :], ACT.Copy).then_inc(av_ok, 1)
            for i in range(NU):
                n = UNITS[i][4]
                act.wait_ge(z_ok, i + 1)
                if i >= 2:
                    act.wait_ge(w_ok, i - 1)
                nc.scalar.activation(gelu_sb[:, i % 2, 0:n], z_sb[i % 3][:, 0:n], ACT.Gelu).then_inc(gelu_ok, 1)
                if group < len(ENDS) and i == ENDS[group] + 1:
                    copy_av(group)
                    group += 1
            copy_av(group)

            nc.scalar.preload_act_table(ACT.Exp)
            act.wait_ge(av_added, group + 1)
            def relu_hidden(u, bias, base):
                for f in range(FF):
                    act.wait_ge(top_h_ps, after(base(f)))
                    nc.scalar.activation(hid[:, u, f, :], ps_h[f][:, :], ACT.Relu, bias=bias[:, f:f + 1]).then_inc(top_h_sb, 1)
            def copy_top(h, u):
                act.wait_ge(t4_ps, after(2 * h + (T4_TOP + u)))
                nc.scalar.activation(YT(h, u), ps_t4[:, :], ACT.Copy).then_inc(t4_sb, 1)
            def router_relu(h, u, left=NG):
                act.wait_ge(logit_ps, after(2 * h + (u - 2)))
                relu_hidden(u, rb1, lambda f: 8 * h + (4 * u + f))
                if left > 1:
                    copy_top(h + u, 1 - u)
            copy_top(0, 0)
            with act.Fori(0, NG // 2 - 1) as h:
                for u in range(2):
                    router_relu(h, u)
            for u in range(2):
                router_relu(NG // 2 - 1, u, left=2 - u)
            act.wait_ge(shift_ok, 1)
            nc.scalar.activation(route[:, 3].rearrange("p t e -> p (t e)"), route[:, 2].rearrange("p t e -> p (t e)"),
                                 ACT.Exp).then_inc(exp_ok, 1)
            for g in range(NG):
                act.wait_ge(gate_t, g + 1)
                if g >= 2:
                    act.wait_ge(gate_b, g - 1)
                nc.scalar.activation(gatesT[:, g % 2, :], ps_t4[0:NE, :], ACT.Copy).then_inc(gate_T, 1)
            for e in range(NE):
                with act.Fori(0, NG // 2) as h:
                    for u in range(2):
                        act.wait_ge(top_y_ps, after(2 * h + (NG * e + u - 2)))
                        relu_hidden(u, top_b1[:, e, :], lambda f: 8 * h + (4 * (NG * (e + 1) + u) + f))

        @block.vector
        def _(dve):
            for s in names["dve"]:
                dve.sem_inc(s, CREDIT)
            nc.vector.memset(ones_row[:], 1.0).then_inc(const_ok, 1)
            nc.vector.memset(zeros[:], 0.0).then_inc(const_ok, 1)
            inputs_in(dve, "bias")

            dve.wait_ge(const_ok, 4)
            nc.vector.tensor_scalar(rel_rows[:], zeros[0:32, :], rel_bias[:, 0:1], None, ALU.add).then_inc(rel_ok, 1)

            def first_norm(begin, h, u):
                xs = [X[:, 4 * (2 * h + u) + j, :] for j in range(4)]
                rs = [R[:, 4 * (2 * h + u) + j, :] for j in range(4)]
                if begin:
                    ln_begin(dve, xs, 2 * h + u, u)
                else:
                    ln_end(dve, xs, rs, 2 * h + u, u)
            inputs_in(dve, "x0")
            first_norm(True, 0, 0)
            first_norm(True, 0, 1)
            inputs_in(dve, "x")
            with dve.Fori(0, NG // 2 - 1) as h:
                for u in range(2):
                    first_norm(False, h, u)
                    first_norm(True, h + 1, u)
            for u in range(2):
                first_norm(False, NG // 2 - 1, u)
            dve.wait_ge(bias_ps, 1)
            for j, (c0, n) in enumerate(((0, 512), (512, 512), (1024, P))):
                nc.vector.tensor_scalar(dist_bias[:, c0:c0 + n], psum[(0, 1, 4)[j]][:, 0:n], float(P ** 0.5 / STD),
                                        float(0.75 - MU / STD), ALU.mult, ALU.add).then_inc(bias_ok, 1)
            dve.wait_ge(ln_out, after(NG - 1))
            inputs_in(dve, "retention")

            def norm_begin(t, T, u, l, k):
                ln_begin(dve, [R[:, t, :]], k, u)

            def norm_end(t, T, u, l, k):
                dve.wait_ge(xt_ps, after(T - 2))
                ln_end(dve, [R[:, t, :]], [xn[:, u, 0:P]], k, u)

            def read_products(T, i, u, l):
                dve.wait_ge(fm_ps, after(T))
                dve.wait_ge(qk_spread, after(T - 1))
                n0 = P * (i % TPS)
                nc.vector.scalar_tensor_tensor(qs[:], ps_fm[:, 0:P], proj_bc[:, l, 0:1],
                                               decay_q[:, n0:n0 + P], ALU.add, ALU.mult)
                nc.vector.scalar_tensor_tensor(ks[:], ps_fm[:, P:2 * P], proj_bc[:, l, 1:2],
                                               decay_k[:, n0:n0 + P], ALU.add, ALU.mult).then_inc(qk_sb, 1)
                dve.wait_ge(kv_ps, after(T))
                dve.wait_ge(o_ps, after(T - 2))
                nc.vector.tensor_tensor(kv[:, u], ps_kv, kv_bias[:, l, :].unsqueeze(1).to_broadcast([P, 4, 256]),
                                        ALU.add).then_inc(kv_biased, 1)

            def make_probs(T):
                dve.wait_ge(scores_ps, after(T))
                dve.wait_ge(o_ps, after(T - 1))
                nc.vector.tensor_tensor(probs[:], ps_sc, causal.unsqueeze(1).to_broadcast([P, 4, P]),
                                        ALU.mult).then_inc(probs_sb, 1)

            def gate_out(T, u):
                dve.wait_ge(o_ps, after(T))
                dve.wait_ge(gate_sb, after(T))
                dve.wait_ge(y_ps, after(T - 2))
                for g in range(4):
                    q = slice(32 * g, 32 * g + 32)
                    last = nc.vector.tensor_tensor(
                        ret[q, u, :].rearrange("p (s n) -> p s n", s=4), ps_o[q, :, g, :],
                        gate_x[q, u, :].rearrange("p (s n) -> p s n", s=4), ALU.mult)
                last.then_inc(ret_sb, 1)

            def add_residual(t, T):
                dve.wait_ge(y_ps, after(T))
                nc.vector.tensor_tensor(R[:, t, :], R[:, t, :], ps_y, ALU.add).then_inc(res_done, 1)

            def retention_tile(b, i, l, first=False, left=8):
                t, T, k = TPS * b + i, TPS * b + (l * NT + i), TPS * b + (LN_RET[l] + i)
                u = i % 2
                if left > 2:
                    norm_begin(TPS * b + i + 2 if isinstance(b, int) or i < 6 else TPS * (b + 1) + i - 6, T + 2, u, l, k + 2)
                if not first:
                    gate_out(T - 1, 1 - u)
                make_probs(T)
                if not first:
                    add_residual(TPS * b + i - 1 if isinstance(b, int) or i > 0 else TPS * (b - 1) + 7, T - 1)
                if left > 1:
                    read_products(T + 1, i + 1, 1 - u, l)
                if left > 2:
                    norm_end(TPS * b + i + 2 if isinstance(b, int) or i < 6 else TPS * (b + 1) + i - 6, T + 2, u, l, k + 2)

            def tiles_of(h, u):
                return [R[:, 8 * h + (4 * u + j), :] for j in range(4)]

            def ffn_norm(h, u, l, shift=0):
                k = 2 * h + (LN_FFN[l] + u)
                G = 2 * h + (l * NG + u)
                ts = tiles_of(h, u)
                ln_begin(dve, ts, k, u)
                dve.wait_ge(t4_ps, after(G - 2))
                ln_end(dve, ts, quarters(xn[:, u, :]), k, u)

            def ffn_add(h, u, l):
                G = 2 * h + (l * NG + u)
                dve.wait_ge(y4_ps, after(G))
                r = R[:, :, :].rearrange("p (g t) d -> p g (t d)", t=4)[:, 2 * h + u, :]
                nc.vector.tensor_tensor(r, r, ps_y4[:, :], ALU.add).then_inc(y4_done, 1)

            for l in range(LAYERS):
                if l:
                    dve.wait_ge(bias_done, after(NG - 1))
                for i in range(2):
                    norm_begin(i, l * NT + i, i, l, LN_RET[l] + i)
                    norm_end(i, l * NT + i, i, l, LN_RET[l] + i)
                read_products(l * NT, 0, 0, l)
                for i in range(TPS):
                    retention_tile(0, i, l, first=i == 0)
                with dve.Fori(1, NB - 1) as b:
                    for i in range(TPS):
                        retention_tile(b, i, l)
                for i in range(TPS):
                    retention_tile(NB - 1, i, l, left=TPS - i)
                gate_out(l * NT + NT - 1, 1)
                add_residual(NT - 1, l * NT + NT - 1)
                dve.wait_ge(res_done, after(l * NT + NT - 1))
                ffn_norm(0, 0, l)
                ffn_norm(0, 1, l)
                with dve.Fori(0, NG // 2 - 1) as h:
                    for u in range(2):
                        ffn_norm(h + 1, u, l)
                        ffn_add(h, u, l)
                for u in range(2):
                    ffn_add(NG // 2 - 1, u, l)

            dve.wait_ge(bias_done, after(2 * NG - 1))
            X_groups = X[:, :, :].rearrange("p (g t) d -> p g (t d)", t=4)

            def x_tiles(h, u):
                return [X[:, 8 * h + (4 * u + j), :] for j in range(4)]

            def final_add(h, u):
                g = 2 * h + u
                dve.wait_ge(fin_b, after(g))
                nc.vector.tensor_tensor(X_groups[:, 2 * h + u, :], X_groups[:, 2 * h + u, :], xn[:, u, :],
                                        ALU.add).then_inc(fin_x, 1)
            def final_begin(h, u):
                ln_begin(dve, tiles_of(h, u), 2 * h + (LN_FIN + u), u)
            def final_end(h, u):
                dve.wait_ge(fin_x, after(2 * h + (u - 2)))
                ln_end(dve, tiles_of(h, u), quarters(xn[:, u, :]), 2 * h + (LN_FIN + u), u)
            final_begin(0, 0)
            final_begin(0, 1)
            final_end(0, 0)
            with dve.Fori(0, NG // 2 - 1) as h:
                for u in range(2):
                    final_begin(h + 1, u)
                    final_end(h + u, 1 - u)
                    final_add(h, u)
            final_end(NG // 2 - 1, 1)
            for u in range(2):
                final_add(NG // 2 - 1, u)
            dve.wait_ge(fin_x, after(NG - 1))
            dve.sem_inc(passed, 1)

            def y_norm_begin(h, u):
                ln_begin(dve, x_tiles(h, u), 2 * h + (LN_FIN + NG + u), u)
            def y_norm_end(h, u):
                ln_end(dve, x_tiles(h, u), tiles_of(h, u), 2 * h + (LN_FIN + NG + u), u)
            for u in range(2):
                y_norm_begin(0, u)
            with dve.Fori(0, NG // 2 - 1) as h:
                for u in range(2):
                    y_norm_end(h, u)
                    y_norm_begin(h + 1, u)
            for u in range(2):
                y_norm_end(NG // 2 - 1, u)
            dve.wait_ge(ln_out, after(LN_FIN + 2 * NG - 1))
            dve.sem_inc(passed, 1)

            def score_norm_begin(h, u):
                ln_begin(dve, tiles_of(h, u), 2 * h + (LN_FIN + 2 * NG + u), u)
            def score_norm_end(h, u):
                dve.wait_ge(t4_ps, after(2 * h + (LAYERS * NG + u - 2)))
                ln_end(dve, tiles_of(h, u), quarters(xn[:, u, :]), 2 * h + (LN_FIN + 2 * NG + u), u)
            def keep_scores(h, u):
                dve.wait_ge(score_ps, after(2 * h + u))
                nc.vector.tensor_copy(
                    score[:].rearrange("p e (g j) -> p e g j", j=4)[:, :, 2 * h + u, :],
                    ps_y4[:, 0:4 * NE].rearrange("p (j e) -> p e j", e=NE)).then_inc(score_sb, 1)
            for u in range(2):
                score_norm_begin(0, u)
            score_norm_end(0, 0)
            with dve.Fori(0, NG // 2 - 1) as h:
                for u in range(2):
                    score_norm_begin(h + 1, u)
                    score_norm_end(h + u, 1 - u)
                    keep_scores(h, u)
            score_norm_end(NG // 2 - 1, 1)
            for u in range(2):
                keep_scores(NG // 2 - 1, u)

            n_steps = [0]

            def step(ins):
                n_steps[0] += 1
                ins.then_inc(step_ok, 1)
                dve.wait_ge(step_ok, n_steps[0])
            dve.wait_ge(score_sb, after(NG - 1))
            bits = score[:].rearrange("p e t -> p (e t)")
            step(nc.vector.tensor_scalar(key[:, 0, :].bitcast(I32), bits.bitcast(I32), 31, -2 ** 31,
                                         ALU.arith_shift_right, ALU.bitwise_or))
            step(nc.vector.tensor_tensor(key[:, 1, :], bits.bitcast(U32), key[:, 0, :], ALU.bitwise_xor))
            step(nc.vector.tensor_scalar(key[:, 2, :], key[:, 1, :], 16, None, ALU.logical_shift_right))
            step(nc.vector.tensor_scalar(key[:, 3, :], key[:, 1, :], 65535, None, ALU.bitwise_and))
            for j in range(2):
                last = nc.vector.tensor_scalar(key_f[:, 2 * j:2 * j + 2, :].rearrange("p a n -> p (a n)"),
                                               key[:, 2 + j, :], 1.0, None, ALU.add)
            last.then_inc(key_ok, 1)
            dve.wait_ge(key_tp, 1)
            nc.vector.tensor_copy(key_t.rearrange("p a n -> p (a n)"), ps_t4[:, :]).then_inc(key_ok, 1)
            nc.vector.memset(all_ones[:], 1.0)
            nc.vector.memset(zeros512, 0.0)
            nc.vector.memset(cols[:, 0:9], 0.0)
            nc.vector.memset(free, 1.0)
            nc.vector.memset(slot_sum, 0.0)
            step(nc.vector.memset(cols[:, 9:10], -1.0))
            nc.vector.tensor_copy(junk, zeros512).then_inc(key_ok, 1)

            def col(n):
                return cols[:, n:n + 1]
            STEPS = 4 * 2 * 5 + 18
            start = n_steps[0]

            def assign(e):
                m = [0]
                c = [0]

                def step(ins):
                    m[0] += 1
                    ins.then_inc(step_ok, 1)
                    dve.wait_ge(step_ok, STEPS * e + (start + m[0]))

                def summed(ins):
                    c[0] += 1
                    ins.then_inc(count_in, 1)
                    dve.wait_ge(count_ps, COUNTS * e + c[0])

                def search_key(row, need):
                    for it in range(4):
                        size = 16.0 ** (3 - it)
                        if it:
                            step(nc.vector.tensor_tensor(col(2), col(it % 2), thr_const[:, it:it + 1], ALU.add))
                        thr = col(2) if it else thr_const[:, 0:1]
                        step(nc.vector.tensor_scalar(junk, row, thr, None, ALU.is_ge, ALU.add, accum_out=col(4)))
                        summed(nc.vector.tensor_scalar(hot_counts[:], digit_hot, col(4), None, ALU.mult))
                        step(nc.vector.tensor_scalar(hot_junk[:], ps_fm[:, 0:16], need, None, ALU.is_ge, ALU.add,
                                                     accum_out=col(3)))
                        if it:
                            step(nc.vector.scalar_tensor_tensor(col((it + 1) % 2), col(3), size, col(it % 2),
                                                                ALU.mult, ALU.add))
                        else:
                            step(nc.vector.tensor_scalar(col(1), col(3), size, None, ALU.mult))
                    step(nc.vector.tensor_scalar(col(6), col(0), -4368.0, None, ALU.add))

                step(nc.vector.tensor_tensor(hi_left, keys_hi[:, e, :], free, ALU.mult))
                search_key(hi_left, float(CAP))
                summed(nc.vector.tensor_scalar(above, hi_left, col(6), None, ALU.is_gt, ALU.add, accum_out=col(CNT)))
                nc.vector.tensor_scalar(col(7), ps_fm[:, 16:17], -1.0, float(CAP), ALU.mult, ALU.add)
                step(nc.vector.scalar_tensor_tensor(lo_left, hi_left, col(6), keys_lo[:, e, :], ALU.is_equal, ALU.mult))
                search_key(lo_left, col(7))
                nc.vector.tensor_scalar(tie, lo_left, col(6), None, ALU.is_equal)
                summed(nc.vector.tensor_scalar(chosen, lo_left, col(6), None, ALU.is_gt, ALU.add, accum_out=col(CNT)))
                step(nc.vector.tensor_tensor(col(8), col(7), ps_fm[:, 16:17], ALU.subtract))
                summed(nc.vector.tensor_tensor_scan(scan_tie, tie, zeros512, 0.0, ALU.add, ALU.add))
                step(nc.vector.tensor_tensor(col(8), col(8), ps_fm[:, 16:17], ALU.subtract))
                step(nc.vector.scalar_tensor_tensor(tie, scan_tie, col(8), tie, ALU.is_le, ALU.mult))
                step(nc.vector.tensor_tensor(above, above, tie, ALU.add))
                step(nc.vector.tensor_tensor(chosen, chosen, above, ALU.add))
                nc.vector.tensor_tensor(free, free, chosen, ALU.subtract)
                summed(nc.vector.tensor_tensor_scan(scan, chosen, zeros512, 0.0, ALU.add, ALU.add))
                step(nc.vector.tensor_tensor(col(10), ps_fm[:, 17:18], col(9), ALU.add))
                nc.vector.tensor_scalar(col(9), col(9), float(CAP), None, ALU.add)
                step(nc.vector.scalar_tensor_tensor(scan, scan, col(10), chosen, ALU.add, ALU.mult))
                step(nc.vector.tensor_tensor(slot_sum, slot_sum, scan, ALU.add))
                while m[0] < STEPS:
                    m[0] += 1
                    dve.sem_inc(step_ok, 1)
                assert m[0] == STEPS and c[0] == COUNTS, (m, c)
            inputs_in(dve, "moe")
            for e in range(NE):
                dve.wait_ge(key_in[e], 16 * 2)
            with dve.Fori(0, NE) as e:
                assign(e)
            dve.sem_inc(slots_ok, 1)
            dve.wait_ge(slots_tp, 1)
            nc.vector.tensor_copy(slots[:].rearrange("p (q j) -> p q j", j=4),
                                  ps_t4[:, 0:32].rearrange("p (j q) -> p q j", q=8)).then_inc(slots_ok, 1)

            def routed_norm(e):
                dve.wait_ge(routed_in[e % 4], 16 * (e // 4 + 1))
                ln_begin(dve, quarters(routed[e % 4]), LN_MOE + e, e % 2)
                if e >= 2:
                    dve.wait_ge(routed_t, e - 1)
                ln_end(dve, quarters(routed[e % 4]), quarters(xn[:, e % 2, :]), LN_MOE + e, e % 2)
            routed_norm(0)
            routed_norm(1)
            for e in range(NE):
                if e + 2 < NE:
                    routed_norm(e + 2)
                dve.wait_ge(moe_y_ps, e + 1)
                nc.vector.tensor_tensor(routed[e % 4], routed[e % 4], ps_y4[:, :], ALU.add).then_inc(moe_y_sb, 1)
            dve.wait_ge(gathered, 16 * NT)
            flat = "p t d -> p (t d)"
            nc.vector.tensor_tensor(X[:].rearrange(flat), X[:].rearrange(flat), R[:].rearrange(flat),
                                    ALU.add).then_inc(moe_added, 1)

            dve.wait_ge(moe_added, 1)
            def att_norm(h, u):
                ln_begin(dve, x_tiles(h, u), 2 * h + (LN_ATT + u), u)
                dve.wait_ge(t4_ps, after(2 * h + (T4_ATT + u - 2)))
                ln_end(dve, x_tiles(h, u), quarters(xn[:, u, :]), 2 * h + (LN_ATT + u), u)
            def make_qk(h, u):
                dve.wait_ge(z_ready, after(2 * h + u))
                for j, dst in enumerate((qT_all, kT_all)):
                    last = nc.vector.tensor_scalar(dst.rearrange("p (g n) -> p g n", n=512)[:, 2 * h + u, :],
                                                   rows512[:, u, :], gamma[:, j:j + 1], beta[:, j:j + 1],
                                                   ALU.mult, ALU.add)
                last.then_inc(qk_ready, 1)
            for u in range(2):
                att_norm(0, u)
            with dve.Fori(0, NG // 2 - 1) as h:
                for u in range(2):
                    att_norm(h + 1, u)
                    make_qk(h, u)
            for u in range(2):
                make_qk(NG // 2 - 1, u)

            dve.wait_ge(bias_in, 16)
            group = 0
            def add_av(group):
                b, half = UNITS[ENDS[group]][0:2]
                dve.wait_ge(avT_ps, group + 1)
                t0 = TPS * b + 4 * half
                xg = X[:, t0:t0 + 4, :].rearrange("p t d -> p (t d)")
                nc.vector.tensor_tensor(xg, xg, ps_t4[:, :], ALU.add).then_inc(av_added, 1)
            def make_z(i):
                b, half, m, n0, n = UNITS[i]
                x0, z = n0 - P * m, z_sb[i % 3][:, 0:n]
                dve.wait_ge(sim_ps, i + 1)
                if i >= 3:
                    dve.wait_ge(gelu_ok, i - 2)
                    dve.wait_ge(recip_ok, i - 2)
                nc.vector.scalar_tensor_tensor(z, ps_sim[i % 3][:, 0:n], float(1 / (SEQ * STD)), toeplitz[:, x0:x0 + n],
                                               ALU.mult, ALU.add).then_inc(z1_sb, 1)
            def shift_z(i):
                z = z_sb[i % 3][:, 0:UNITS[i][4]]
                dve.wait_ge(z1_sb, i + 1)
                nc.vector.tensor_scalar(z, z, 0.75, 2.0 ** -26, ALU.subtract, ALU.add).then_inc(z_ok, 1)
            def invert(i):
                n = UNITS[i][4]
                dve.wait_ge(z_ok, i + 1)
                if i >= 2:
                    dve.wait_ge(w_ok, i - 1)
                nc.vector.reciprocal(recip_sb[:, i % 2, 0:n], z_sb[i % 3][:, 0:n]).then_inc(recip_ok, 1)
            for i in range(2):
                make_z(i)
                shift_z(i)
            for i in range(NU):
                if i + 2 < NU:
                    make_z(i + 2)
                invert(i)
                if i + 2 < NU:
                    shift_z(i + 2)
                if group < len(ENDS) and i == ENDS[group] + 3:
                    add_av(group)
                    group += 1
            add_av(group)
            dve.wait_ge(av_added, group + 1)

            def top_norm(h, u):
                ln_begin(dve, x_tiles(h, u), 2 * h + (LN_TOP + u), u)
                dve.wait_ge(t4_ps, after(2 * h + (T4_TOP + u - 2)))
                ln_end(dve, x_tiles(h, u), quarters(xn[:, u, :]), 2 * h + (LN_TOP + u), u)
            def keep_logits(h, u):
                dve.wait_ge(logit_ps, after(2 * h + u))
                nc.vector.tensor_tensor(logits.rearrange("p (g t) e -> p g t e", t=4)[:, 2 * h + u],
                                        ps_y4[:, 0:4 * NE].rearrange("p (t e) -> p t e", e=NE),
                                        rb2[:].unsqueeze(1).to_broadcast([P, 4, NE]), ALU.add).then_inc(logit_sb, 1)
            for u in range(2):
                top_norm(0, u)
            with dve.Fori(0, NG // 2 - 1) as h:
                for u in range(2):
                    top_norm(h + 1, u)
                    keep_logits(h, u)
            for u in range(2):
                keep_logits(NG // 2 - 1, u)
            dve.wait_ge(logit_sb, after(NG - 1))

            n_steps[0] = start + NE * STEPS

            def over(ap):
                return ap.unsqueeze(2).to_broadcast([P, NT, NE])

            def first_of(values, top, out):
                step(nc.vector.tensor_tensor(out, values, over(top), ALU.is_equal))
                step(nc.vector.tensor_tensor(out, out, order.unsqueeze(1).to_broadcast([P, NT, NE]), ALU.mult))
                step(nc.vector.tensor_reduce(peak[:, 3, :], out, AX.X, ALU.max))
                step(nc.vector.tensor_tensor(out, out, over(peak[:, 3, :]), ALU.is_equal))
            step(nc.vector.tensor_reduce(peak[:, 0, :], logits, AX.X, ALU.max))
            nc.vector.tensor_tensor(route[:, 2], logits, over(peak[:, 0, :]), ALU.subtract).then_inc(shift_ok, 1)
            first_of(logits, peak[:, 0, :], route[:, 0])
            step(nc.vector.scalar_tensor_tensor(
                route[:, 1].rearrange("p t e -> p (t e)"), route[:, 0].rearrange("p t e -> p (t e)"), -3e38,
                logits.rearrange("p t e -> p (t e)"), ALU.mult, ALU.add))
            step(nc.vector.tensor_reduce(peak[:, 1, :], route[:, 1], AX.X, ALU.max))
            first_of(route[:, 1], peak[:, 1, :], gates[:])
            step(nc.vector.tensor_tensor(gates[:], gates[:], route[:, 0], ALU.add))
            dve.wait_ge(exp_ok, 1)
            step(nc.vector.tensor_tensor(gates[:], gates[:], route[:, 3], ALU.mult))
            step(nc.vector.tensor_reduce(peak[:, 2, :], gates[:], AX.X, ALU.add))
            step(nc.vector.reciprocal(peak[:, 1, :], peak[:, 2, :]))
            nc.vector.tensor_tensor(gates[:], gates[:], over(peak[:, 1, :]), ALU.mult).then_inc(gates_ok, 1)
            for g in range(NG):
                dve.wait_ge(gate_b, g + 1)
                xg = X[:, 4 * g:4 * g + 4, :].rearrange("p t d -> p (t d)")
                nc.vector.tensor_tensor(xg, xg, ps_y4[:, :], ALU.add).then_inc(gate_added, 1)
            dve.wait_ge(gate_added, NG)
            for e in range(NE):
                with dve.Fori(0, NG // 2) as h:
                    for u in range(2):
                        U = 2 * h + (NG * e + u)
                        dve.wait_ge(top_y_ps, after(U))
                        if e:
                            dve.wait_ge(top_added, after(2 * h + (NG * (e - 1) + u)))
                        for j in range(4):
                            t = 8 * h + (4 * u + j)
                            last = nc.vector.scalar_tensor_tensor(X[:, t, :], ps_top[u][:, P * j:P * (j + 1)],
                                                                  gates[:, t, e:e + 1], X[:, t, :], ALU.mult, ALU.add)
                        last.then_inc(top_added, 1)

        @block.gpsimd
        def _(pool):
            for s in names["pool"]:
                pool.sem_inc(s, CREDIT)
            nc.gpsimd.memset(mhalf[:], -0.5).then_inc(const_ok, 1)
            nc.gpsimd.memset(eps4[:], EPS).then_inc(const_ok, 1)
            pool.wait_ge(const_ok, 4)
            with pool.Fori(0, NG // 2) as h:
                for u in range(2):
                    ln_root(pool, 4, 2 * h + u, u)

            def spread(T, u):
                pool.wait_ge(qk_sb, after(T))
                pool.wait_ge(o_ps, after(T - 2))
                for src, mask, dst in ((qs, quad_mask, q_quads), (ks, slot_mask, k_slots)):
                    last = nc.gpsimd.tensor_tensor(
                        dst[:, u], src[:, :].rearrange("p (s n) -> p s n", s=4).unsqueeze(2).to_broadcast([P, 4, 4, SUB]),
                        mask.unsqueeze(1).unsqueeze(3).to_broadcast([P, 4, 4, SUB]), ALU.mult)
                last.then_inc(qk_spread, 1)

            def decay_kv(T, i, u):
                pool.wait_ge(kv_biased, after(T))
                c0 = 4 * (i % TPS)
                nc.gpsimd.tensor_tensor(kv[:, u, :, 0:P], kv[:, u, :, 0:P], decay_rows[:, c0:c0 + 4, :], ALU.mult)
                nc.gpsimd.tensor_tensor(kv[:, u, :, P:2 * P], kv[:, u, :, P:2 * P],
                                        slot_rows.unsqueeze(1).to_broadcast([P, 4, P]), ALU.mult).then_inc(kv_ready, 1)

            def retention_tile(b, i, l, left=8):
                T, k = TPS * b + (l * NT + i), TPS * b + (LN_RET[l] + i)
                u = i % 2
                if left > 2:
                    ln_root(pool, 1, k + 2, u)
                if left > 1:
                    spread(T + 1, 1 - u)
                    decay_kv(T + 1, i + 1, 1 - u)

            def ffn_bias(h, u, l):
                G = 2 * h + (l * NG + u)
                pool.wait_ge(y4_done, after(G))
                r = R[:, :, :].rearrange("p (g t) d -> p g t d", t=4)[:, 2 * h + u, :, :]
                nc.gpsimd.tensor_tensor(r, r, ffn2_b[:, l, :].unsqueeze(1).to_broadcast([P, 4, P]),
                                        ALU.add).then_inc(bias_done, 1)

            inputs_in(pool, "retention", "decays")
            for l in range(LAYERS):
                for i in range(2):
                    ln_root(pool, 1, LN_RET[l] + i, i)
                spread(l * NT, 0)
                decay_kv(l * NT, 0, 0)
                with pool.Fori(0, NB - 1) as b:
                    for i in range(TPS):
                        retention_tile(b, i, l)
                for i in range(TPS):
                    retention_tile(NB - 1, i, l, left=TPS - i)
                ln_root(pool, 4, LN_FFN[l], 0)
                ln_root(pool, 4, LN_FFN[l] + 1, 1)
                with pool.Fori(0, NG // 2 - 1) as h:
                    for u in range(2):
                        ln_root(pool, 4, 2 * h + (LN_FFN[l] + u + 2), u)
                        ffn_bias(h, u, l)
                for u in range(2):
                    ffn_bias(NG // 2 - 1, u, l)
            def final_scale(h, u):
                g = 2 * h + u
                pool.wait_ge(ln_out, after(2 * h + (LN_FIN + u)))
                y = xn[:, u, :].rearrange("p (t d) -> p t d", t=4)
                nc.gpsimd.tensor_tensor(y, y, lnf_g[:, :].unsqueeze(1).to_broadcast([P, 4, P]), ALU.mult).then_inc(fin_g, 1)
                pool.wait_ge(fin_g, after(g))
                nc.gpsimd.tensor_tensor(y, y, lnf_b[:, :].unsqueeze(1).to_broadcast([P, 4, P]), ALU.add).then_inc(fin_b, 1)
            for u in range(2):
                ln_root(pool, 4, LN_FIN + u, u)
            with pool.Fori(0, NG // 2 - 1) as h:
                for u in range(2):
                    final_scale(h, u)
                    ln_root(pool, 4, 2 * h + (LN_FIN + u + 2), u)
            for u in range(2):
                final_scale(NG // 2 - 1, u)
            with pool.Fori(0, NG) as h:
                for u in range(2):
                    ln_root(pool, 4, 2 * h + (LN_FIN + NG + u), u)

            pool.wait_ge(slots_ok, 2)
            for t in range(NT):
                nc.gpsimd.indirect_dma_start(
                    out=routed_d, out_offset=bass.IndirectOffsetOnAxis(ap=slots[:, t:t + 1], axis=0),
                    in_=R[:, t, :], in_offset=None).then_inc(scattered, 16)
            for e in range(2):
                ln_root(pool, 4, LN_MOE + e, e)
            for e in range(NE):
                if e + 2 < NE:
                    ln_root(pool, 4, LN_MOE + e + 2, e % 2)
                pool.wait_ge(moe_y_sb, e + 1)
                r = routed[e % 4].rearrange("p (t d) -> p t d", t=4)
                nc.gpsimd.tensor_tensor(r, r, moe_b2[:, e, :].unsqueeze(1).to_broadcast([P, 4, P]),
                                        ALU.add).then_inc(moe_out, 1)
            for u in range(4):
                pool.wait_ge(moe_stored[u], 16 * NE // 4)
            for t in range(NT):
                nc.gpsimd.indirect_dma_start(
                    out=R[:, t, :], out_offset=None, in_=moe_d,
                    in_offset=bass.IndirectOffsetOnAxis(ap=slots[:, t:t + 1], axis=0)).then_inc(gathered, 16)

            with pool.Fori(0, NG // 2) as h:
                for u in range(2):
                    ln_root(pool, 4, 2 * h + (LN_ATT + u), u)
            for i in range(NU):
                n = UNITS[i][4]
                pool.wait_ge(gelu_ok, i + 1)
                pool.wait_ge(recip_ok, i + 1)
                if i >= 2:
                    pool.wait_ge(pv_done, i - 1)
                nc.gpsimd.tensor_tensor(w_sb[:, i % 2, 0:n], gelu_sb[:, i % 2, 0:n], recip_sb[:, i % 2, 0:n],
                                        ALU.mult).then_inc(w_ok, 1)
                if i in DIAG:
                    pool.wait_ge(w_ok, i + 1)
                    nc.gpsimd.affine_select(out=w_sb[:, i % 2, 0:P], in_=w_sb[:, i % 2, 0:P], compare_op=ALU.is_ge,
                                            fill=0.0, base=0, pattern=[[1, P]], channel_multiplier=-1).then_inc(masked, 1)
            with pool.Fori(0, NG // 2) as h:
                for u in range(2):
                    ln_root(pool, 4, 2 * h + (LN_TOP + u), u)


def kernel(**inputs):
    import numpy as _np
    import concourse.bacc as _bacc
    from concourse import mybir as _mybir
    from concourse.bass_utils import run_bass_kernel_spmd as _run

    nc = _bacc.Bacc("TRN2", target_bir_lowering=False, num_devices=1)
    arrays, aps = {}, {}
    for name, a in list(inputs.items()) + list(pack(inputs).items()) + list(constants().items()):
        a = _np.ascontiguousarray(a)
        arrays[f"in_{name}_dram"] = a
        aps[name] = nc.dram_tensor(f"in_{name}_dram", a.shape, _mybir.dt.from_np(a.dtype), kind="ExternalInput").ap()
    out = nc.dram_tensor("out_0_dram", (NB, SEQ, P), F32, kind="ExternalOutput").ap()
    mega_kernel(nc, aps, out)
    r = _run(nc, [arrays], core_ids=[0])
    return r.results[0]["out_0_dram"]
```

```python
from contextlib import ExitStack

import numpy as np

import concourse.bass as bass
from concourse import mybir

F32 = mybir.dt.float32
I32 = mybir.dt.int32
U32 = mybir.dt.uint32
ALU = mybir.AluOpType
ACT = mybir.ActivationFunctionType
AX = mybir.AxisListType

P = 128
NB = 4
SEQ = 1024
TPS = SEQ // P
NT = NB * TPS
NG = NT // 4
TOK = NT * P
LAYERS = 2
SUB = 32
EPS = 1e-5
NE = 8
CAP = TOK // NE
FF = 4
MU = 0.5 ** 0.5
STD = (0.25 * np.pi) ** 0.5
CREDIT = 8
BLOCKS = 2 * NT + NE
COUNTS = 9


COLUMNS = [("L0_attn_proj_b", np.s_[:], LAYERS * 4), ("L0_attn_ffn1_b", np.s_[:], LAYERS * FF),
           ("L0_attn_ln1_g", np.s_[:], LAYERS), ("L0_attn_ln1_b", np.s_[:], LAYERS),
           ("L0_attn_ln2_g", np.s_[:], LAYERS), ("L0_attn_ln2_b", np.s_[:], LAYERS),
           ("L0_ffn_b1", np.s_[:], NE * FF), ("L0_ffn_ln_g", np.s_[:], 1), ("L0_ffn_ln_b", np.s_[:], 1),
           ("L0_ffn_centroids", np.s_[:], NE), ("L1_attn_bqk", np.s_[:], 1),
           ("L1_attn_gamma", np.s_[:], 2), ("L1_attn_beta", np.s_[:], 2),
           ("L1_ffn_rb1", np.s_[:], FF), ("L1_ffn_b1", np.s_[:], NE * FF)]
REPEATED = [("L0_attn_proj_b", np.s_[:, P:3 * P], LAYERS * 2 * P), ("L0_attn_ffn2_b", np.s_[:], LAYERS * P),
            ("L0_attn_reto_b", np.s_[:], LAYERS * P), ("L0_attn_lnf_g", np.s_[:], P), ("L0_attn_lnf_b", np.s_[:], P),
            ("L0_ffn_b2", np.s_[:], NE * P), ("L1_ffn_rb2", np.s_[:], NE)]


def pack(inputs):
    columns = [np.asarray(inputs[name])[part].reshape(n, P).T for name, part, n in COLUMNS]
    rows = [np.asarray(inputs[name])[part].reshape(1, n) for name, part, n in REPEATED]
    return {"vectors": np.concatenate(columns, 1), "repeated": np.concatenate(rows, 1)}


def constants():
    head_gamma = 1.0 - 2.0 ** (-5.0 - np.arange(16, dtype=np.float64))
    g = np.repeat(head_gamma, 8)
    n = np.arange(SEQ, dtype=np.float64)
    p = np.arange(P)
    decay_q = g[:, None] ** n[None]
    decay_k = g[:, None] ** -n[None]
    slot = (p // 8) % 4
    m = p % SUB
    chunk = np.arange(SEQ // SUB)
    decay_rows = g[None, None, :] ** -(chunk[None, :, None] * SUB + m[:, None, None])
    decay_rows = decay_rows * (p[:, None, None] // SUB == slot[None, None, :])
    slot_rows = (p[:, None] // SUB == slot[None]).astype(np.float64)
    causal = (np.tile(np.arange(SUB), 4)[None] >= m[:, None]).astype(np.float64)
    slot_mask = (slot[:, None] == np.arange(4)[None]).astype(np.float64)
    quad_mask = (p[:, None] // 32 == np.arange(4)[None]).astype(np.float64)
    ident = np.eye(P)
    order = np.tile(8.0 - np.arange(8), (P, 1))
    small = np.concatenate([ident, causal, slot_rows, slot_mask, quad_mask, order], 1)
    d = np.maximum(np.arange(-P + 1, SEQ), 0)
    large = 16 + (np.log(np.maximum(d, 1) / 16) / np.log(8) * 16 + 1e-9).astype(int)
    bucket = np.where(d < 16, d, np.minimum(large, 31))
    onehot = (np.arange(32)[:, None] == bucket[None])
    onehot = np.concatenate([onehot, np.zeros((32, 1))], 1)
    dig, part = p // 8, p % 8
    steps = np.array([4096, 256, 16, 1])
    digit_hot = (dig[:, None] == np.arange(16)[None]).astype(np.float64)
    before = np.cumsum(steps) - steps
    thr = 1 + dig[:, None] * steps[None] - before[None]
    earlier = ((dig[:, None] == dig[None]) & (part[:, None] < part[None])).astype(np.float64)
    part_hot = (part[:, None] == np.arange(8)[None]).astype(np.float64)
    own = np.stack([dig + 1.0, CAP * dig - 1.0], 1)
    search = np.concatenate([digit_hot, thr, earlier, part_hot, own], 1)
    choices = 1 + P * np.arange(2 * NT)[None] + p[:, None]
    dispatch = np.concatenate([p[:, None] < p[None], np.ones((P, P)), np.tile(p, (P, 1)), choices,
                               1 + 2 * TOK + P * np.arange(BLOCKS)[None] + p[:, None]], 1)
    f = np.float32
    return {
        "decay_q": decay_q.astype(f), "decay_k": decay_k.astype(f),
        "decay_rows": decay_rows.reshape(P, -1).astype(f), "small": small.astype(f),
        "onehot": onehot.astype(f), "search": search.astype(f), "dispatch": dispatch.astype(f),
    }


def after(n):
    return n + 1 + CREDIT


def mega_kernel(nc, w, out):
    with ExitStack() as ctx:
        def sb(name, shape, dt=F32):
            return ctx.enter_context(nc.sbuf_tensor(name, shape, dt))

        def sem(name):
            return ctx.enter_context(nc.semaphore(name))

        X = sb("X", [P, NT, P])
        R = sb("R", [P, NT, P])
        small = sb("small", [P, 400])
        ident, causal, slot_rows = small[:, 0:128], small[:, 128:256], small[:, 256:384]
        slot_mask, quad_mask = small[:, 384:388], small[:, 388:392]
        order = small[:, 392:400]
        ones_row = sb("ones_row", [1, P])
        zeros = sb("zeros", [P, P])
        vectors = sb("vectors", [P, sum(n for _, _, n in COLUMNS)])
        repeated = sb("repeated", [P, sum(n for _, _, n in REPEATED)])

        def packed(buf, table):
            views, c = [], 0
            for _, _, n in table:
                views.append(buf[:, c:c + n])
                c += n
            return views
        (proj_bc, ffn1_b, ln1_g, ln1_b, ln2_g, ln2_b, moe_b1, moe_g, moe_b, centroids, bqk, gamma, beta,
         rb1, top_b1) = packed(vectors, COLUMNS)
        proj_bc = proj_bc.rearrange("p (l j) -> p l j", l=LAYERS)
        ffn1_b = ffn1_b.rearrange("p (l j) -> p l j", l=LAYERS)
        moe_b1 = moe_b1.rearrange("p (e f) -> p e f", e=NE)
        top_b1 = top_b1.rearrange("p (e f) -> p e f", e=NE)
        kv_bias, ffn2_b, reto_b, lnf_g, lnf_b, moe_b2, rb2 = packed(repeated, REPEATED)
        kv_bias = kv_bias.rearrange("p (l n) -> p l n", l=LAYERS)
        ffn2_b = ffn2_b.rearrange("p (l n) -> p l n", l=LAYERS)
        reto_b = reto_b.rearrange("p (l n) -> p l n", l=LAYERS)
        moe_b2 = moe_b2.rearrange("p (e n) -> p e n", e=NE)
        decay_rows = sb("decay_rows", [P, SEQ // SUB, P])
        decay_q = sb("decay_q", [P, SEQ])
        decay_k = sb("decay_k", [P, SEQ])
        proj_w = sb("proj_w", [P, LAYERS, 512])
        reto_w = sb("reto_w", [P, LAYERS, P])
        ffn1_w = sb("ffn1_w", [P, LAYERS, 512])
        ffn2_w = sb("ffn2_w", [P, LAYERS, FF, P])
        moe_w1 = sb("moe_w1", [P, NE, 512])
        moe_w2 = sb("moe_w2", [P, NE, FF, P])
        arena = sb("arena", [P, TOK])
        keys_hi = decay_rows[:].rearrange("p c f -> p (c f)").rearrange("p (e f) -> p e f", e=NE)
        keys_lo = arena[:].rearrange("p (e f) -> p e f", e=NE)
        search = sb("search", [P, 158])
        digit_hot, thr_const, earlier = search[:, 0:16], search[:, 16:20], search[:, 20:148]
        part_hot, own_code, own_base = search[:, 148:156], search[:, 156:157], search[:, 157:158]
        score = sb("score", [P, NE, NT])
        key = decay_q[:].bitcast(U32).rearrange("p (a n) -> p a n", a=4)
        key_f, key_t = [decay_k[:, 512 * j:512 * (j + 1)].rearrange("p (a n) -> p a n", a=4) for j in range(2)]
        cols = sb("cols", [P, 16])
        holds = sb("holds", [P, 16])
        failing = sb("failing", [P, 64])
        routed_token = sb("routed_token", [P, NT], U32)
        slot_i, slot_row_i, slot_col_i, token_f, row_f, col_f = [decay_k[:, NT * j:NT * (j + 1)] for j in range(6)]
        slot_i, slot_row_i, slot_col_i = [x.bitcast(U32) for x in (slot_i, slot_row_i, slot_col_i)]
        keys_d = nc.dram_tensor("keys_d", (2, NE, NT, P), F32).ap()
        tokens_d = nc.dram_tensor("tokens_d", (TOK, P), F32).ap()
        moe_d = nc.dram_tensor("moe_d", (TOK, P), F32).ap()
        wqk, wv = sb("wqk", [P, P]), sb("wv", [P, P])
        bv_row = sb("bv_row", [1, P])
        rel_bias = sb("rel_bias", [32, 1])
        rel_rows = sb("rel_rows", [32, P])
        toeplitz = sb("toeplitz", [P, SEQ])
        qT_all = moe_w1[:].rearrange("p e n -> p (e n)")
        kT_all = moe_w2[:].rearrange("p e f n -> p (e f n)")
        v_all = R
        bias_d = nc.dram_tensor("bias_d", (P, SEQ + P), F32).ap()
        rw1 = sb("rw1", [P, 512])
        rw2 = sb("rw2", [P, FF, NE])
        top_b2 = sb("top_b2", [NE, P])
        top_w1 = decay_rows[:].rearrange("p (e f) n -> p e (f n)", e=NE)
        top_w2 = arena[:].rearrange("p (e f n) -> p e f n", e=NE, f=FF)
        logits = score[:].rearrange("p a b -> p (a b)").rearrange("p (t e) -> p t e", e=NE)
        gates = sb("gates", [P, NT, NE])
        route = sb("route", [P, 4, NT, NE])
        peak = sb("peak", [P, 4, NT])
        gatesT = sb("gatesT", [NE, 2, 512])
        dispatch = sb("dispatch", [P, 3 * P + 2 * NT + BLOCKS])
        before_in_tile, all_ones, iota = [dispatch[:, P * j:P * (j + 1)] for j in range(3)]
        choice_id, empty_id = dispatch[:, 3 * P:3 * P + 2 * NT], dispatch[:, 3 * P + 2 * NT:]
        y_d = nc.dram_tensor("y_d", (TOK, P), F32).ap()
        top_d = nc.dram_tensor("top_d", (2 * TOK + BLOCKS * P, P), F32).ap()
        stats = sb("stats", [P, 2, 4, 6])
        first_st = sb("first_st", [P, 2, 4, 6])
        first_mv = sb("first_mv", [P, 2, 4, 2])
        first_ve = sb("first_ve", [P, 2, 4])
        first_rs = sb("first_rs", [P, 2, 4])
        mv = sb("mv", [P, 2, 4, 2])
        veps = sb("veps", [P, 2, 4])
        rstd = sb("rstd", [P, 2, 4])
        z_shift = sb("z_shift", [P, 2])
        mhalf, eps4 = sb("mhalf", [P, 4]), sb("eps4", [P, 4])
        xn = sb("xn", [P, 2, 512])
        xT = sb("xT", [P, 2, 512])
        x_rows = sb("x_rows", [P, 2, 4, 4, SUB])
        qs, ks = sb("qs", [P, P]), sb("ks", [P, P])
        q_quads = sb("q_quads", [P, 2, 4, 4, SUB])
        k_slots = sb("k_slots", [P, 2, 4, 4, SUB])
        gate_x = sb("gate_x", [P, 2, P])
        kv = sb("kv", [P, 2, 4, 256])
        probs = sb("probs", [P, 4, P])
        snap = sb("snap", [P, 4, P])
        ret = sb("ret", [P, 2, P])
        hid = sb("hid", [P, 2, FF, 512])

        routed = [R[:, 4 * e:4 * e + 4, :].rearrange("p t d -> p (t d)") for e in range(NE)]
        slot_row_hot = x_rows[:].rearrange("p u s c n -> p (u s) (c n)")
        slot_col_hot = xT[:, 0, 0:8 * NT].rearrange("p (k n) -> p k n", k=8)
        onehot = hid[0:32].rearrange("p u f n -> p (u f n)")[:, 0:SEQ + P]
        dist_bias = hid[:].rearrange("p u f n -> p (u f n)")[:, 2048:2048 + SEQ + P]
        rows512 = hid[:].rearrange("p u f n -> p (u f) n")
        hi_left, lo_left, free, code, chosen, scan, tie, scan_tie = [rows512[:, j, :] for j in range(8)]
        above, junk, zeros512 = xT[:, 0, :], xT[:, 1, :], xn[:, 0, :]
        COUNT = 4

        _, gelu_sb, recip_sb, w_sb = [rows512[:, 2 * j:2 * j + 2, :] for j in range(4)]
        z_sb = [rows512[:, 0, :], rows512[:, 1, :], xn[:, 0, :]]
        av_sb = xT

        w1_now, w2_now = [kT_all[:, 2048 * j:2048 * (j + 1)].rearrange("p (k n) -> p k n", k=4) for j in range(2)]
        block_x = x_rows[:, 0].rearrange("p s c n -> p s (c n)")
        block_y = x_rows[:, 1].rearrange("p s c n -> p s (c n)")
        block_xT = q_quads[:, 0, 0:2].rearrange("p s g n -> p s (g n)")
        b1_now = k_slots[:, 0, 0, 0, 0:16].rearrange("p (k f) -> p k f", k=4)
        bias_sums = qT_all
        second = decay_rows

        halves = [rows512[:, j, 256 * i:256 * (i + 1)] for j in (2, 3, 4) for i in range(2)]
        mask, second_hot, totals, running, slot_of, product = halves
        def by_tile(ap):
            return ap.rearrange("p (t e) -> p t e", e=NE)
        def by_expert(ap):
            return ap.rearrange("p (e t) -> p e t", e=NE)
        line = rows512[:, 5, :]
        starts, tokens_of, blocks_i, blocks_of, block_ends, shift_of = [line[:, 8 * i:8 * i + 8] for i in range(6)]
        slot_f, slot_row, slot_block, top_slots, row_i, block_i, top_gates = [line[:, 64 * i:64 * i + 64] for i in range(1, 8)]
        top_slots, row_i, block_i, blocks_i = [x.bitcast(U32) for x in (top_slots, row_i, block_i, blocks_i)]
        row_hot = xT[:].rearrange("p u (k n) -> p (u k) n", n=P)
        block_hot = rows512[:, 6:8, :].rearrange("p u n -> p (u n)")[:, 0:8 * BLOCKS].rearrange("p (k n) -> p k n", k=8)
        ended = rows512[:, 6:8, :].rearrange("p u n -> p (u n)")[:, 0:NE * BLOCKS].rearrange("p (b e) -> p b e", e=NE)
        expert_f = rows512[:, 7, 288:288 + BLOCKS]
        expert_of = rows512[:, 7, 360:360 + BLOCKS].bitcast(I32)
        choice_f, is_empty = [halves[j][:, 0:BLOCKS] for j in range(2)]
        choice_of, token_of = [halves[j][:, 128:128 + BLOCKS].bitcast(U32) for j in range(2)]

        psum = [ctx.enter_context(nc.psum_tensor(f"ps{i}", [P, 512], F32)) for i in range(2)]
        psum2 = ctx.enter_context(nc.psum_tensor("psb", [P, 1024], F32))
        psum += [None, None] + [ctx.enter_context(nc.psum_tensor(f"ps{i}", [P, 512], F32)) for i in range(4, 8)]
        ps_xt = psum[0][:, 0:128]
        ps_y = psum[5][:, 0:128]
        ps_gate = psum[7][:, 0:128]
        ps_fm = psum[1]
        ps_kv = psum2[:, :].rearrange("p (s c) -> p s c", s=4)
        ps_sc = psum[4][:, :].rearrange("p (s c) -> p s c", s=4)
        ps_o = psum[5][:, :].rearrange("p (s g n) -> p s g n", s=4, g=4)
        ps_st = psum[6][:, 0:128]
        ps_t4 = psum[0]
        ps_h = [psum[1], psum[4], psum[5], psum[6]]
        ps_y4 = psum[7]
        ps_sim = [psum[1], psum[4], psum[5]]
        ps_av = [psum[6], psum[7]]
        ps_rank, ps_total, ps_token = psum[1][:, 0:256], psum[1][:, 256:512], psum[4][:, 0:BLOCKS]
        ps_bx, ps_bh, ps_by = psum[0][:, 0:P], [psum[1], psum[4]], [psum[5][:, 0:P], psum[6][:, 0:P]]
        ps_gT, ps_gb = psum2[0:NE, 0:512], psum2[:, 512:1024]

        def YT(h, u):
            return R[:].rearrange("p (g t) d -> p g (t d)", t=4)[:, 2 * h + u, :]

        names = {}

        def counter(name, engine):
            s = sem(name)
            names.setdefault(engine, []).append(s)
            return s

        loaded = {phase: sem(f"loaded_{phase}") for phase in ("x0", "x", "bias", "retention", "decays", "ffn", "moe", "rest")}
        passed = sem("passed")
        stored = sem("stored")
        const_ok = sem("const_ok")
        ln_stats = counter("ln_stats", "dve")
        ln_moments = counter("ln_moments", "dve")
        ln_veps = counter("ln_veps", "pool")
        ln_rstd = counter("ln_rstd", "pool")
        ln_out = counter("ln_out", "dve")
        first_moments = counter("first_moments", "dve")
        first_rstd = counter("first_rstd", "pool")
        first_out = counter("first_out", "dve")
        xt_ps = counter("xt_ps", "pe")
        xt_sb = counter("xt_sb", "act")
        fm_ps = counter("fm_ps", "pe")
        gate_ps = counter("gate_ps", "pe")
        kv_ps = counter("kv_ps", "pe")
        qk_sb = counter("qk_sb", "dve")
        gate_sb = counter("gate_sb", "act")
        kv_biased = counter("kv_biased", "dve")
        kv_ready = counter("kv_ready", "pool")
        qk_spread = counter("qk_spread", "pool")
        scores_ps = counter("scores_ps", "pe")
        probs_sb = counter("probs_sb", "dve")
        state_ps = sem("state_ps")
        snap_sb = sem("snap_sb")
        o_ps = counter("o_ps", "pe")
        ret_sb = counter("ret_sb", "dve")
        y_ps = counter("y_ps", "pe")
        reto_b_in = counter("reto_b_in", "pool")
        res_done = counter("res_done", "dve")
        t4_ps = counter("t4_ps", "pe")
        t4_sb = counter("t4_sb", "act")
        h_ps = counter("h_ps", "pe")
        h_sb = counter("h_sb", "act")
        y4_ps = counter("y4_ps", "pe")
        y4_done = counter("y4_done", "dve")
        bias_done = counter("bias_done", "pool")
        fin_g = counter("fin_g", "pool")
        fin_b = counter("fin_b", "pool")
        fin_x = counter("fin_x", "dve")

        score_ps = counter("score_ps", "pe")
        score_sb = counter("score_sb", "dve")
        key_ok = sem("key_ok")
        key_tp = sem("key_tp")
        key_out = sem("key_out")
        key_in = [sem(f"key_in{e}") for e in range(NE)]
        step_ok = sem("step_ok")
        count_in = sem("count_in")
        count_ps = sem("count_ps")
        slots_tp = sem("slots_tp")
        slots_ok = sem("slots_ok")
        tokens_out = sem("tokens_out")
        slot_hot_ok = counter("slot_hot_ok", "dve")
        slot_hot_used = counter("slot_hot_used", "pe")
        routed_in = [sem(f"routed_in{e}") for e in range(NE)]
        routed_t = sem("routed_t")
        routed_T = sem("routed_T")
        moe_h_ps = sem("moe_h_ps")
        moe_h_sb = sem("moe_h_sb")
        moe_y_ps = sem("moe_y_ps")
        moe_y_sb = sem("moe_y_sb")
        moe_out = sem("moe_out")
        moe_stored = sem("moe_stored")
        moe_back = [sem(f"moe_back{b}") for b in range(NB)]
        moe_added = sem("moe_added")

        qk_ps = counter("qk_ps", "pe")
        v_ps = counter("v_ps", "pe")
        z_ready = counter("z_ready", "act")
        v_ready = counter("v_ready", "act")
        qk_ready = counter("qk_ready", "dve")
        late = sem("late")
        bias_ok = sem("bias_ok")
        bias_ps = sem("bias_ps")
        bias_out = sem("bias_out")
        bias_in = sem("bias_in")
        sim_ps = sem("sim_ps")
        z1_sb = sem("z1_sb")
        z_mid = sem("z_mid")
        z_ok = sem("z_ok")
        gelu_ok = sem("gelu_ok")
        recip_ok = sem("recip_ok")
        w_ok = sem("w_ok")
        masked = sem("masked")
        pv_done = sem("pv_done")
        av_ok = sem("av_ok")
        avT_ps = sem("avT_ps")
        av_added = sem("av_added")
        rel_ok = sem("rel_ok")
        logit_ps = counter("logit_ps", "pe")
        logit_sb = counter("logit_sb", "dve")
        shift_ok = sem("shift_ok")
        exp_ok = sem("exp_ok")
        gates_ok = sem("gates_ok")
        gate_t = counter("gate_t", "pe")
        gate_T = counter("gate_T", "act")
        gate_b = counter("gate_b", "pe")
        gate_kept = counter("gate_kept", "act")
        top_h_ps = counter("top_h_ps", "pe")
        top_h_sb = counter("top_h_sb", "act")
        y_out = [sem(f"y_out{u}") for u in range(2)]
        mask_ok = sem("mask_ok")
        rank_ps = sem("rank_ps")
        hot_ok = counter("hot_ok", "dve")
        hot_used = counter("hot_used", "pe")
        tokens_ok = sem("tokens_ok")
        block_in = [sem(f"block_in{k}") for k in range(4)]
        block_t = counter("block_t", "pe")
        block_T = counter("block_T", "act")
        weights_now = counter("weights_now", "dve")
        block_h_ps = counter("block_h_ps", "pe")
        block_h_sb = counter("block_h_sb", "act")
        block_y_ps = counter("block_y_ps", "pe")
        block_y_sb = counter("block_y_sb", "dve")
        block_out = [sem(f"block_out{k}") for k in range(4)]
        back = [sem(f"back{g}") for g in range(NG)]
        top_added = sem("top_added")

        UNITS = [(b, half, m, max(512 * half, P * m), 512 * (half + 1) - max(512 * half, P * m))
                 for b in range(NB) for half in range(2) for m in range(4 * half + 4)]
        NU = len(UNITS)
        DIAG = [i for i, x in enumerate(UNITS) if x[3] == P * x[2]]
        ENDS = [i for i, x in enumerate(UNITS) if x[2] == 4 * x[1] + 3]

        def masks_before(i):
            return sum(d <= i for d in DIAG)

        n_loads = {}

        def inputs_in(engine, *phases):
            for phase in phases:
                engine.wait_ge(loaded[phase], n_loads[phase])

        def ln_begin(dve, tiles, k, u):
            for j, t in enumerate(tiles):
                last = nc.vector.bn_stats(stats[:, u, j, :], t)
            last.then_inc(ln_stats, 1)
            dve.wait_ge(ln_stats, after(k))
            dve.sem_inc(passed, 1)
            for j in range(len(tiles)):
                last = nc.vector.bn_aggr(mv[:, u, j, :], stats[:, u, j, :])
            last.then_inc(ln_moments, 1)

        def ln_root(pool, n, k, u):
            pool.wait_ge(ln_moments, after(k))
            nc.gpsimd.tensor_tensor(veps[:, u, 0:n], mv[:, u, 0:n, 1], eps4[:, 0:n], ALU.add).then_inc(ln_veps, 1)
            pool.wait_ge(ln_veps, after(k))
            nc.gpsimd.tensor_tensor(rstd[:, u, 0:n], veps[:, u, 0:n], mhalf[:, 0:n], ALU.pow).then_inc(ln_rstd, 1)

        def ln_end(dve, tiles, outs, k, u):
            dve.wait_ge(ln_rstd, after(k))
            for j, (t, o) in enumerate(zip(tiles, outs)):
                last = nc.vector.tensor_scalar(o, t, mv[:, u, j, 0:1], rstd[:, u, j:j + 1],
                                               ALU.subtract, ALU.mult)
            last.then_inc(ln_out, 1)

        def quarters(ap):
            return [ap[:, P * j:P * (j + 1)] for j in range(4)]

        LN0 = 0
        LN_RET = [LN0 + 2, LN0 + 2 + NT + NG]
        LN_FFN = [x + NT for x in LN_RET]
        LN_SCORE = LN_FFN[1] + NG
        LN_MOE = LN_SCORE + NG
        FINAL = 2 * (NB - 1)
        LN_ATT = LN_MOE + NE
        LN_TOP = LN_ATT + NG
        T4_ATT = (LAYERS + 1) * NG
        T4_TOP = T4_ATT + NG

        block = ctx.enter_context(nc.Block())

        @block.sync
        def _(sp):
            def load(phase, dst, src):
                sp.dma_start(dst, src, allow_slow_non_contiguous=True).then_inc(loaded[phase], 16)
                n_loads[phase] = n_loads.get(phase, 0) + 16
            load("x0", X[:, 0:TPS, :], w["L0_attn_x"][0].rearrange("(t p) d -> p t d", p=P))
            load("bias", rel_bias[:], w["L1_attn_rel_bias"].rearrange("(p o) -> p o", o=1))
            load("bias", onehot, w["onehot"])
            load("retention", small[:], w["small"])
            load("retention", vectors[:], w["vectors"])
            load("retention", proj_w[:], w["L0_attn_proj_w"].rearrange("l k n -> k l n"))
            load("retention", decay_q[:], w["decay_q"])
            load("retention", decay_k[:], w["decay_k"])
            load("retention", reto_w[:], w["L0_attn_reto_w"].rearrange("l k n -> k l n"))
            load("retention", repeated[:], w["repeated"].to_broadcast([P, repeated.shape[1]]))
            load("decays", decay_rows[:].rearrange("p c f -> p (c f)"), w["decay_rows"])
            for b in range(1, NB):
                load("x", X[:, b * TPS:(b + 1) * TPS, :], w["L0_attn_x"][b].rearrange("(t p) d -> p t d", p=P))
            load("ffn", ffn1_w[:], w["L0_attn_ffn1_w"].rearrange("l k n -> k l n"))
            load("ffn", ffn2_w[:], w["L0_attn_ffn2_w"].rearrange("l (f k) n -> k l f n", k=P))
            load("moe", moe_w1[:], w["L0_ffn_w1"].rearrange("e k n -> k e n"))
            load("moe", moe_w2[:], w["L0_ffn_w2"].rearrange("e (f k) n -> k e f n", k=P))
            load("moe", search[:], w["search"])
            load("rest", wqk[:], w["L1_attn_wqk"])
            load("rest", wv[:], w["L1_attn_wv"])
            load("rest", bv_row[:], w["L1_attn_bv"].rearrange("(o n) -> o n", o=1))
            load("rest", rw1[:], w["L1_ffn_rw1"])
            load("rest", rw2[:], w["L1_ffn_rw2"].rearrange("(f k) n -> k f n", k=P))
            load("rest", top_b2[:], w["L1_ffn_b2"])
            load("moe", dispatch[:], w["dispatch"])

            sp.wait_ge(bias_ok, 3)
            sp.dma_start(bias_d, dist_bias).then_inc(bias_out, 16)
            sp.wait_ge(bias_out, 16)
            sp.dma_start(toeplitz[:], bass.AP(bias_d.tensor, P - 1, [[SEQ + P - 1, P], [1, SEQ]])).then_inc(bias_in, 16)

            sp.wait_ge(first_out, after(FINAL + 2 * NG - 1))
            sp.dma_start(tokens_d.rearrange("(t p) d -> p t d", p=P), R[:]).then_inc(tokens_out, 16)

            sp.wait_ge(key_ok, 3)
            sp.dma_start(keys_d.rearrange("h (a e) t n -> (e t) (h a) n", a=2), key_t).then_inc(key_out, 16)
            sp.wait_ge(key_out, 16)
            for e in range(NE - 1):
                for h, keys in enumerate((keys_hi, keys_lo)):
                    src = keys_d[h, e].rearrange("(q t) n -> q (t n)", q=8).unsqueeze(0).to_broadcast([16, 8, 512])
                    sp.dma_start(keys[:, e, :], src).then_inc(key_in[e], 16)

            sp.wait_ge(slots_ok, 2)
            sp.dma_start(top_w1, w["L1_ffn_W1"].rearrange("e k n -> k e n")).then_inc(late, 16)
            sp.dma_start(top_w2, w["L1_ffn_W2"].rearrange("e (f k) n -> k e f n", k=P)).then_inc(late, 16)

            sp.wait_ge(moe_stored, 64 * NE)
            for b in range(NB):
                sp.dma_start(R[:, TPS * b:TPS * (b + 1), :],
                             moe_d[SEQ * b:SEQ * (b + 1)].rearrange("(t p) d -> p t d", p=P)).then_inc(moe_back[b], 16)
            for g in range(NG):
                sp.wait_ge(ln_out, after(LN_TOP + g))
                sp.dma_start(y_d.rearrange("(g t p) d -> p g t d", g=NG, p=P)[:, g],
                             xn[:, g % 2, :].rearrange("p (t d) -> p t d", t=4)).then_inc(y_out[g % 2], 16)
            for k in range(4):
                sp.wait_ge(block_out[k], 16 * BLOCKS // 4)
            for g in range(NG):
                for c, results in enumerate((R, second)):
                    sp.dma_start(results[:, 4 * g:4 * g + 4, :],
                                 top_d[0:2 * TOK].rearrange("(c g t p) d -> p c g t d", c=2, g=NG, p=P)[:, c, g]).then_inc(back[g], 16)
            for g in range(NG):
                sp.wait_ge(top_added, g + 1)
                sp.dma_start(out.rearrange("b (t p) d -> p (b t) d", p=P)[:, 4 * g:4 * g + 4, :],
                             X[:, 4 * g:4 * g + 4, :]).then_inc(stored, 16)
            sp.wait_ge(stored, 16 * NG)

        @block.tensor
        def _(pe):
            for s in names["pe"]:
                pe.sem_inc(s, CREDIT)
            pe.wait_ge(const_ok, 6)
            inputs_in(pe, "bias")
            pe.wait_ge(rel_ok, 1)
            for j, (c0, n) in enumerate(((0, 512), (512, 512), (1024, P))):
                m = nc.tensor.matmul(psum[(0, 1, 4)[j]][0:P, 0:n], rel_rows[:], onehot[:, c0:c0 + n], start=True, stop=True)
            m.then_inc(bias_ps, 1)
            pe.wait_ge(bias_ok, 3)
            inputs_in(pe, "retention")

            def transpose_tile(T, u, lnk):
                pe.wait_ge(ln_out, after(lnk))
                pe.wait_ge(xt_sb, after(T - 1))
                nc.tensor.transpose(ps_xt, xn[:, u, 0:P], ident).then_inc(xt_ps, 1)

            def project(T, u, l):
                pe.wait_ge(xt_sb, after(T))
                pe.wait_ge(qk_sb, after(T - 1))
                x = x_rows[:, u, :, 0, :]
                for c in range(2):
                    last = nc.tensor.matmul(ps_fm[:, c * P:(c + 1) * P], proj_w[:, l, c * P:(c + 1) * P], x,
                                            start=True, stop=True)
                last.then_inc(fm_ps, 1)
                pe.wait_ge(gate_sb, after(T - 1))
                nc.tensor.matmul(ps_gate, proj_w[:, l, 3 * P:4 * P], x, start=True, stop=True).then_inc(gate_ps, 1)

            def project_kv(T, u, l):
                pe.wait_ge(kv_biased, after(T - 1))
                for s in range(4):
                    rows = x_rows[:, u, s].rearrange("p a b -> p (a b)")
                    last = nc.tensor.matmul(ps_kv[:, s, :], rows, proj_w[:, l, P:3 * P], start=True, stop=True)
                last.then_inc(kv_ps, 1)

            def scores(T, u, slots):
                if slots[0] == 0:
                    pe.wait_ge(qk_spread, after(T))
                    pe.wait_ge(probs_sb, after(T - 1))
                for s in slots:
                    last = nc.tensor.matmul(ps_sc[:, s, :], k_slots[:, u, s].rearrange("p a b -> p (a b)"),
                                            q_quads[:, u, s].rearrange("p a b -> p (a b)"), start=True, stop=True)
                if slots[-1] == 3:
                    last.then_inc(scores_ps, 1)

            def retain(T, u, seq, i, k, left):
                if i == 0:
                    nc.tensor.matmul(ps_st, zeros[:], zeros[:], start=True, stop=False,
                                     skip_group_check=True).then_inc(state_ps, 1)
                pe.wait_ge(kv_ready, after(T))
                pe.wait_ge(ret_sb, after(T - 1))
                pe.wait_ge(res_done, after(T - 1))
                for s in range(4):
                    if s == 3 and left > 2:
                        transpose_tile(T + 2, u, k + 2)
                    pe.wait_ge(snap_sb, 32 * seq + 4 * i + s + 1)
                    nc.tensor.matmul(ps_st, kv[:, u, s, 0:P], kv[:, u, s, P:2 * P], start=False, stop=False,
                                     skip_group_check=True).then_inc(state_ps, 1)
                    o = ps_o[:, s].rearrange("p g n -> p (g n)")
                    nc.tensor.matmul(o, snap[:, s, :], q_quads[:, u, s].rearrange("p a b -> p (a b)"),
                                     start=True, stop=False)
                    if s == 0:
                        pe.wait_ge(probs_sb, after(T))
                    last = nc.tensor.matmul(o, kv[:, u, s, P:2 * P], probs[:, s, :], start=False, stop=True)
                    if s == 3:
                        last.then_inc(o_ps, 1)
                    if left > 1 and s:
                        scores(T + 1, 1 - u, ((), (0,), (1,), (2, 3))[s])

            def project_out(T, u, l):
                pe.wait_ge(ret_sb, after(T))
                nc.tensor.matmul(ps_y, ret[:, u, :], reto_w[:, l, :], start=True, stop=True).then_inc(y_ps, 1)

            def retention_tile(b, i, l, first=False, left=8):
                T, k = l * NT + TPS * b + i, LN_RET[l] + TPS * b + i
                u = i % 2
                if left > 1:
                    project(T + 1, 1 - u, l)
                if not first:
                    project_out(T - 1, 1 - u, l)
                if left > 1:
                    project_kv(T + 1, 1 - u, l)
                retain(T, u, l * NB + b, i, k, left)

            def transposes(k, G, u):
                pe.wait_ge(ln_out, after(k))
                pe.wait_ge(t4_sb, after(G - 1))
                for j in range(4):
                    t = nc.tensor.transpose(ps_t4[:, P * j:P * (j + 1)], xn[:, u, P * j:P * (j + 1)], ident)
                t.then_inc(t4_ps, 1)

            def ffn_hidden(G, u, l):
                pe.wait_ge(t4_sb, after(G))
                for f in range(FF):
                    pe.wait_ge(h_sb, after(4 * (G - 1) + f))
                    nc.tensor.matmul(ps_h[f][:, :], ffn1_w[:, l, P * f:P * (f + 1)], xT[:, u, :],
                                     start=True, stop=True).then_inc(h_ps, 1)

            def ffn_out(G, u, l):
                pe.wait_ge(h_sb, after(4 * G + 3))
                pe.wait_ge(y4_done, after(G - 1))
                for j in range(4):
                    for f in range(FF):
                        m = nc.tensor.matmul(ps_y4[:, P * j:P * (j + 1)], hid[:, u, f, P * j:P * (j + 1)],
                                             ffn2_w[:, l, f, :], start=(f == 0), stop=(f == FF - 1))
                m.then_inc(y4_ps, 1)

            def ffn_step(g, u, l, left=NG):
                G, k = l * NG + g, LN_FFN[l] + g
                if left > 1:
                    ffn_hidden(G + 1, 1 - u, l)
                if left > 2:
                    transposes(k + 2, G + 2, u)
                ffn_out(G, u, l)

            for l in range(LAYERS):
                for i in range(2):
                    transpose_tile(l * NT + i, i, LN_RET[l] + i)
                project(l * NT, 0, l)
                project_kv(l * NT, 0, l)
                scores(l * NT, 0, (0, 1, 2, 3))
                for i in range(TPS):
                    retention_tile(0, i, l, first=i == 0)
                with pe.Fori(1, NB - 1) as b:
                    for i in range(TPS):
                        retention_tile(b, i, l)
                for i in range(TPS):
                    retention_tile(NB - 1, i, l, left=TPS - i)
                project_out(l * NT + NT - 1, 1, l)
                if l == 0:
                    inputs_in(pe, "ffn")
                transposes(LN_FFN[l], l * NG, 0)
                ffn_hidden(l * NG, 0, l)
                transposes(LN_FFN[l] + 1, l * NG + 1, 1)
                with pe.Fori(0, NG // 2 - 1) as h:
                    for u in range(2):
                        ffn_step(2 * h + u, u, l)
                for u in range(2):
                    ffn_step(NG - 2 + u, u, l, left=2 - u)

            def score_group(h, u):
                G = 2 * h + (LAYERS * NG + u)
                transposes(2 * h + (LN_SCORE + u), G, u)
                pe.wait_ge(t4_sb, after(G))
                pe.wait_ge(score_sb, after(2 * h + (u - 1)))
                for j in range(4):
                    m = nc.tensor.matmul(ps_y4[:, NE * j:NE * (j + 1)], xT[:, u, P * j:P * (j + 1)], centroids[:],
                                         start=True, stop=True)
                m.then_inc(score_ps, 1)
            with pe.Fori(0, NG // 2) as h:
                for u in range(2):
                    score_group(h, u)

            pe.wait_ge(key_ok, 1)
            for j in range(4):
                t = nc.tensor.transpose(ps_t4[:, P * j:P * (j + 1)], key_f[:, j, :], ident)
            t.then_inc(key_tp, 1)

            inputs_in(pe, "moe")
            with pe.Fori(0, NE - 1) as e:
                for n in range(COUNTS):
                    pe.wait_ge(count_in, COUNTS * e + (n + 1))
                    if n < COUNTS - 1:
                        m = nc.tensor.matmul(ps_fm[:, 0:16], cols[:, COUNT:COUNT + 1].to_broadcast([P, P]), digit_hot,
                                             start=True, stop=True)
                    else:
                        m = nc.tensor.matmul(ps_fm[:, 16:17], earlier, scan_tie[:, 511:512], start=True, stop=True)
                    m.then_inc(count_ps, 1)
            pe.wait_ge(count_in, COUNTS * (NE - 1) + 1)
            nc.tensor.matmul(ps_fm[:, 16:17], earlier, scan[:, 511:512], start=True, stop=True).then_inc(count_ps, 1)
            pe.wait_ge(slots_ok, 1)
            for j in range(4):
                t = nc.tensor.matmul(ps_t4[:, 8 * j:8 * j + 8], chosen[:, P * j:P * (j + 1)], part_hot, start=True, stop=True)
            t.then_inc(slots_tp, 1)
            for t in range(NT):
                pe.wait_ge(slot_hot_ok, after(t))
                nc.tensor.matmul(ps_fm[:, 0:NT], slot_row_hot[:, t % 8, :], slot_col_hot[:, t % 8, :], start=t == 0,
                                 stop=t == NT - 1).then_inc(slot_hot_used, 1)

            inputs_in(pe, "rest")
            def moe_transposes(e):
                pe.wait_ge(ln_out, after(LN_MOE + e))
                if e:
                    pe.wait_ge(routed_T, e)
                for j in range(4):
                    t = nc.tensor.transpose(ps_t4[:, P * j:P * (j + 1)], xn[:, e % 2, P * j:P * (j + 1)], ident)
                t.then_inc(routed_t, 1)

            def moe_hidden(e):
                pe.wait_ge(routed_T, e + 1)
                for f in range(FF):
                    if e:
                        pe.wait_ge(moe_h_sb, 4 * (e - 1) + f + 1)
                    nc.tensor.matmul(ps_h[f][:, :], moe_w1[:, e, P * f:P * (f + 1)], xT[:, e % 2, :],
                                     start=True, stop=True).then_inc(moe_h_ps, 1)

            pe.wait_ge(slots_ok, 2)
            moe_transposes(0)
            moe_hidden(0)
            moe_transposes(1)
            for e in range(NE):
                if e + 1 < NE:
                    moe_hidden(e + 1)
                if e + 2 < NE:
                    moe_transposes(e + 2)
                pe.wait_ge(moe_h_sb, 4 * e + 4)
                if e:
                    pe.wait_ge(moe_y_sb, e)
                for j in range(4):
                    for f in range(FF):
                        m = nc.tensor.matmul(ps_y4[:, P * j:P * (j + 1)], hid[:, e % 2, f, P * j:P * (j + 1)],
                                             moe_w2[:, e, f, :], start=(f == 0), stop=(f == FF - 1))
                m.then_inc(moe_y_ps, 1)

            pe.wait_ge(moe_added, NB)
            def projections(g, u, left=NG):
                if left > 1:
                    transposes(LN_ATT + g + 1, T4_ATT + g + 1, 1 - u)
                pe.wait_ge(t4_sb, after(T4_ATT + g))
                pe.wait_ge(z_ready, after(g - 2))
                nc.tensor.matmul(ps_h[2 * u][:, :], wqk[:], xT[:, u, :], start=True, stop=True).then_inc(qk_ps, 1)
                pe.wait_ge(v_ready, after(g - 2))
                for j in range(4):
                    o = ps_h[2 * u + 1][:, P * j:P * (j + 1)]
                    nc.tensor.matmul(o, xT[:, u, P * j:P * (j + 1)], wv[:], start=True, stop=False)
                    m = nc.tensor.matmul(o, ones_row[0:1, :], bv_row[0:1, :], start=False, stop=True)
                m.then_inc(v_ps, 1)
            transposes(LN_ATT, T4_ATT, 0)
            with pe.Fori(0, NG // 2 - 1) as h:
                for u in range(2):
                    projections(2 * h + u, u)
            for u in range(2):
                projections(NG - 2 + u, u, left=2 - u)

            def similarity(i):
                b, half, m, n0, n = UNITS[i]
                if i >= 3:
                    pe.wait_ge(z1_sb, i - 2)
                if i == 0:
                    pe.wait_ge(qk_ready, after(NG - 1))
                    pe.wait_ge(v_ready, after(NG - 1))
                nc.tensor.matmul(ps_sim[i % 3][:, 0:n], kT_all[:, SEQ * b + P * m:SEQ * b + P * (m + 1)],
                                 qT_all[:, SEQ * b + n0:SEQ * b + n0 + n], start=True, stop=True).then_inc(sim_ps, 1)

            def weigh(i, group):
                b, half, m, n0, n = UNITS[i]
                if m == 0 and group >= 2:
                    pe.wait_ge(av_ok, group - 1)
                pe.wait_ge(w_ok, i + 1)
                if i in DIAG:
                    pe.wait_ge(masked, masks_before(i))
                x = nc.tensor.matmul(ps_av[group % 2][:, n0 - 512 * half:512], v_all[:, TPS * b + m, :], w_sb[:, i % 2, 0:n],
                                     start=(m == 0), stop=(i in ENDS))
                x.then_inc(pv_done, 1)

            def turn(group):
                pe.wait_ge(av_ok, group + 1)
                if group:
                    pe.wait_ge(av_added, group)
                for j in range(4):
                    t = nc.tensor.transpose(ps_t4[:, P * j:P * (j + 1)], av_sb[:, group % 2, P * j:P * (j + 1)], ident)
                t.then_inc(avT_ps, 1)

            for i in range(3):
                similarity(i)
            group = 0
            for i in range(NU):
                if i + 3 < NU:
                    similarity(i + 3)
                weigh(i, group)
                if group and i == ENDS[group - 1] + 1:
                    turn(group - 1)
                if i in ENDS:
                    group += 1
            turn(group - 1)

            pe.wait_ge(av_added, group)
            def router_hidden(h, u):
                pe.wait_ge(t4_sb, after(2 * h + (T4_TOP + u)))
                for f in range(FF):
                    pe.wait_ge(top_h_sb, after(8 * h + (4 * u + f - 4)))
                    nc.tensor.matmul(ps_h[f][:, :], rw1[:, P * f:P * (f + 1)], YT(h, u),
                                     start=True, stop=True).then_inc(top_h_ps, 1)

            def router_step(h, u, left=NG):
                if left > 1:
                    router_hidden(h + u, 1 - u)
                if left > 2:
                    transposes(2 * h + (LN_TOP + u + 2), 2 * h + (T4_TOP + u + 2), u)
                pe.wait_ge(top_h_sb, after(8 * h + (4 * u + 3)))
                pe.wait_ge(logit_sb, after(2 * h + (u - 1)))
                for j in range(4):
                    for f in range(FF):
                        m = nc.tensor.matmul(ps_y4[:, NE * j:NE * (j + 1)], hid[:, u, f, P * j:P * (j + 1)],
                                             rw2[:, f, :], start=(f == 0), stop=(f == FF - 1))
                m.then_inc(logit_ps, 1)

            transposes(LN_TOP, T4_TOP, 0)
            router_hidden(0, 0)
            transposes(LN_TOP + 1, T4_TOP + 1, 1)
            with pe.Fori(0, NG // 2 - 1) as h:
                for u in range(2):
                    router_step(h, u)
            for u in range(2):
                router_step(NG // 2 - 1, u, left=2 - u)

            pe.wait_ge(mask_ok, 1)
            nc.tensor.matmul(ps_rank, before_in_tile, mask, start=True, stop=True)
            nc.tensor.matmul(ps_total, all_ones, mask, start=True, stop=True).then_inc(rank_ps, 1)

            pe.wait_ge(gates_ok, 1)
            for g in range(NG):
                u = g % 2
                pe.wait_ge(gate_T, after(g - 1))
                for j in range(4):
                    t = nc.tensor.transpose(ps_gT[:, P * j:P * (j + 1)], gates[:, 4 * g + j, :], ident)
                t.then_inc(gate_t, 1)
                for i in range(NE * g, NE * (g + 1)):
                    pe.wait_ge(hot_ok, after(i))
                    nc.tensor.matmul(ps_token, row_hot[:, i % 8, :], block_hot[:, i % 8, :], start=i == 0,
                                     stop=i == 2 * NT - 1).then_inc(hot_used, 1)
                pe.wait_ge(gate_T, after(g))
                pe.wait_ge(gate_kept, after(g - 1))
                for j in range(4):
                    m = nc.tensor.matmul(ps_gb[:, P * j:P * (j + 1)], gatesT[:, u, P * j:P * (j + 1)], top_b2[:],
                                         start=True, stop=True)
                m.then_inc(gate_b, 1)

            def block_transpose(h, k):
                b = 4 * h + k
                pe.wait_ge(block_in[k], 16 * h + 16)
                pe.wait_ge(block_T, after(b - 1))
                nc.tensor.transpose(ps_bx, block_x[:, k, :], ident).then_inc(block_t, 1)

            def block_hidden(h, k):
                b, u = 4 * h + k, k % 2
                pe.wait_ge(block_T, after(b))
                pe.wait_ge(weights_now, after(b))
                pe.wait_ge(block_h_sb, after(b - 2))
                for f in range(FF):
                    m = nc.tensor.matmul(ps_bh[u][:, P * f:P * (f + 1)], w1_now[:, k, P * f:P * (f + 1)], block_xT[:, u, :],
                                         start=True, stop=True)
                m.then_inc(block_h_ps, 1)

            def block_result(h, k):
                b, u = 4 * h + k, k % 2
                pe.wait_ge(block_h_sb, after(b))
                pe.wait_ge(block_y_sb, after(b - 2))
                for f in range(FF):
                    m = nc.tensor.matmul(ps_by[u], rows512[:, u, P * f:P * (f + 1)], w2_now[:, k, P * f:P * (f + 1)],
                                         start=f == 0, stop=f == FF - 1)
                m.then_inc(block_y_ps, 1)

            def four_blocks(h, last=False):
                for k in range(4):
                    if not (last and k == 3):
                        block_hidden(h + (k + 1) // 4, (k + 1) % 4)
                    if not (last and k >= 2):
                        block_transpose(h + (k + 2) // 4, (k + 2) % 4)
                    block_result(h, k)

            block_transpose(0, 0)
            block_hidden(0, 0)
            block_transpose(0, 1)
            with pe.Fori(0, BLOCKS // 4 - 1) as h:
                four_blocks(h)
            four_blocks(BLOCKS // 4 - 1, last=True)

        @block.scalar
        def _(act):
            for s in names["act"]:
                act.sem_inc(s, CREDIT)
            inputs_in(act, "retention")
            act.wait_ge(const_ok, 6)

            def copy_xt(T, u, l):
                act.wait_ge(xt_ps, after(T))
                act.wait_ge(kv_ps, after(T - 2))
                src = ps_xt.rearrange("p (s m) -> p s m", s=4).unsqueeze(2).to_broadcast([P, 4, 4, SUB])
                nc.scalar.activation(x_rows[:, u], src, ACT.Identity, bias=ln1_b[:, l:l + 1],
                                     scale=ln1_g[:, l:l + 1]).then_inc(xt_sb, 1)

            def silu_gate(T, u, l):
                act.wait_ge(gate_ps, after(T))
                act.wait_ge(ret_sb, after(T - 2))
                nc.scalar.activation(gate_x[:, u, :], ps_gate, ACT.Silu,
                                     bias=proj_bc[:, l, 3:4]).then_inc(gate_sb, 1)

            def snapshots(T, seq, i):
                act.wait_ge(o_ps, after(T - 1))
                for s in range(4):
                    act.wait_ge(state_ps, 33 * seq + 1 + 4 * i + s)
                    nc.scalar.activation(snap[:, s, :], ps_st, ACT.Copy).then_inc(snap_sb, 1)

            def retention_tile(b, i, l, left=8):
                T = l * NT + TPS * b + i
                if left > 1:
                    silu_gate(T + 1, 1 - i % 2, l)
                snapshots(T, l * NB + b, i)
                if left > 2:
                    copy_xt(T + 2, i % 2, l)

            def copy_t4(G, u, bias, scale):
                act.wait_ge(t4_ps, after(G))
                nc.scalar.activation(xT[:, u, :], ps_t4[:, :], ACT.Identity, bias=bias, scale=scale).then_inc(t4_sb, 1)

            def ffn_gelu(G, u, l):
                act.wait_ge(y4_ps, after(G - 2))
                for f in range(FF):
                    act.wait_ge(h_ps, after(4 * G + f))
                    nc.scalar.activation(hid[:, u, f, :], ps_h[f][:, :], ACT.Gelu,
                                         bias=ffn1_b[:, l, f:f + 1]).then_inc(h_sb, 1)

            def ffn_step(G, u, l, left=NG):
                ffn_gelu(G, u, l)
                if left > 1:
                    copy_t4(G + 1, 1 - u, ln2_b[:, l:l + 1], ln2_g[:, l:l + 1])

            for l in range(LAYERS):
                nc.scalar.preload_act_table(ACT.Silu)
                for i in range(2):
                    copy_xt(l * NT + i, i, l)
                silu_gate(l * NT, 0, l)
                with act.Fori(0, NB - 1) as b:
                    for i in range(TPS):
                        retention_tile(b, i, l)
                for i in range(TPS):
                    retention_tile(NB - 1, i, l, left=TPS - i)
                nc.scalar.preload_act_table(ACT.Gelu)
                if l == 0:
                    act.wait_ge(bias_out, 16)
                copy_t4(l * NG, 0, ln2_b[:, l:l + 1], ln2_g[:, l:l + 1])
                with act.Fori(0, NG // 2 - 1) as h:
                    for u in range(2):
                        ffn_step(2 * h + (l * NG + u), u, l)
                for u in range(2):
                    ffn_step(l * NG + NG - 2 + u, u, l, left=2 - u)

            with act.Fori(0, NG // 2) as h:
                for u in range(2):
                    copy_t4(2 * h + (LAYERS * NG + u), u, moe_b[:, 0:1], moe_g[:, 0:1])

            nc.scalar.preload_act_table(ACT.Gelu_apprx_tanh)
            def copy_routed(e):
                act.wait_ge(routed_t, e + 1)
                nc.scalar.activation(xT[:, e % 2, :], ps_t4[:, :], ACT.Identity, bias=moe_b[:, 0:1],
                                     scale=moe_g[:, 0:1]).then_inc(routed_T, 1)
            copy_routed(0)
            for e in range(NE):
                if e >= 2:
                    act.wait_ge(moe_y_ps, e - 1)
                for f in range(FF):
                    act.wait_ge(moe_h_ps, 4 * e + f + 1)
                    nc.scalar.activation(hid[:, e % 2, f, :], ps_h[f][:, :], ACT.Gelu_apprx_tanh,
                                         bias=moe_b1[:, e, f:f + 1]).then_inc(moe_h_sb, 1)
                if e + 1 < NE:
                    copy_routed(e + 1)

            nc.scalar.preload_act_table(ACT.Silu)
            act.wait_ge(moe_added, NB)
            def copy_att(G, u):
                act.wait_ge(t4_ps, after(G))
                nc.scalar.activation(xT[:, u, :], ps_t4[:, :], ACT.Copy).then_inc(t4_sb, 1)
            def silus(h, u, left=NG):
                if left > 1:
                    copy_att(2 * h + (T4_ATT + u + 1), 1 - u)
                act.wait_ge(qk_ps, after(2 * h + u))
                act.wait_ge(qk_ready, after(2 * h + (u - 2)))
                nc.scalar.activation(rows512[:, u, :], ps_h[2 * u][:, :], ACT.Silu, bias=bqk[:, 0:1]).then_inc(z_ready, 1)
                act.wait_ge(v_ps, after(2 * h + u))
                nc.scalar.activation(YT(h, u), ps_h[2 * u + 1][:, :], ACT.Silu).then_inc(v_ready, 1)
            copy_att(T4_ATT, 0)
            with act.Fori(0, NG // 2 - 1) as h:
                for u in range(2):
                    silus(h, u)
            for u in range(2):
                silus(NG // 2 - 1, u, left=2 - u)

            nc.scalar.preload_act_table(ACT.Gelu)
            group = 0
            def copy_av(group):
                act.wait_ge(pv_done, ENDS[group] + 1)
                if group >= 2:
                    act.wait_ge(avT_ps, group - 1)
                nc.scalar.activation(av_sb[:, group % 2, :], ps_av[group % 2][:, :], ACT.Copy).then_inc(av_ok, 1)
            for i in range(NU):
                n = UNITS[i][4]
                z = z_sb[i % 3][:, 0:n]
                act.wait_ge(z1_sb, i + 1)
                nc.scalar.activation(z, z, ACT.Identity, bias=z_shift[:, 0:1]).then_inc(z_mid, 1)
                act.wait_ge(z_mid, i + 1)
                nc.scalar.activation(z, z, ACT.Identity, bias=z_shift[:, 1:2]).then_inc(z_ok, 1)
                act.wait_ge(z_ok, i + 1)
                if i >= 2:
                    act.wait_ge(w_ok, i - 1)
                nc.scalar.activation(gelu_sb[:, i % 2, 0:n], z_sb[i % 3][:, 0:n], ACT.Gelu).then_inc(gelu_ok, 1)
                if group < len(ENDS) and i == ENDS[group] + 1:
                    copy_av(group)
                    group += 1
            copy_av(group)

            nc.scalar.preload_act_table(ACT.Exp)
            act.wait_ge(av_added, group + 1)
            def relu_hidden(u, bias, base):
                for f in range(FF):
                    act.wait_ge(top_h_ps, after(base(f)))
                    nc.scalar.activation(hid[:, u, f, :], ps_h[f][:, :], ACT.Relu, bias=bias[:, f:f + 1]).then_inc(top_h_sb, 1)
            def copy_top(h, u):
                act.wait_ge(t4_ps, after(2 * h + (T4_TOP + u)))
                nc.scalar.activation(YT(h, u), ps_t4[:, :], ACT.Copy).then_inc(t4_sb, 1)
            def router_relu(h, u, left=NG):
                act.wait_ge(logit_ps, after(2 * h + (u - 2)))
                relu_hidden(u, rb1, lambda f: 8 * h + (4 * u + f))
                if left > 1:
                    copy_top(h + u, 1 - u)
            copy_top(0, 0)
            with act.Fori(0, NG // 2 - 1) as h:
                for u in range(2):
                    router_relu(h, u)
            for u in range(2):
                router_relu(NG // 2 - 1, u, left=2 - u)
            act.wait_ge(shift_ok, 1)
            nc.scalar.activation(route[:, 3].rearrange("p t e -> p (t e)"), route[:, 2].rearrange("p t e -> p (t e)"),
                                 ACT.Exp).then_inc(exp_ok, 1)
            for g in range(NG):
                u = g % 2
                act.wait_ge(gate_t, after(g))
                act.wait_ge(gate_b, after(g - 2))
                nc.scalar.activation(gatesT[:, u, :], ps_gT, ACT.Copy).then_inc(gate_T, 1)
                act.wait_ge(gate_b, after(g))
                nc.scalar.activation(bias_sums[:, 512 * g:512 * (g + 1)], ps_gb, ACT.Copy).then_inc(gate_kept, 1)

            def block_copy(h, k):
                act.wait_ge(block_t, after(4 * h + k))
                nc.scalar.activation(block_xT[:, k % 2, :], ps_bx, ACT.Copy).then_inc(block_T, 1)

            def block_relu(h, k):
                b, u = 4 * h + k, k % 2
                act.wait_ge(block_h_ps, after(b))
                act.wait_ge(block_y_ps, after(b - 2))
                for f in range(FF):
                    a = nc.scalar.activation(rows512[:, u, P * f:P * (f + 1)], ps_bh[u][:, P * f:P * (f + 1)], ACT.Relu,
                                             bias=b1_now[:, k, f:f + 1])
                a.then_inc(block_h_sb, 1)

            block_copy(0, 0)
            block_relu(0, 0)
            block_copy(0, 1)
            with act.Fori(0, BLOCKS // 4 - 1) as h:
                for k in range(4):
                    block_copy(h + (k + 2) // 4, (k + 2) % 4)
                    block_relu(h + (k + 1) // 4, (k + 1) % 4)
            for k in range(3):
                if k < 2:
                    block_copy(BLOCKS // 4 - 1, k + 2)
                block_relu(BLOCKS // 4 - 1, k + 1)

        @block.vector
        def _(dve):
            for s in names["dve"]:
                dve.sem_inc(s, CREDIT)
            nc.vector.memset(ones_row[:], 1.0).then_inc(const_ok, 1)
            nc.vector.memset(zeros[:], 0.0).then_inc(const_ok, 1)
            inputs_in(dve, "bias")

            dve.wait_ge(const_ok, 6)
            nc.vector.tensor_scalar(rel_rows[:], zeros[0:32, :], rel_bias[:, 0:1], None, ALU.add).then_inc(rel_ok, 1)

            def first_norm(begin, h, u):
                xs = [X[:, 4 * (2 * h + u) + j, :] for j in range(4)]
                rs = [R[:, 4 * (2 * h + u) + j, :] for j in range(4)]
                if begin:
                    ln_begin(dve, xs, 2 * h + u, u)
                else:
                    ln_end(dve, xs, rs, 2 * h + u, u)
            inputs_in(dve, "x0")
            first_norm(True, 0, 0)
            first_norm(True, 0, 1)
            for u in range(2):
                first_norm(False, 0, u)
            dve.wait_ge(bias_ps, 1)
            for j, (c0, n) in enumerate(((0, 512), (512, 512), (1024, P))):
                nc.vector.tensor_scalar(dist_bias[:, c0:c0 + n], psum[(0, 1, 4)[j]][:, 0:n], float(P ** 0.5 / STD),
                                        float(0.75 - MU / STD), ALU.mult, ALU.add).then_inc(bias_ok, 1)
            dve.wait_ge(ln_out, after(1))
            inputs_in(dve, "retention")

            def next_first_norm(b, i):
                g, pair = i // 4, i % 2 * 2
                F = 2 * b + g
                tiles = [TPS * b + (TPS + 4 * g + pair + j) for j in range(2)]
                if i % 4 < 2:
                    for j, t in enumerate(tiles):
                        last = nc.vector.bn_stats(first_st[:, 0, pair + j, :], X[:, t, :])
                    if pair:
                        last.then_inc(first_moments, 1)
                        dve.wait_ge(first_moments, after(2 * F))
                        dve.sem_inc(passed, 1)
                        for j in range(4):
                            last = nc.vector.bn_aggr(first_mv[:, 0, j, :], first_st[:, 0, j, :])
                        last.then_inc(first_moments, 1)
                else:
                    if pair == 0:
                        dve.wait_ge(first_rstd, after(2 * F + 1))
                    for j, t in enumerate(tiles):
                        last = nc.vector.tensor_scalar(R[:, t, :], X[:, t, :], first_mv[:, 0, pair + j, 0:1],
                                                       first_rs[:, 0, pair + j:pair + j + 1], ALU.subtract, ALU.mult)
                    if pair:
                        last.then_inc(first_out, 1)

            def norm_begin(t, T, u, l, k):
                ln_begin(dve, [R[:, t, :]], k, u)

            def norm_end(t, T, u, l, k):
                dve.wait_ge(xt_ps, after(T - 2))
                ln_end(dve, [R[:, t, :]], [xn[:, u, 0:P]], k, u)

            def read_products(T, i, u, l):
                dve.wait_ge(fm_ps, after(T))
                dve.wait_ge(qk_spread, after(T - 1))
                n0 = P * (i % TPS)
                nc.vector.scalar_tensor_tensor(qs[:], ps_fm[:, 0:P], proj_bc[:, l, 0:1],
                                               decay_q[:, n0:n0 + P], ALU.add, ALU.mult)
                nc.vector.scalar_tensor_tensor(ks[:], ps_fm[:, P:2 * P], proj_bc[:, l, 1:2],
                                               decay_k[:, n0:n0 + P], ALU.add, ALU.mult).then_inc(qk_sb, 1)
                dve.wait_ge(kv_ps, after(T))
                dve.wait_ge(o_ps, after(T - 2))
                nc.vector.tensor_tensor(kv[:, u], ps_kv, kv_bias[:, l, :].unsqueeze(1).to_broadcast([P, 4, 256]),
                                        ALU.add).then_inc(kv_biased, 1)

            def make_probs(T):
                dve.wait_ge(scores_ps, after(T))
                dve.wait_ge(o_ps, after(T - 1))
                nc.vector.tensor_tensor(probs[:], ps_sc, causal.unsqueeze(1).to_broadcast([P, 4, P]),
                                        ALU.mult).then_inc(probs_sb, 1)

            def gate_out(T, u):
                dve.wait_ge(o_ps, after(T))
                dve.wait_ge(gate_sb, after(T))
                dve.wait_ge(y_ps, after(T - 2))
                for g in range(4):
                    q = slice(32 * g, 32 * g + 32)
                    last = nc.vector.tensor_tensor(
                        ret[q, u, :].rearrange("p (s n) -> p s n", s=4), ps_o[q, :, g, :],
                        gate_x[q, u, :].rearrange("p (s n) -> p s n", s=4), ALU.mult)
                last.then_inc(ret_sb, 1)

            def add_residual(t, T):
                dve.wait_ge(y_ps, after(T))
                dve.wait_ge(reto_b_in, after(T))
                nc.vector.tensor_tensor(R[:, t, :], R[:, t, :], ps_y, ALU.add).then_inc(res_done, 1)

            def retention_tile(b, i, l, first=False, left=8, more=False):
                t, T, k = TPS * b + i, TPS * b + (l * NT + i), TPS * b + (LN_RET[l] + i)
                u = i % 2
                if l == 0 and i == 6 and more:
                    dve.wait_ge(first_out, after(2 * b))
                if l == 0 and i == 2 and not (isinstance(b, int) and b == 0):
                    dve.wait_ge(first_out, after(2 * b - 1))
                if left > 2:
                    norm_begin(TPS * b + i + 2 if isinstance(b, int) or i < 6 else TPS * (b + 1) + i - 6, T + 2, u, l, k + 2)
                if not first:
                    gate_out(T - 1, 1 - u)
                make_probs(T)
                if not first:
                    add_residual(TPS * b + i - 1 if isinstance(b, int) or i > 0 else TPS * (b - 1) + 7, T - 1)
                if left > 1:
                    read_products(T + 1, i + 1, 1 - u, l)
                if l == 0 and more:
                    if first:
                        inputs_in(dve, "x")
                    next_first_norm(b, i)
                if left > 2:
                    norm_end(TPS * b + i + 2 if isinstance(b, int) or i < 6 else TPS * (b + 1) + i - 6, T + 2, u, l, k + 2)

            def tiles_of(h, u):
                return [R[:, 8 * h + (4 * u + j), :] for j in range(4)]

            def ffn_begin(h, u, l):
                ln_begin(dve, tiles_of(h, u), 2 * h + (LN_FFN[l] + u), u)

            def ffn_end(h, u, l):
                dve.wait_ge(t4_ps, after(2 * h + (l * NG + u - 2)))
                ln_end(dve, tiles_of(h, u), quarters(xn[:, u, :]), 2 * h + (LN_FFN[l] + u), u)

            def ffn_add(h, u, l):
                G = 2 * h + (l * NG + u)
                dve.wait_ge(y4_ps, after(G))
                r = R[:, :, :].rearrange("p (g t) d -> p g (t d)", t=4)[:, 2 * h + u, :]
                nc.vector.tensor_tensor(r, r, ps_y4[:, :], ALU.add).then_inc(y4_done, 1)

            X_groups = X[:, :, :].rearrange("p (g t) d -> p g (t d)", t=4)

            def group_of(x, h, u):
                return x[:].rearrange("p (g t) d -> p g (t d)", t=4)[:, 2 * h + u, :]

            def x_tiles(h, u):
                return [X[:, 8 * h + (4 * u + j), :] for j in range(4)]

            def behind_begin(tiles, F, c):
                for j, t in enumerate(tiles):
                    last = nc.vector.bn_stats(first_st[:, c, j, :], t)
                last.then_inc(first_moments, 1)
                dve.wait_ge(first_moments, after(2 * F))
                dve.sem_inc(passed, 1)
                for j in range(4):
                    last = nc.vector.bn_aggr(first_mv[:, c, j, :], first_st[:, c, j, :])
                last.then_inc(first_moments, 1)

            def behind_end(tiles, outs, F, c):
                dve.wait_ge(first_rstd, after(2 * F + 1))
                for j, (t, o) in enumerate(zip(tiles, outs)):
                    last = nc.vector.tensor_scalar(o, t, first_mv[:, c, j, 0:1], first_rs[:, c, j:j + 1],
                                                   ALU.subtract, ALU.mult)
                last.then_inc(first_out, 1)

            def final_begin(h, u):
                dve.wait_ge(bias_done, after(2 * h + (NG + u)))
                dve.sem_inc(passed, 1)
                behind_begin(tiles_of(h, u), 4 * h + (FINAL + 2 * u), 0)

            def final_end(h, u):
                behind_end(tiles_of(h, u), tiles_of(h, u), 4 * h + (FINAL + 2 * u), 0)

            def final_add(h, u):
                dve.wait_ge(fin_b, after(2 * h + u))
                nc.vector.tensor_tensor(X_groups[:, 2 * h + u, :], X_groups[:, 2 * h + u, :], group_of(R, h, u),
                                        ALU.add).then_inc(fin_x, 1)

            def y_begin(h, u):
                dve.wait_ge(fin_x, after(2 * h + u))
                dve.sem_inc(passed, 1)
                behind_begin(x_tiles(h, u), 4 * h + (FINAL + 2 * u + 1), 1)

            def y_end(h, u):
                behind_end(x_tiles(h, u), tiles_of(h, u), 4 * h + (FINAL + 2 * u + 1), 1)

            def last_ffn_step(h, u, left=NG):
                before = (h, 0) if u else (h - 1, 1)
                has_one, has_two = (not isinstance(h, int) or 2 * h + u >= n for n in (1, 2))
                if left > 2:
                    ffn_end(h + 1, u, LAYERS - 1)
                if has_two:
                    final_add(h - 1, u)
                    y_begin(h - 1, u)
                if has_one:
                    final_begin(*before)
                if left > 3:
                    ffn_begin(h + (1 + u), 1 - u, LAYERS - 1)
                if has_two:
                    y_end(h - 1, u)
                if has_one:
                    final_end(*before)
                ffn_add(h, u, LAYERS - 1)

            def ffn_step(h, u, l, left=NG):
                if left > 2:
                    ffn_end(h + 1, u, l)
                if left > 3:
                    ffn_begin(h + (1 + u), 1 - u, l)
                ffn_add(h, u, l)

            for l in range(LAYERS):
                if l:
                    dve.wait_ge(bias_done, after(NG - 1))
                for i in range(2):
                    norm_begin(i, l * NT + i, i, l, LN_RET[l] + i)
                    norm_end(i, l * NT + i, i, l, LN_RET[l] + i)
                read_products(l * NT, 0, 0, l)
                for i in range(TPS):
                    retention_tile(0, i, l, first=i == 0, more=True)
                with dve.Fori(1, NB - 1) as b:
                    for i in range(TPS):
                        retention_tile(b, i, l, more=True)
                for i in range(TPS):
                    retention_tile(NB - 1, i, l, left=TPS - i)
                gate_out(l * NT + NT - 1, 1)
                add_residual(NT - 1, l * NT + NT - 1)
                dve.wait_ge(res_done, after(l * NT + NT - 1))
                ffn_begin(0, 0, l)
                ffn_begin(0, 1, l)
                ffn_end(0, 0, l)
                ffn_begin(1, 0, l)
                ffn_end(0, 1, l)
                if l < LAYERS - 1:
                    with dve.Fori(0, NG // 2 - 2) as h:
                        for u in range(2):
                            ffn_step(h, u, l)
                    for h in (NG // 2 - 2, NG // 2 - 1):
                        for u in range(2):
                            ffn_step(h, u, l, left=NG - 2 * h - u)

            for u in range(2):
                last_ffn_step(0, u)
            with dve.Fori(1, NG // 2 - 2) as h:
                for u in range(2):
                    last_ffn_step(h, u)
            for h in (NG // 2 - 2, NG // 2 - 1):
                for u in range(2):
                    last_ffn_step(h, u, left=NG - 2 * h - u)
            final_add(NG // 2 - 1, 0)
            y_begin(NG // 2 - 1, 0)
            final_begin(NG // 2 - 1, 1)
            y_end(NG // 2 - 1, 0)
            final_end(NG // 2 - 1, 1)
            final_add(NG // 2 - 1, 1)
            y_begin(NG // 2 - 1, 1)
            y_end(NG // 2 - 1, 1)
            dve.wait_ge(first_out, after(FINAL + 2 * NG - 1))
            dve.sem_inc(passed, 1)

            def score_norm_begin(h, u):
                ln_begin(dve, tiles_of(h, u), 2 * h + (LN_SCORE + u), u)
            def score_norm_end(h, u):
                dve.wait_ge(t4_ps, after(2 * h + (LAYERS * NG + u - 2)))
                ln_end(dve, tiles_of(h, u), quarters(xn[:, u, :]), 2 * h + (LN_SCORE + u), u)
            def keep_scores(h, u):
                dve.wait_ge(score_ps, after(2 * h + u))
                nc.vector.tensor_copy(
                    score[:].rearrange("p e (g j) -> p e g j", j=4)[:, :, 2 * h + u, :],
                    ps_y4[:, 0:4 * NE].rearrange("p (j e) -> p e j", e=NE)).then_inc(score_sb, 1)
            for u in range(2):
                score_norm_begin(0, u)
            score_norm_end(0, 0)
            with dve.Fori(0, NG // 2 - 1) as h:
                for u in range(2):
                    score_norm_begin(h + 1, u)
                    score_norm_end(h + u, 1 - u)
                    keep_scores(h, u)
            score_norm_end(NG // 2 - 1, 1)
            for u in range(2):
                keep_scores(NG // 2 - 1, u)

            n_steps = [0]

            def step(ins):
                n_steps[0] += 1
                ins.then_inc(step_ok, 1)
                dve.wait_ge(step_ok, n_steps[0])
            dve.wait_ge(score_sb, after(NG - 1))
            bits = score[:].rearrange("p e t -> p (e t)")
            step(nc.vector.tensor_scalar(key[:, 0, :].bitcast(I32), bits.bitcast(I32), 31, -2 ** 31,
                                         ALU.arith_shift_right, ALU.bitwise_or))
            step(nc.vector.tensor_tensor(key[:, 1, :], bits.bitcast(U32), key[:, 0, :], ALU.bitwise_xor))
            step(nc.vector.tensor_scalar(key[:, 2, :], key[:, 1, :], 16, None, ALU.logical_shift_right))
            step(nc.vector.tensor_scalar(key[:, 3, :], key[:, 1, :], 65535, None, ALU.bitwise_and))
            for j in range(2):
                last = nc.vector.tensor_scalar(key_f[:, 2 * j:2 * j + 2, :].rearrange("p a n -> p (a n)"),
                                               key[:, 2 + j, :], 1.0, None, ALU.add)
            last.then_inc(key_ok, 1)
            dve.wait_ge(key_tp, 1)
            nc.vector.tensor_copy(key_t.rearrange("p a n -> p (a n)"), ps_t4[:, :]).then_inc(key_ok, 1)
            nc.vector.memset(zeros512, 0.0)
            nc.vector.memset(free, 1.0)
            step(nc.vector.memset(code, 0.0))
            nc.vector.tensor_copy(junk, zeros512).then_inc(key_ok, 1)

            def col(n):
                return cols[:, n:n + 1]
            STEPS = 51
            start = n_steps[0]

            def assign(e):
                m = [0]
                c = [0]

                def begin(ins):
                    m[0] += 1
                    ins.then_inc(step_ok, 1)

                def step(ins):
                    begin(ins)
                    dve.wait_ge(step_ok, STEPS * e + (start + m[0]))

                def summed(ins, *meanwhile):
                    c[0] += 1
                    ins.then_inc(count_in, 1)
                    for f in meanwhile:
                        begin(f())
                    if meanwhile:
                        dve.wait_ge(step_ok, STEPS * e + (start + m[0]))
                    dve.wait_ge(count_ps, COUNTS * e + c[0])

                def search_key(row, need, first):
                    for it in range(4):
                        size = 16.0 ** (3 - it)
                        digits, other = col(it % 2), col((it + 1) % 2)
                        thr = col(2) if it else thr_const[:, 0:1]
                        count = nc.vector.tensor_scalar(junk, row, thr, None, ALU.is_ge, ALU.add, accum_out=col(COUNT))
                        if it == 0:
                            summed(count, first) if first else summed(count)
                        else:
                            held = 16.0 ** (4 - it)
                            if it == 1:
                                grow = lambda: nc.vector.tensor_scalar(digits, col(3), held, None, ALU.mult)
                            else:
                                grow = lambda: nc.vector.scalar_tensor_tensor(digits, col(3), held, other, ALU.mult, ALU.add)
                            summed(count, grow)
                            if it < 3:
                                step(nc.vector.tensor_tensor(col(5), digits, thr_const[:, it + 1:it + 2], ALU.add))
                            else:
                                step(nc.vector.tensor_scalar(col(5), digits, -4368.0, None, ALU.add))
                        add = col(5) if it else thr_const[:, 1:2]
                        step(nc.vector.tensor_scalar(holds[:], ps_fm[:, 0:16], need, None, ALU.is_ge, ALU.add,
                                                     accum_out=col(3)))
                        begin(nc.vector.scalar_tensor_tensor(col(6 if it == 3 else 2), col(3), size, add, ALU.mult, ALU.add))
                        step(nc.vector.scalar_tensor_tensor(failing[:, 16 * it:16 * it + 16], holds[:], 0.5, ps_fm[:, 0:16],
                                                            ALU.is_lt, ALU.mult))
                    step(nc.vector.tensor_reduce(col(9), failing[:], AX.X, ALU.max))

                step(nc.vector.tensor_tensor(hi_left, keys_hi[:, e, :], free, ALU.mult))
                search_key(hi_left, float(CAP), lambda: nc.vector.tensor_tensor(code, code, free, ALU.add))
                begin(nc.vector.tensor_scalar(col(7), col(9), -1.0, float(CAP), ALU.mult, ALU.add))
                begin(nc.vector.scalar_tensor_tensor(lo_left, hi_left, col(6), keys_lo[:, e, :], ALU.is_equal, ALU.mult))
                step(nc.vector.tensor_scalar(chosen, hi_left, col(6), None, ALU.is_gt))
                search_key(lo_left, col(7), lambda: nc.vector.tensor_tensor(free, free, chosen, ALU.subtract))
                step(nc.vector.tensor_scalar(tie, lo_left, col(6), None, ALU.is_equal))
                summed(nc.vector.tensor_tensor_scan(scan_tie, tie, zeros512, 0.0, ALU.add, ALU.add),
                       lambda: nc.vector.tensor_scalar(chosen, lo_left, col(6), None, ALU.is_gt),
                       lambda: nc.vector.tensor_tensor(col(8), col(7), col(9), ALU.subtract))
                begin(nc.vector.tensor_tensor(free, free, chosen, ALU.subtract))
                step(nc.vector.tensor_tensor(col(8), col(8), ps_fm[:, 16:17], ALU.subtract))
                step(nc.vector.scalar_tensor_tensor(tie, scan_tie, col(8), tie, ALU.is_le, ALU.mult))
                step(nc.vector.tensor_tensor(free, free, tie, ALU.subtract))
                assert m[0] == STEPS and c[0] == COUNTS, (m, c)
            inputs_in(dve, "moe")
            for e in range(NE - 1):
                dve.wait_ge(key_in[e], 16 * 2)
            with dve.Fori(0, NE - 1) as e:
                assign(e)
            n_steps[0] = start + STEPS * (NE - 1)
            step(nc.vector.tensor_tensor(code, code, free, ALU.add))
            step(nc.vector.tensor_scalar(chosen, code, own_code, None, ALU.is_equal))
            nc.vector.tensor_tensor_scan(scan, chosen, zeros512, 0.0, ALU.add, ALU.add).then_inc(count_in, 1)
            dve.wait_ge(count_ps, COUNTS * (NE - 1) + 1)
            step(nc.vector.tensor_tensor(col(8), ps_fm[:, 16:17], own_base, ALU.add))
            nc.vector.scalar_tensor_tensor(chosen, scan, col(8), chosen, ALU.add, ALU.mult).then_inc(slots_ok, 1)
            dve.wait_ge(slots_tp, 1)
            step(nc.vector.tensor_copy(slot_i.rearrange("p (q j) -> p q j", j=4),
                                       ps_t4[:, 0:32].rearrange("p (j q) -> p q j", q=8)))
            for i, (x, y) in enumerate(((slot_row_i, row_f), (slot_col_i, col_f))):
                step(nc.vector.tensor_scalar(x, slot_i, (P - 1, 7)[i], None, (ALU.bitwise_and, ALU.logical_shift_right)[i]))
                step(nc.vector.tensor_copy(y, x))
            with dve.Fori(0, NT // 8) as h:
                for k in range(8):
                    t = 8 * h + k
                    dve.wait_ge(slot_hot_used, after(t - 8))
                    nc.vector.tensor_scalar(slot_row_hot[:, k, :], iota, row_f.unsqueeze(2)[:, t, :], None, ALU.is_equal)
                    nc.vector.tensor_scalar(slot_col_hot[:, k, :], iota[:, 0:NT], col_f.unsqueeze(2)[:, t, :],
                                            choice_id.unsqueeze(2)[:, t, :], ALU.is_equal, ALU.mult).then_inc(slot_hot_ok, 1)
            dve.wait_ge(slot_hot_used, after(NT - 1))
            nc.vector.tensor_scalar(routed_token[:], ps_fm[:, 0:NT], -1.0, None, ALU.add).then_inc(slots_ok, 1)

            def routed_norm(e):
                dve.wait_ge(routed_in[e], 64)
                ln_begin(dve, quarters(routed[e]), LN_MOE + e, e % 2)
                if e >= 2:
                    dve.wait_ge(routed_t, e - 1)
                ln_end(dve, quarters(routed[e]), quarters(xn[:, e % 2, :]), LN_MOE + e, e % 2)
            for e in range(3):
                routed_norm(e)
            for e in range(NE):
                if e + 3 < NE:
                    routed_norm(e + 3)
                dve.wait_ge(moe_y_ps, e + 1)
                nc.vector.tensor_tensor(routed[e], routed[e], ps_y4[:, :], ALU.add).then_inc(moe_y_sb, 1)
                dve.wait_ge(moe_y_sb, e + 1)
                r = routed[e].rearrange("p (t d) -> p t d", t=4)
                nc.vector.tensor_tensor(r, r, moe_b2[:, e, :].unsqueeze(1).to_broadcast([P, 4, P]),
                                        ALU.add).then_inc(moe_out, 1)
            flat = "p t d -> p (t d)"
            for b in range(NB):
                dve.wait_ge(moe_back[b], 16)
                x, r = [m[:, TPS * b:TPS * (b + 1), :].rearrange(flat) for m in (X, R)]
                nc.vector.tensor_tensor(x, x, r, ALU.add).then_inc(moe_added, 1)

            dve.wait_ge(moe_added, NB)
            def att_norm(h, u):
                ln_begin(dve, x_tiles(h, u), 2 * h + (LN_ATT + u), u)
                dve.wait_ge(t4_ps, after(2 * h + (T4_ATT + u - 2)))
                ln_end(dve, x_tiles(h, u), quarters(xn[:, u, :]), 2 * h + (LN_ATT + u), u)
            def make_qk(h, u):
                dve.wait_ge(z_ready, after(2 * h + u))
                for j, dst in enumerate((qT_all, kT_all)):
                    last = nc.vector.tensor_scalar(dst.rearrange("p (g n) -> p g n", n=512)[:, 2 * h + u, :],
                                                   rows512[:, u, :], gamma[:, j:j + 1], beta[:, j:j + 1],
                                                   ALU.mult, ALU.add)
                last.then_inc(qk_ready, 1)
            for u in range(2):
                att_norm(0, u)
            with dve.Fori(0, NG // 2 - 1) as h:
                for u in range(2):
                    att_norm(h + 1, u)
                    make_qk(h, u)
            for u in range(2):
                make_qk(NG // 2 - 1, u)

            dve.wait_ge(bias_in, 16)
            group = 0
            def add_av(group):
                b, half = UNITS[ENDS[group]][0:2]
                dve.wait_ge(avT_ps, group + 1)
                t0 = TPS * b + 4 * half
                xg = X[:, t0:t0 + 4, :].rearrange("p t d -> p (t d)")
                nc.vector.tensor_tensor(xg, xg, ps_t4[:, :], ALU.add).then_inc(av_added, 1)
            def make_z(i):
                b, half, m, n0, n = UNITS[i]
                x0, z = n0 - P * m, z_sb[i % 3][:, 0:n]
                dve.wait_ge(sim_ps, i + 1)
                if i >= 3:
                    dve.wait_ge(gelu_ok, i - 2)
                    dve.wait_ge(recip_ok, i - 2)
                nc.vector.scalar_tensor_tensor(z, ps_sim[i % 3][:, 0:n], float(1 / (SEQ * STD)), toeplitz[:, x0:x0 + n],
                                               ALU.mult, ALU.add).then_inc(z1_sb, 1)
            def invert(i):
                n = UNITS[i][4]
                dve.wait_ge(z_ok, i + 1)
                if i >= 2:
                    dve.wait_ge(w_ok, i - 1)
                nc.vector.reciprocal(recip_sb[:, i % 2, 0:n], z_sb[i % 3][:, 0:n]).then_inc(recip_ok, 1)
            for i in range(2):
                make_z(i)
            for i in range(NU):
                if i + 2 < NU:
                    make_z(i + 2)
                invert(i)
                if group < len(ENDS) and i == ENDS[group] + 3:
                    add_av(group)
                    group += 1
            add_av(group)
            dve.wait_ge(av_added, group + 1)

            def top_begin(h, u):
                ln_begin(dve, x_tiles(h, u), 2 * h + (LN_TOP + u), u)
            def top_end(h, u, first=False):
                dve.wait_ge(t4_ps, after(2 * h + (T4_TOP + u - 2)))
                if not first:
                    dve.wait_ge(y_out[u], 16 * h)
                ln_end(dve, x_tiles(h, u), quarters(xn[:, u, :]), 2 * h + (LN_TOP + u), u)
            def keep_logits(h, u):
                dve.wait_ge(logit_ps, after(2 * h + u))
                nc.vector.tensor_tensor(logits.rearrange("p (g t) e -> p g t e", t=4)[:, 2 * h + u],
                                        ps_y4[:, 0:4 * NE].rearrange("p (t e) -> p t e", e=NE),
                                        rb2[:].unsqueeze(1).to_broadcast([P, 4, NE]), ALU.add).then_inc(logit_sb, 1)
            top_begin(0, 0)
            top_begin(0, 1)
            top_end(0, 0, first=True)
            top_begin(1, 0)
            top_end(0, 1, first=True)
            with dve.Fori(0, NG // 2 - 2) as h:
                for u in range(2):
                    top_end(h + 1, u)
                    top_begin(h + (1 + u), 1 - u)
                    keep_logits(h, u)
            top_end(NG // 2 - 1, 0)
            top_begin(NG // 2 - 1, 1)
            keep_logits(NG // 2 - 2, 0)
            top_end(NG // 2 - 1, 1)
            for g in range(NG - 3, NG):
                keep_logits(g // 2, g % 2)
            dve.wait_ge(logit_sb, after(NG - 1))


            def over(ap):
                return ap.unsqueeze(2).to_broadcast([P, NT, NE])

            def first_of(values, top, out):
                step(nc.vector.tensor_tensor(out, values, over(top), ALU.is_equal))
                step(nc.vector.tensor_tensor(out, out, order.unsqueeze(1).to_broadcast([P, NT, NE]), ALU.mult))
                step(nc.vector.tensor_reduce(peak[:, 3, :], out, AX.X, ALU.max))
                step(nc.vector.tensor_tensor(out, out, over(peak[:, 3, :]), ALU.is_equal))
            step(nc.vector.tensor_reduce(peak[:, 0, :], logits, AX.X, ALU.max))
            nc.vector.tensor_tensor(route[:, 2], logits, over(peak[:, 0, :]), ALU.subtract).then_inc(shift_ok, 1)
            first_of(logits, peak[:, 0, :], route[:, 0])
            step(nc.vector.scalar_tensor_tensor(
                route[:, 1].rearrange("p t e -> p (t e)"), route[:, 0].rearrange("p t e -> p (t e)"), -3e38,
                logits.rearrange("p t e -> p (t e)"), ALU.mult, ALU.add))
            step(nc.vector.tensor_reduce(peak[:, 1, :], route[:, 1], AX.X, ALU.max))
            first_of(route[:, 1], peak[:, 1, :], by_tile(second_hot))
            step(nc.vector.tensor_tensor(by_tile(mask), by_tile(second_hot), route[:, 0], ALU.add))
            dve.sem_inc(mask_ok, 1)
            dve.wait_ge(exp_ok, 1)
            step(nc.vector.tensor_tensor(gates[:], by_tile(mask), route[:, 3], ALU.mult))
            step(nc.vector.tensor_reduce(peak[:, 2, :], gates[:], AX.X, ALU.add))
            step(nc.vector.reciprocal(peak[:, 1, :], peak[:, 2, :]))
            step(nc.vector.tensor_tensor(gates[:], gates[:], over(peak[:, 1, :]), ALU.mult))
            dve.sem_inc(gates_ok, 1)

            def begin(ins):
                n_steps[0] += 1
                ins.then_inc(step_ok, 1)
            dve.wait_ge(rank_ps, 1)
            begin(nc.vector.memset(product, 0.0))
            step(nc.vector.tensor_copy(by_expert(totals), by_tile(ps_total).rearrange("p t e -> p e t")))
            step(nc.vector.tensor_tensor_scan(running, totals, product, 0.0, ALU.add, ALU.add))
            last_tile = by_expert(running)[:, :, NT - 1]
            begin(nc.vector.memset(starts[:, 0:1], 0.0))
            begin(nc.vector.tensor_tensor(slot_of, running, totals, ALU.subtract))
            step(nc.vector.tensor_copy(starts[:, 1:NE], last_tile[:, 0:NE - 1]))
            step(nc.vector.tensor_tensor(tokens_of, last_tile, starts, ALU.subtract))
            step(nc.vector.tensor_scalar(blocks_i, tokens_of, float(P - 1), None, ALU.add))
            step(nc.vector.tensor_scalar(blocks_i, blocks_i, 7, None, ALU.logical_shift_right))
            step(nc.vector.tensor_copy(blocks_of, blocks_i))
            step(nc.vector.tensor_tensor_scan(block_ends, blocks_of, product[:, 0:NE], 0.0, ALU.add, ALU.add))
            step(nc.vector.tensor_tensor(shift_of, block_ends, blocks_of, ALU.subtract))
            step(nc.vector.scalar_tensor_tensor(shift_of, shift_of, float(P), starts, ALU.mult, ALU.subtract))
            step(nc.vector.tensor_tensor(by_expert(slot_of), by_expert(slot_of),
                                         shift_of.unsqueeze(2).to_broadcast([P, NE, NT]), ALU.add))
            step(nc.vector.tensor_tensor(by_expert(slot_of), by_expert(slot_of),
                                         by_tile(ps_rank).rearrange("p t e -> p e t"), ALU.add))
            for c, hot in enumerate((route[:, 0], by_tile(second_hot))):
                for values, sums in ((by_expert(slot_of).rearrange("p e t -> p t e"), slot_f), (gates[:], top_gates)):
                    step(nc.vector.tensor_tensor(by_tile(product), hot, values, ALU.mult))
                    step(nc.vector.tensor_reduce(sums[:, NT * c:NT * (c + 1)], by_tile(product), AX.X, ALU.add))
            step(nc.vector.tensor_copy(top_slots, slot_f))
            begin(nc.vector.tensor_scalar(row_i, top_slots, P - 1, None, ALU.bitwise_and))
            step(nc.vector.tensor_scalar(block_i, top_slots, 7, None, ALU.logical_shift_right))
            begin(nc.vector.tensor_copy(slot_row, row_i))
            step(nc.vector.tensor_copy(slot_block, block_i))
            step(nc.vector.tensor_tensor(ended, block_ends.unsqueeze(1).to_broadcast([P, BLOCKS, NE]),
                                         iota[:, 0:BLOCKS].unsqueeze(2).to_broadcast([P, BLOCKS, NE]), ALU.is_le))
            step(nc.vector.tensor_reduce(expert_f, ended, AX.X, ALU.add))
            step(nc.vector.tensor_scalar(expert_of, expert_f, float(NE - 1), None, ALU.min))
            with dve.Fori(0, 2 * NT // 8) as h:
                for k in range(8):
                    i = 8 * h + k
                    dve.wait_ge(hot_used, after(i - 8))
                    nc.vector.tensor_scalar(row_hot[:, k, :], iota, slot_row.unsqueeze(2)[:, i, :], None, ALU.is_equal)
                    nc.vector.tensor_scalar(block_hot[:, k, :], iota[:, 0:BLOCKS], slot_block.unsqueeze(2)[:, i, :],
                                            choice_id.unsqueeze(2)[:, i, :], ALU.is_equal, ALU.mult).then_inc(hot_ok, 1)
            dve.wait_ge(hot_used, after(2 * NT - 1))
            step(nc.vector.tensor_copy(choice_f, ps_token))
            step(nc.vector.tensor_scalar(is_empty, choice_f, 0.0, None, ALU.is_equal))
            step(nc.vector.tensor_tensor(is_empty, is_empty, empty_id, ALU.mult))
            step(nc.vector.tensor_tensor(choice_f, choice_f, is_empty, ALU.add))
            step(nc.vector.tensor_scalar(choice_of, choice_f, -1.0, None, ALU.add))
            nc.vector.tensor_scalar(token_of, choice_of, TOK - 1, None, ALU.bitwise_and).then_inc(tokens_ok, 1)

            dve.wait_ge(late, 32)
            dve.wait_ge(tokens_ok, 1)
            def stage_weights(h, k):
                b = 4 * h + k
                e = dve.value_load(expert_of.unsqueeze(2)[0:1, b, :], min_val=0, max_val=NE - 1)
                dve.wait_ge(block_y_ps, after(b - 4))
                nc.vector.tensor_copy(w1_now[:, k, :], top_w1[:, e, :])
                nc.vector.tensor_copy(w2_now[:, k, :], arena[:].rearrange("p (e n) -> p e n", e=NE)[:, e, :])
                nc.vector.tensor_copy(b1_now[:, k, :], top_b1[:, e, :]).then_inc(weights_now, 1)

            def four_results(h, first=False, last=False):
                for k in range(4):
                    dve.wait_ge(block_y_ps, after(4 * h + k))
                    if not first:
                        dve.wait_ge(block_out[k], 16 * h)
                    nc.vector.tensor_copy(block_y[:, k, :], ps_by[k % 2]).then_inc(block_y_sb, 1)
                    if not last:
                        stage_weights(h + 1, k)
            for k in range(4):
                stage_weights(0, k)
            four_results(0, first=True)
            with dve.Fori(1, BLOCKS // 4 - 1) as h:
                four_results(h)
            four_results(BLOCKS // 4 - 1, last=True)

            for g in range(NG):
                dve.wait_ge(gate_kept, after(g))
                step(nc.vector.tensor_tensor(X_groups[:, g, :], X_groups[:, g, :], bias_sums[:, 512 * g:512 * (g + 1)],
                                             ALU.add))
                dve.wait_ge(back[g], 16 * 2)
                for c, results in enumerate((R, second)):
                    for j in range(4):
                        t = 4 * g + j
                        last = nc.vector.scalar_tensor_tensor(X[:, t, :], results[:, t, :], top_gates[:, NT * c + t:NT * c + t + 1],
                                                              X[:, t, :], ALU.mult, ALU.add)
                    step(last)
                dve.sem_inc(top_added, 1)

        @block.gpsimd
        def _(pool):
            for s in names["pool"]:
                pool.sem_inc(s, CREDIT)
            nc.gpsimd.memset(mhalf[:], -0.5).then_inc(const_ok, 1)
            nc.gpsimd.memset(eps4[:], EPS).then_inc(const_ok, 1)
            nc.gpsimd.memset(z_shift[:, 0:1], -0.75).then_inc(const_ok, 1)
            nc.gpsimd.memset(z_shift[:, 1:2], 2.0 ** -26).then_inc(const_ok, 1)
            pool.wait_ge(const_ok, 6)
            for u in range(2):
                ln_root(pool, 4, u, u)

            def first_root(F, c=0):
                pool.wait_ge(first_moments, after(2 * F + 1))
                nc.gpsimd.tensor_tensor(first_ve[:, c], first_mv[:, c, :, 1], eps4[:, 0:4], ALU.add).then_inc(first_rstd, 1)
                pool.wait_ge(first_rstd, after(2 * F))
                nc.gpsimd.tensor_tensor(first_rs[:, c], first_ve[:, c], mhalf[:, 0:4], ALU.pow).then_inc(first_rstd, 1)

            def spread(T, u):
                pool.wait_ge(qk_sb, after(T))
                pool.wait_ge(o_ps, after(T - 2))
                for src, mask, dst in ((qs, quad_mask, q_quads), (ks, slot_mask, k_slots)):
                    last = nc.gpsimd.tensor_tensor(
                        dst[:, u], src[:, :].rearrange("p (s n) -> p s n", s=4).unsqueeze(2).to_broadcast([P, 4, 4, SUB]),
                        mask.unsqueeze(1).unsqueeze(3).to_broadcast([P, 4, 4, SUB]), ALU.mult)
                last.then_inc(qk_spread, 1)

            def decay_kv(T, i, u):
                pool.wait_ge(kv_biased, after(T))
                c0 = 4 * (i % TPS)
                nc.gpsimd.tensor_tensor(kv[:, u, :, 0:P], kv[:, u, :, 0:P], decay_rows[:, c0:c0 + 4, :], ALU.mult)
                nc.gpsimd.tensor_tensor(kv[:, u, :, P:2 * P], kv[:, u, :, P:2 * P],
                                        slot_rows.unsqueeze(1).to_broadcast([P, 4, P]), ALU.mult).then_inc(kv_ready, 1)

            def add_reto_b(t, T, k, l):
                pool.wait_ge(ln_out, after(k))
                nc.gpsimd.tensor_tensor(R[:, t, :], R[:, t, :], reto_b[:, l, :], ALU.add).then_inc(reto_b_in, 1)

            def retention_tile(b, i, l, left=8, more=False):
                T, k = TPS * b + (l * NT + i), TPS * b + (LN_RET[l] + i)
                u = i % 2
                if left > 2:
                    ln_root(pool, 1, k + 2, u)
                if left > 1:
                    spread(T + 1, 1 - u)
                    decay_kv(T + 1, i + 1, 1 - u)
                    add_reto_b(TPS * b + (i + 1), T + 1, k + 1, l)
                if l == 0 and more and i % 4 == 1:
                    first_root(2 * b + i // 4)

            def ffn_bias(h, u, l):
                G = 2 * h + (l * NG + u)
                pool.wait_ge(y4_done, after(G))
                r = R[:, :, :].rearrange("p (g t) d -> p g t d", t=4)[:, 2 * h + u, :, :]
                nc.gpsimd.tensor_tensor(r, r, ffn2_b[:, l, :].unsqueeze(1).to_broadcast([P, 4, P]),
                                        ALU.add).then_inc(bias_done, 1)

            inputs_in(pool, "retention")
            for l in range(LAYERS):
                for i in range(2):
                    ln_root(pool, 1, LN_RET[l] + i, i)
                spread(l * NT, 0)
                if l == 0:
                    inputs_in(pool, "decays")
                decay_kv(l * NT, 0, 0)
                add_reto_b(0, l * NT, LN_RET[l], l)
                with pool.Fori(0, NB - 1) as b:
                    for i in range(TPS):
                        retention_tile(b, i, l, more=True)
                for i in range(TPS):
                    retention_tile(NB - 1, i, l, left=TPS - i)
                for g in range(3):
                    ln_root(pool, 4, LN_FFN[l] + g, g % 2)
                if l < LAYERS - 1:
                    with pool.Fori(0, NG // 2 - 2) as h:
                        for u in range(2):
                            ln_root(pool, 4, 2 * h + (LN_FFN[l] + u + 3), 1 - u)
                            ffn_bias(h, u, l)
                    ln_root(pool, 4, LN_FFN[l] + NG - 1, 1)
                    for g in range(NG - 4, NG):
                        ffn_bias(g // 2, g % 2, l)

            def final_scale(h, u):
                g = 2 * h + u
                pool.wait_ge(first_out, after(4 * h + (FINAL + 2 * u)))
                pool.sem_inc(passed, 1)
                y = R[:].rearrange("p (g t) d -> p g t d", t=4)[:, 2 * h + u, :, :]
                nc.gpsimd.tensor_tensor(y, y, lnf_g[:, :].unsqueeze(1).to_broadcast([P, 4, P]), ALU.mult).then_inc(fin_g, 1)
                pool.wait_ge(fin_g, after(g))
                pool.sem_inc(passed, 1)
                nc.gpsimd.tensor_tensor(y, y, lnf_b[:, :].unsqueeze(1).to_broadcast([P, 4, P]), ALU.add).then_inc(fin_b, 1)
            def last_ffn_step(h, u, left=NG):
                before = (h, 0) if u else (h - 1, 1)
                has_one, has_two = (not isinstance(h, int) or 2 * h + u >= n for n in (1, 2))
                if has_two:
                    first_root(4 * (h - 1) + (FINAL + 2 * u + 1), 1)
                if has_one:
                    first_root(4 * before[0] + (FINAL + 2 * before[1]), 0)
                if left > 3:
                    ln_root(pool, 4, 2 * h + (LN_FFN[1] + u + 3), 1 - u)
                if has_one:
                    final_scale(*before)
                ffn_bias(h, u, LAYERS - 1)
            for u in range(2):
                last_ffn_step(0, u)
            with pool.Fori(1, NG // 2 - 2) as h:
                for u in range(2):
                    last_ffn_step(h, u)
            for h in (NG // 2 - 2, NG // 2 - 1):
                for u in range(2):
                    last_ffn_step(h, u, left=NG - 2 * h - u)
            first_root(FINAL + 2 * NG - 3, 1)
            first_root(FINAL + 2 * NG - 2, 0)
            final_scale(NG // 2 - 1, 1)
            first_root(FINAL + 2 * NG - 1, 1)
            with pool.Fori(0, NG // 2) as h:
                for u in range(2):
                    ln_root(pool, 4, 2 * h + (LN_SCORE + u), u)

            pool.wait_ge(slots_ok, 2)
            pool.wait_ge(tokens_out, 16)

            def gather_routed(e):
                for j in range(4):
                    nc.gpsimd.indirect_dma_start(
                        out=routed[e][:, P * j:P * (j + 1)], out_offset=None, in_=tokens_d,
                        in_offset=bass.IndirectOffsetOnAxis(ap=routed_token[:, 4 * e + j:4 * e + j + 1], axis=0)
                    ).then_inc(routed_in[e], 16)
            for e in range(2):
                gather_routed(e)
            for e in range(3):
                ln_root(pool, 4, LN_MOE + e, e % 2)
                gather_routed(e + 2)
            gather_routed(5)
            for e in range(NE):
                if e + 3 < NE:
                    ln_root(pool, 4, LN_MOE + e + 3, (e + 1) % 2)
                if e + 6 < NE:
                    gather_routed(e + 6)
                pool.wait_ge(moe_out, e + 1)
                for j in range(4):
                    nc.gpsimd.indirect_dma_start(
                        out=moe_d, out_offset=bass.IndirectOffsetOnAxis(ap=routed_token[:, 4 * e + j:4 * e + j + 1], axis=0),
                        in_=routed[e][:, P * j:P * (j + 1)], in_offset=None).then_inc(moe_stored, 16)

            with pool.Fori(0, NG // 2) as h:
                for u in range(2):
                    ln_root(pool, 4, 2 * h + (LN_ATT + u), u)
            for i in range(NU):
                n = UNITS[i][4]
                pool.wait_ge(gelu_ok, i + 1)
                pool.wait_ge(recip_ok, i + 1)
                if i >= 2:
                    pool.wait_ge(pv_done, i - 1)
                nc.gpsimd.tensor_tensor(w_sb[:, i % 2, 0:n], gelu_sb[:, i % 2, 0:n], recip_sb[:, i % 2, 0:n],
                                        ALU.mult).then_inc(w_ok, 1)
                if i in DIAG:
                    pool.wait_ge(w_ok, i + 1)
                    nc.gpsimd.affine_select(out=w_sb[:, i % 2, 0:P], in_=w_sb[:, i % 2, 0:P], compare_op=ALU.is_ge,
                                            fill=0.0, base=0, pattern=[[1, P]], channel_multiplier=-1).then_inc(masked, 1)
            with pool.Fori(0, NG // 2) as h:
                for u in range(2):
                    ln_root(pool, 4, 2 * h + (LN_TOP + u), u)

            pool.wait_ge(tokens_ok, 1)
            for u in range(2):
                pool.wait_ge(y_out[u], 16 * NG // 2)

            def gather_block(b):
                nc.gpsimd.indirect_dma_start(
                    out=block_x[:, b % 4, :], out_offset=None, in_=y_d,
                    in_offset=bass.IndirectOffsetOnAxis(ap=token_of[:, b:b + 1], axis=0)).then_inc(block_in[b % 4], 16)
            for b in range(4):
                gather_block(b)
            for b in range(BLOCKS):
                if b + 4 < BLOCKS:
                    pool.wait_ge(block_t, after(b))
                    gather_block(b + 4)
                pool.wait_ge(block_y_sb, after(b))
                nc.gpsimd.indirect_dma_start(
                    out=top_d, out_offset=bass.IndirectOffsetOnAxis(ap=choice_of[:, b:b + 1], axis=0),
                    in_=block_y[:, b % 4, :], in_offset=None).then_inc(block_out[b % 4], 16)


def kernel(**inputs):
    import numpy as _np
    import concourse.bacc as _bacc
    from concourse import mybir as _mybir
    from concourse.bass_utils import run_bass_kernel_spmd as _run

    nc = _bacc.Bacc("TRN2", target_bir_lowering=False, num_devices=1)
    arrays, aps = {}, {}
    for name, a in list(inputs.items()) + list(pack(inputs).items()) + list(constants().items()):
        a = _np.ascontiguousarray(a)
        arrays[f"in_{name}_dram"] = a
        aps[name] = nc.dram_tensor(f"in_{name}_dram", a.shape, _mybir.dt.from_np(a.dtype), kind="ExternalInput").ap()
    out = nc.dram_tensor("out_0_dram", (NB, SEQ, P), F32, kind="ExternalOutput").ap()
    mega_kernel(nc, aps, out)
    r = _run(nc, [arrays], core_ids=[0])
    return r.results[0]["out_0_dram"]
```
